# Optimizing a Trainium2 kernel written in Bass

```python
import numpy as np
import jax
import jax.numpy as jnp

def _softmax(x, axis=-1):
    return jax.nn.softmax(x, axis=axis)

def _gelu(x):
    return jax.nn.gelu(x, approximate=True)

def _silu(x):
    return jax.nn.silu(x)

def _sigmoid(x):
    return jax.nn.sigmoid(x)

def _layernorm(x, axis=-1, eps=1e-05):
    m = jnp.mean(x, axis=axis, keepdims=True)
    v = jnp.var(x, axis=axis, keepdims=True)
    return (x - m) / jnp.sqrt(v + eps)

def _scatter_add(tgt, idx, src, axis=0):
    return tgt.at[idx].add(src)

def _segment_sum(src, seg, n):
    return jax.ops.segment_sum(src, seg, n)
kernel_name = 'mk_gnn_resnorm_d4_gnn_r64_53a157'

def setup_inputs(seed: int=0):
    np.random.seed(seed)
    _w = jnp.asarray

    def _rec_inputs():
        import jax
        import jax.numpy as jnp
        _gk = jax.random.key(seed)
        x = -0.000202 + 1 * jax.random.normal(jax.random.fold_in(_gk, 1), (100000, 128), jnp.float32)
        src = jax.random.randint(jax.random.fold_in(_gk, 2), (50000,), 0, 100000, jnp.int32)
        dst = jnp.minimum((100000 * jax.random.uniform(jax.random.fold_in(_gk, 3), (50000,)) ** 2.0).astype(jnp.int32), 99999)
        _o = jnp.argsort(dst, stable=True)
        src = src[_o]
        dst = dst[_o]
        edge_attr_64 = jax.random.uniform(jax.random.fold_in(_gk, 12), (50000, 64), jnp.float32, 0.0, 1)
        return (x, src, dst, edge_attr_64)
    x, src, dst, edge_attr_64 = _rec_inputs()

    def _L0_gnn_setup():
        import jax, jax.numpy as jnp
        import numpy as np
        N, E, IN_C, H, C = (50000, 12500, 128, 4, 32)
        key = jax.random.key(seed)
        ks = jax.random.split(key, 10)
        s = 1.0 / np.sqrt(IN_C)
        x = jax.random.normal(ks[0], (N, IN_C), dtype=jnp.float32)
        edge_index = jax.random.randint(ks[1], (2, E), 0, N, dtype=jnp.int64)
        Wq = jax.random.uniform(ks[2], (IN_C, H * C), jnp.float32, -s, s)
        bq = jax.random.uniform(ks[3], (H * C,), jnp.float32, -s, s)
        Wk = jax.random.uniform(ks[4], (IN_C, H * C), jnp.float32, -s, s)
        bk = jax.random.uniform(ks[5], (H * C,), jnp.float32, -s, s)
        Wv = jax.random.uniform(ks[6], (IN_C, H * C), jnp.float32, -s, s)
        bv = jax.random.uniform(ks[7], (H * C,), jnp.float32, -s, s)
        Wr = jax.random.uniform(ks[8], (IN_C, H * C), jnp.float32, -s, s)
        br = jax.random.uniform(ks[9], (H * C,), jnp.float32, -s, s)
        return {'x': x, 'edge_index': edge_index, 'Wq': Wq, 'bq': bq, 'Wk': Wk, 'bk': bk, 'Wv': Wv, 'bv': bv, 'Wr': Wr, 'br': br}
    _L0_gnn_all = _L0_gnn_setup()
    _L0_gnn_in = {k: v for k, v in _L0_gnn_all.items() if k in ('Wq', 'bq', 'Wk', 'bk', 'Wv', 'bv', 'Wr', 'br')}
    del _L0_gnn_all

    def _L1_gnn_setup():
        import jax, jax.numpy as jnp
        import numpy as np
        N_NODES = 625
        N_EDGES = 10000
        IN_CH = 128
        OUT_CH = 128
        NUM_RBF = 64
        key = jax.random.key(seed)
        ks = jax.random.split(key, 8)
        x = jax.random.normal(ks[0], (N_NODES, IN_CH), dtype=jnp.float32)
        edge_index = jax.random.randint(ks[1], (2, N_EDGES), 0, N_NODES, dtype=jnp.int64)
        edge_rbf = jax.random.uniform(ks[2], (N_EDGES, NUM_RBF), dtype=jnp.float32)
        s1 = 1.0 / np.sqrt(NUM_RBF)
        s2 = 1.0 / np.sqrt(OUT_CH)
        sl = 1.0 / np.sqrt(IN_CH)
        W1 = jax.random.normal(ks[3], (NUM_RBF, OUT_CH), dtype=jnp.float32) * s1
        b1 = jnp.zeros((OUT_CH,), dtype=jnp.float32)
        W2 = jax.random.normal(ks[4], (OUT_CH, OUT_CH), dtype=jnp.float32) * s2
        b2 = jnp.zeros((OUT_CH,), dtype=jnp.float32)
        Wl = jax.random.normal(ks[5], (IN_CH, OUT_CH), dtype=jnp.float32) * sl
        bl = jnp.zeros((OUT_CH,), dtype=jnp.float32)
        return {'x': x, 'edge_index': edge_index, 'edge_rbf': edge_rbf, 'W1': W1, 'b1': b1, 'W2': W2, 'b2': b2, 'Wl': Wl, 'bl': bl}
    _L1_gnn_all = _L1_gnn_setup()
    _L1_gnn_in = {k: v for k, v in _L1_gnn_all.items() if k in ('W1', 'b1', 'W2', 'b2', 'Wl', 'bl')}
    del _L1_gnn_all

    def _L2_gnn_setup():
        import jax, jax.numpy as jnp
        import numpy as np
        N_NODES = 10000
        N_EDGES = 2500
        DIM_FEAT = 128
        NUM_HEADS = 4
        key = jax.random.key(seed)
        ks = jax.random.split(key, 9)
        feat = jax.random.normal(ks[0], (N_NODES, DIM_FEAT), dtype=jnp.float32)
        src = jax.random.randint(ks[1], (N_EDGES,), 0, N_NODES, dtype=jnp.int32)
        dst = jax.random.randint(ks[2], (N_EDGES,), 0, N_NODES, dtype=jnp.int32)
        sd1 = (2.0 / (DIM_FEAT + DIM_FEAT * NUM_HEADS)) ** 0.5
        W_fc = jax.random.normal(ks[3], (DIM_FEAT, DIM_FEAT * NUM_HEADS), dtype=jnp.float32) * sd1
        att_ns = jax.random.normal(ks[4], (1, NUM_HEADS, DIM_FEAT), dtype=jnp.float32) * 0.1
        att_nd = jax.random.normal(ks[5], (1, NUM_HEADS, DIM_FEAT), dtype=jnp.float32) * 0.1
        sd2 = (2.0 / (DIM_FEAT * NUM_HEADS + DIM_FEAT)) ** 0.5
        W_trans = jax.random.normal(ks[6], (DIM_FEAT * NUM_HEADS, DIM_FEAT), dtype=jnp.float32) * sd2
        b_trans = jnp.zeros((DIM_FEAT,), dtype=jnp.float32)
        return {'feat': feat, 'W_fc': W_fc, 'att_ns': att_ns, 'att_nd': att_nd, 'W_trans': W_trans, 'b_trans': b_trans, 'src': src, 'dst': dst}
    _L2_gnn_all = _L2_gnn_setup()
    _L2_gnn_in = {k: v for k, v in _L2_gnn_all.items() if k in ('W_fc', 'att_ns', 'att_nd', 'W_trans', 'b_trans')}
    del _L2_gnn_all

    def _L3_gnn_setup():
        import jax, jax.numpy as jnp
        import numpy as np
        N_NODES = 50000
        N_EDGES = 12500
        D = 128
        key = jax.random.key(seed)
        ks = jax.random.split(key, 6)
        feat = jax.random.normal(ks[0], (N_NODES, D), dtype=jnp.float32)
        src = jax.random.randint(ks[1], (N_EDGES,), 0, N_NODES)
        dst = jax.random.randint(ks[2], (N_EDGES,), 0, N_NODES)
        W_edge = jax.random.normal(ks[3], (D, 2 * D), dtype=jnp.float32) * (1.0 / np.sqrt(2 * D))
        W_node = jax.random.normal(ks[4], (D, D), dtype=jnp.float32) * (1.0 / np.sqrt(D))
        b_node = jax.random.normal(ks[5], (D,), dtype=jnp.float32) * 0.01
        return {'feat': feat, 'src': src, 'dst': dst, 'W_edge': W_edge, 'W_node': W_node, 'b_node': b_node}
    _L3_gnn_all = _L3_gnn_setup()
    _L3_gnn_in = {k: v for k, v in _L3_gnn_all.items() if k in ('W_edge', 'W_node', 'b_node')}
    del _L3_gnn_all
    return {'x': x, 'src': src, 'dst': dst, 'edge_attr_64': edge_attr_64, 'L0_gnn_Wq': _L0_gnn_in['Wq'], 'L0_gnn_bq': _L0_gnn_in['bq'], 'L0_gnn_Wk': _L0_gnn_in['Wk'], 'L0_gnn_bk': _L0_gnn_in['bk'], 'L0_gnn_Wv': _L0_gnn_in['Wv'], 'L0_gnn_bv': _L0_gnn_in['bv'], 'L0_gnn_Wr': _L0_gnn_in['Wr'], 'L0_gnn_br': _L0_gnn_in['br'], 'L1_gnn_W1': _L1_gnn_in['W1'], 'L1_gnn_b1': _L1_gnn_in['b1'], 'L1_gnn_W2': _L1_gnn_in['W2'], 'L1_gnn_b2': _L1_gnn_in['b2'], 'L1_gnn_Wl': _L1_gnn_in['Wl'], 'L1_gnn_bl': _L1_gnn_in['bl'], 'L2_gnn_W_fc': _L2_gnn_in['W_fc'], 'L2_gnn_att_ns': _L2_gnn_in['att_ns'], 'L2_gnn_att_nd': _L2_gnn_in['att_nd'], 'L2_gnn_W_trans': _L2_gnn_in['W_trans'], 'L2_gnn_b_trans': _L2_gnn_in['b_trans'], 'L3_gnn_W_edge': _L3_gnn_in['W_edge'], 'L3_gnn_W_node': _L3_gnn_in['W_node'], 'L3_gnn_b_node': _L3_gnn_in['b_node']}

def reference(x, src, dst, edge_attr_64, L0_gnn_Wq, L0_gnn_bq, L0_gnn_Wk, L0_gnn_bk, L0_gnn_Wv, L0_gnn_bv, L0_gnn_Wr, L0_gnn_br, L1_gnn_W1, L1_gnn_b1, L1_gnn_W2, L1_gnn_b2, L1_gnn_Wl, L1_gnn_bl, L2_gnn_W_fc, L2_gnn_att_ns, L2_gnn_att_nd, L2_gnn_W_trans, L2_gnn_b_trans, L3_gnn_W_edge, L3_gnn_W_node, L3_gnn_b_node):
    import jax
    import jax.numpy as jnp

    def _L0_gnn_ref(x, edge_index, Wq, bq, Wk, bk, Wv, bv, Wr, br):
        import jax, jax.numpy as jnp
        import numpy as np
        N, E, IN_C, H, C = (50000, 12500, 128, 4, 32)
        n = x.shape[0]
        row, col = (edge_index[0], edge_index[1])
        q = (x @ Wq + bq).reshape(n, H, C)
        k = (x @ Wk + bk).reshape(n, H, C)
        v = (x @ Wv + bv).reshape(n, H, C)
        scores = jnp.einsum('ehc,ehc->eh', q[col], k[row]) / np.sqrt(C)
        m = jax.ops.segment_max(scores, col, num_segments=n)
        ex = jnp.exp(scores - m[col])
        denom = jax.ops.segment_sum(ex, col, num_segments=n)
        w = ex / denom[col]
        out = jax.ops.segment_sum(v[row] * w[:, :, None], col, num_segments=n)
        out = out.reshape(n, H * C)
        root = x @ Wr + br
        return out + root

    def _L1_gnn_ref(x, edge_index, edge_rbf, W1, b1, W2, b2, Wl, bl):
        import jax, jax.numpy as jnp
        import numpy as np
        N_NODES = 625
        N_EDGES = 10000
        IN_CH = 128
        OUT_CH = 128
        NUM_RBF = 64
        weight = jnp.maximum(edge_rbf @ W1 + b1, 0.0) @ W2 + b2
        h = x @ Wl + bl
        row, col = (edge_index[0], edge_index[1])
        msg = h[col] * weight
        out = jax.ops.segment_sum(msg, row, num_segments=x.shape[0])
        return out

    def _L2_gnn_ref(feat, W_fc, att_ns, att_nd, W_trans, b_trans, src, dst):
        import jax, jax.numpy as jnp
        import numpy as np
        N_NODES = 10000
        N_EDGES = 2500
        DIM_FEAT = 128
        NUM_HEADS = 4
        N = feat.shape[0]
        H = att_ns.shape[1]
        D = att_ns.shape[2]
        h = (feat @ W_fc).reshape(N, H, D)
        e_ns = jnp.sum(h * att_ns, axis=-1)
        e_nd = jnp.sum(h * att_nd, axis=-1)
        e = e_ns[src] + e_nd[dst]
        e = jnp.where(e > 0, e, 0.2 * e)
        m = jax.ops.segment_max(e, dst, num_segments=N)
        ex = jnp.exp(e - m[dst])
        denom = jax.ops.segment_sum(ex, dst, num_segments=N)
        a = ex / denom[dst]
        msg = h[src] * a[:, :, None]
        agg = jax.ops.segment_sum(msg, dst, num_segments=N)
        return agg.reshape(N, H * D) @ W_trans + b_trans

    def _L3_gnn_ref(feat, src, dst, W_edge, W_node, b_node):
        import jax, jax.numpy as jnp
        import numpy as np
        N_NODES = 50000
        N_EDGES = 12500
        D = 128
        N = feat.shape[0]
        eh = jnp.concatenate([feat[src], feat[dst]], axis=1) @ W_edge.T
        eh = jax.nn.relu(eh)
        s = jax.ops.segment_sum(eh, dst, num_segments=N)
        cnt = jax.ops.segment_sum(jnp.ones((dst.shape[0],), feat.dtype), dst, num_segments=N)[:, None]
        h = jnp.where(cnt > 0, s / jnp.maximum(cnt, 1.0), 0.0)
        return jax.nn.relu(h @ W_node.T + b_node)
    edge_index = jnp.stack([src, dst])
    x = _layernorm(x + _L0_gnn_ref(x, edge_index, L0_gnn_Wq, L0_gnn_bq, L0_gnn_Wk, L0_gnn_bk, L0_gnn_Wv, L0_gnn_bv, L0_gnn_Wr, L0_gnn_br), axis=-1)
    x = _layernorm(x + _L1_gnn_ref(x, edge_index, edge_attr_64, L1_gnn_W1, L1_gnn_b1, L1_gnn_W2, L1_gnn_b2, L1_gnn_Wl, L1_gnn_bl), axis=-1)
    x = _layernorm(x + _L2_gnn_ref(x, L2_gnn_W_fc, L2_gnn_att_ns, L2_gnn_att_nd, L2_gnn_W_trans, L2_gnn_b_trans, src, dst), axis=-1)
    x = _layernorm(x + _L3_gnn_ref(x, src, dst, L3_gnn_W_edge, L3_gnn_W_node, L3_gnn_b_node), axis=-1)
    return x

_drawn_inputs = setup_inputs


def setup_inputs(seed=0):
    import zlib

    import numpy as np

    out = dict(_drawn_inputs(seed))
    spreads = {'L1_gnn_b1': (0.0, 0.1),
     'L1_gnn_b2': (0.0, 0.1),
     'L1_gnn_bl': (0.0, 0.1),
     'L2_gnn_b_trans': (0.0, 0.1)}
    factors = {'L0_gnn_bq': 27.184, 'L0_gnn_bk': 200.0, 'L2_gnn_att_nd': 28.849, 'L3_gnn_b_node': 7.858}
    for name, (base, spread) in spreads.items():
        noise = np.random.default_rng([zlib.crc32(name.encode()), seed]).standard_normal(out[name].shape)
        drawn = base * np.exp(spread * noise) if base else spread * noise
        out[name] = jnp.asarray(drawn.astype(out[name].dtype))
    for name, factor in factors.items():
        out[name] = (out[name] * factor).astype(out[name].dtype)
    return out
```

```python
from contextlib import ExitStack

import numpy as np
import concourse.bass as bass
import concourse.mybir as mybir

P = 128
D = 128
H = 4
C = D // H
RBF = 64
G = 4
W0 = H * (C + 1) + H
W2 = H * (D + 1) + H
W3 = D + 1
FAR = 1.0e30
SKIP = float(1 << 22)
EPS = 1e-5

F32 = mybir.dt.float32
I32 = mybir.dt.int32
U32 = mybir.dt.uint32
ALU = mybir.AluOpType
ACT = mybir.ActivationFunctionType
X = mybir.AxisListType.X


def steps_of(edges):
    return -(-edges // (P * 2 * G)) * 2 * G


def at2(i, g, back=0):
    return 2 * i + (g + 3 - back)


def at8(i, k, back=0):
    return 8 * i + (k + 9 - back)


def landed(i, n=1, back=0):
    return (16 * n) * i + (16 * n) * (2 - back)


def start_counts(eng, groups=(), steps=(), dmas=(), n=1):
    for s in groups:
        eng.sem_inc(s, 2)
    for s in steps:
        eng.sem_inc(s, 8)
    for s in dmas:
        eng.sem_inc(s, 16 * n)


def scattered_at(i, n, back=0):
    return (16 * n) * i + (16 * n * (1 - back) + 16)


def first_dma(pool, s, ph, sems):
    for n, sem in enumerate(sems):
        pool.dma_start(ph.sb(f"first{n}", [P, 1])[:], s.eps[:]).then_inc(sem, 16)


def now(eng, value):
    return value if isinstance(value, int) else eng.snap(eng.to_reg(value))


class Kept:
    pass


class Phase:

    def __init__(self, nc, name):
        self.nc, self.name, self.ctx, self.sems = nc, name, ExitStack(), []

    def __enter__(self):
        return self

    def __exit__(self, *a):
        self.nc.clear_and_free_semaphores(self.sems)
        self.nc.all_engine_barrier()
        self.ctx.close()

    def sb(self, name, shape, dt=F32):
        return self.ctx.enter_context(self.nc.sbuf_tensor(f"{self.name}_{name}", shape, dt))

    def two(self, name, shape, dt=F32):
        return [self.sb(f"{name}{g}", shape, dt) for g in range(2)]

    def banks(self):
        return [self.ctx.enter_context(self.nc.psum_tensor(f"{self.name}_bank{j}", [P, G * D], F32)) for j in range(8)]

    def sem(self, name):
        self.sems.append(self.nc.alloc_semaphore(f"{self.name}_{name}"))
        return self.sems[-1]

    def sem2(self, name):
        return [self.sem(f"{name}{g}") for g in range(2)]


def rows4(bank):
    return bank[:].rearrange("p (k d) -> p k d", k=G)


def setup_phase(nc, s, a):
    T, N = s.T, s.N
    with Phase(nc, "setup") as ph:
        loaded, made, mult, moved, calc = (ph.sem(n) for n in ("loaded", "made", "multiplied", "moved", "calc"))
        src_i, dst_i, nxt_i = (ph.sb(n, [P, T], I32) for n in ("src_i", "dst_i", "nxt_i"))
        nxt_f, t0 = ph.sb("nxt_f", [P, T]), ph.sb("t0", [P, T])
        wfcT = ph.sb("wfcT", [P, H, D])
        wtr = ph.sb("wtr", [P, H, D + 2])
        bv_row = ph.sb("bv_row", [1, D])
        cnt = ph.sb("cnt", [P, 1])
        bank = ph.banks()
        loads = [
            (src_i[:], a["src2"]), (dst_i[:], a["dst2"]), (nxt_i[:], a["next_dst2"]),
            (s.ident[:], a["c_ident"]), (s.lower[:], a["c_lower"]), (s.headsel[:], a["c_headsel"]), (s.trash[:], a["c_trash"]),
            (s.Wq[:], a["Wq"]), (s.Wk[:], a["Wk"]), (s.Wv[:], a["Wv"]), (s.WrI[:], a["Wr"]),
            (s.W1[:], a["W1"]), (s.W2[:], a["W2"]), (s.Wl[:], a["Wl"]),
            (s.WeT[:], a["WeT"].rearrange("(h p) d -> p h d", p=P)), (s.WnT[:], a["WnT"]),
            (wfcT[:], a["WfcT"].rearrange("(h p) d -> p h d", p=P)),
            (wtr[:, :, 0:D], a["Wtr"].rearrange("(h p) d -> p h d", p=P)),
            (wtr[:, :, D:D + 2], a["att2"]),
            (s.bq[:], a["bq"].rearrange("(p a) -> p a", a=1)), (s.bk[:], a["bk"].rearrange("(p a) -> p a", a=1)),
            (s.b1[:], a["b1"].rearrange("(p a) -> p a", a=1)),
            (s.brv_row[:], a["br"].rearrange("(a n) -> a n", a=1)), (bv_row[:], a["bv"].rearrange("(a n) -> a n", a=1)),
            (s.b2_row[:], a["b2"].rearrange("(a n) -> a n", a=1)), (s.bl_row[:], a["bl"].rearrange("(a n) -> a n", a=1)),
            (s.bn_row[:], a["bn"].rearrange("(a n) -> a n", a=1)),
            (s.br_all[:], a["br"].rearrange("(a n) -> a n", a=1).to_broadcast([P, D])),
            (s.bt_all[:], a["bt"].rearrange("(a n) -> a n", a=1).to_broadcast([P, D])),
            (s.bn_all[:], a["bn"].rearrange("(a n) -> a n", a=1).to_broadcast([P, D])),
        ]
        with nc.Block() as block:
            @block.sync
            def _(sp):
                for out, in_ in loads:
                    sp.dma_start(out, in_, allow_slow_non_contiguous=True).then_inc(loaded, 16)

            @block.gpsimd
            def _(pool):
                pool.memset(s.ones_row[:], 1.0).then_inc(made, 1)
                pool.memset(s.eps[:], EPS).then_inc(made, 1)
                pool.memset(s.zeros[:], 0.0).then_inc(made, 1)

            @block.vector
            def _(dve):
                n = [0]

                def done(ins):
                    n[0] += 1
                    ins.then_inc(calc, 1)
                    dve.wait_ge(calc, n[0])

                dve.wait_ge(loaded, 16 * len(loads))
                done(dve.tensor_tensor(s.WrI[:], s.WrI[:], s.ident[:], ALU.add))
                done(dve.tensor_tensor(s.brv_row[:], s.brv_row[:], bv_row[:], ALU.add))
                done(dve.tensor_scalar(s.rbn_all[:], s.bn_all[:], 0.0, None, ALU.max))
                done(dve.tensor_copy(s.src_f[:], src_i[:]))
                done(dve.tensor_copy(s.dst_f[:], dst_i[:]))
                done(dve.tensor_copy(nxt_f[:], nxt_i[:]))
                done(dve.memset(s.same[:], 0.0))
                done(dve.tensor_tensor(s.same[:, 1:T], s.dst_f[:, 1:T], s.dst_f[:, 0:T - 1], ALU.is_equal))
                done(dve.tensor_scalar(s.cut[:], s.same[:], -1.0, FAR, ALU.add, ALU.mult))
                done(dve.tensor_tensor(t0[:], nxt_f[:], s.dst_f[:], ALU.is_equal))
                done(dve.tensor_copy(s.inner[:], t0[:]))
                done(dve.memset(s.inner[:, T - 1:T], 0))
                done(dve.scalar_tensor_tensor(t0[:], t0[:], SKIP, s.dst_f[:], ALU.mult, ALU.add))
                done(dve.tensor_copy(s.end_idx[:], t0[:]))
                ga = s.gather_idx[:].rearrange("p (n two k) -> p n two k", two=2, k=2 * G)
                done(dve.tensor_scalar(t0[:], s.src_f[:], float(N - 1), None, ALU.min))
                done(dve.tensor_copy(ga[:, :, 0, :], t0[:].rearrange("p (n k) -> p n k", k=2 * G)))
                done(dve.tensor_scalar(t0[:], s.dst_f[:], float(N - 1), None, ALU.min))
                done(dve.tensor_copy(ga[:, :, 1, :], t0[:].rearrange("p (n k) -> p n k", k=2 * G)))
                done(dve.tensor_scalar(s.to_trash[:], s.src_f[:], s.trash[:], -1.0, ALU.subtract, ALU.mult))
                head, tail = s.dst_f[:, 0:1], s.dst_f[:, T - 1:T]
                done(dve.tensor_scalar(t0[:], s.dst_f[:], head, None, ALU.is_equal))
                done(dve.tensor_reduce(cnt[:], t0[:], X, ALU.add))
                done(dve.tensor_scalar(t0[:, 0:1], s.trash[:], -float(N), float(T), ALU.add, ALU.mult))
                done(dve.scalar_tensor_tensor(t0[:, 1:2], cnt[:], -1.0, t0[:, 0:1], ALU.add, ALU.add))
                done(dve.tensor_copy(s.head_row[:], t0[:, 1:2]))
                dve.wait_ge(mult, 1)
                rowT, rowH = bank[0][:, 0:P], bank[0][:, P:2 * P]
                done(dve.tensor_scalar(s.tail_tail[:], rowT, tail, None, ALU.is_equal))
                done(dve.tensor_scalar(s.tail_head[:], rowH, tail, None, ALU.is_equal))
                done(dve.tensor_scalar(s.head_tail[:], rowT, head, None, ALU.is_equal))
                done(dve.tensor_scalar(s.head_head[:], rowH, head, None, ALU.is_equal))
                for far, m in ((s.far_tt, s.tail_tail), (s.far_th, s.tail_head), (s.far_ht, s.head_tail), (s.far_hh, s.head_head)):
                    done(dve.tensor_scalar(far[:], m[:], -1.0, FAR, ALU.add, ALU.mult))
                done(dve.tensor_tensor(t0[:, 0:1], head, tail, ALU.not_equal))
                done(dve.tensor_scalar(s.head_tail[:], s.head_tail[:], t0[:, 0:1], None, ALU.mult))
                done(dve.tensor_scalar(s.head_head[:], s.head_head[:], t0[:, 0:1], None, ALU.mult))
                for h in range(H):
                    dve.wait_ge(mult, 2 + h)
                    done(dve.tensor_copy(s.Wz[:, h, :], bank[1 + h][:, 0:D]))
                    done(dve.tensor_copy(s.att_s[:, h:h + 1], bank[1 + h][:, D:D + 1]))
                    done(dve.tensor_copy(s.att_d[:, h:h + 1], bank[1 + h][:, D + 1:D + 2]))
                dve.wait_ge(made, 3)

            @block.tensor
            def _(pe):
                pe.wait_ge(loaded, 16 * len(loads))
                pe.wait_ge(calc, 5)
                pe.transpose(bank[0][:, 0:P], s.dst_f[:, T - 1:T].to_broadcast([P, P]), s.ident[:])
                pe.transpose(bank[0][:, P:2 * P], s.dst_f[:, 0:1].to_broadcast([P, P]), s.ident[:]).then_inc(mult, 1)
                for h in range(H):
                    pe.matmul(bank[1 + h][:, 0:D + 2], wfcT[:, h, :], wtr[:, h, :], start=True, stop=True).then_inc(mult, 1)


def rowstats(dve, Y, stats, mv, stat_done, aggr_done, i, g):
    for k in range(G):
        ins = dve.bn_stats(stats[:, k, :], Y[:, k, :])
    ins.then_inc(stat_done, 1)
    four = now(dve, at2(i, g))
    dve.wait_ge(stat_done, 3)
    dve.wait_ge(stat_done, four)
    for k in range(G):
        ins = dve.bn_aggr(mv[:, k, :], stats[:, k, :])
    ins.then_inc(aggr_done, 1)


def dense0_phase(nc, s, a):
    with Phase(nc, "dense0") as ph:
        bank = ph.banks()
        x_in, xT, Y, x1 = (ph.two(n, [P, G, D]) for n in ("x_in", "xT", "Y", "x1"))
        stats, mv = ph.two("stats", [P, G, 6]), ph.two("mv", [P, G, 2])
        sd, rs = ph.two("sd", [P, G]), ph.two("rs", [P, G])
        x_loaded, x1_stored, zeroed = ph.sem2("x_loaded"), ph.sem2("x1_stored"), ph.sem("zeroed")
        transposed, xT_copied, product, Y_done, stat_done, aggr_done, sd_done, rs_done, x1_done = (
            ph.sem(n) for n in ("transposed", "xT_copied", "product", "Y_done", "stat_done", "aggr_done", "sd_done", "rs_done", "x1_done"))
        iters = s.blocks // 2

        def both(eng, work):
            with eng.Fori(0, iters - 1) as i:
                work(i, [i * (2 * s.block), i * (2 * s.block) + s.block])
            work(iters - 1, [(2 * iters - 2) * s.block, s.N - s.block])

        zero_rows = P * s.zrows
        with nc.Block() as block:
            @block.sync
            def _(sp):
                start_counts(sp, dmas=x_loaded)
                def work(i, row):
                    for g in range(2):
                        r = sp.snap(row[g]) if not isinstance(row[g], int) else row[g]
                        sp.wait_ge(transposed, at2(i, g, back=2))
                        sp.dma_start(x_in[g][:], a["x"][bass.ds(r, s.block), :].rearrange("(p k) d -> p k d", k=G)).then_inc(x_loaded[g], 16)
                both(sp, work)

            @block.gpsimd
            def _(pool):
                agg = s.agg1
                for j in range(s.zchunks):
                    pool.dma_start(agg[bass.ds(j * zero_rows, zero_rows), :].rearrange("(p r) d -> p (r d)", p=P), s.zeros[:]).then_inc(zeroed, 16)
                rest = s.N + P - s.zchunks * zero_rows
                if rest:
                    pool.dma_start(agg[s.zchunks * zero_rows:s.N + P, :].rearrange("(p r) d -> p (r d)", p=rest // s.zrest), s.zeros[0:rest // s.zrest, 0:s.zrest * D]).then_inc(zeroed, 16)
                pool.wait_ge(zeroed, 16 * (s.zchunks + (1 if rest else 0)))

            @block.tensor
            def _(pe):
                start_counts(pe, [transposed, product])

                def work(i, row):
                    for g in range(2):
                        pe.wait_ge(x_loaded[g], landed(i))
                        pe.wait_ge(xT_copied, at2(i, g, back=2))
                        for k in range(G):
                            ins = pe.transpose(bank[g][:, k * D:(k + 1) * D], x_in[g][:, k, :], s.ident[:])
                        ins.then_inc(transposed, 1)
                        pe.wait_ge(xT_copied, at2(i, g))
                        pe.wait_ge(Y_done, at2(i, g, back=2))
                        for k in range(G):
                            ins = pe.matmul(bank[2 + g][:, k * D:(k + 1) * D], xT[g][:, k, :], s.WrI[:], start=True, stop=True)
                        ins.then_inc(product, 1)
                both(pe, work)

            @block.scalar
            def _(act):
                start_counts(act, dmas=x1_stored)
                start_counts(act, [xT_copied, sd_done])

                def work(i, row):
                    for g in range(2):
                        act.wait_ge(transposed, at2(i, g))
                        act.wait_ge(product, at2(i, g, back=2))
                        act.activation(xT[g][:], rows4(bank[g]), ACT.Copy).then_inc(xT_copied, 1)
                        act.wait_ge(aggr_done, at2(i, g))
                        act.wait_ge(rs_done, at2(i, g, back=2))
                        act.activation(sd[g][:], mv[g][:, :, 1], ACT.Sqrt, bias=s.eps[:]).then_inc(sd_done, 1)
                    for g in range(2):
                        r = act.snap(row[g]) if not isinstance(row[g], int) else row[g]
                        act.wait_ge(x1_done, at2(i, g))
                        if isinstance(i, int) and g == 1:
                            act.wait_ge(x1_stored[0], landed(i))
                            act.wait_ge(x1_stored[1], landed(i, back=1))
                        act.dma_start(s.x1[bass.ds(r, s.block), :].rearrange("(p k) d -> p k d", k=G), x1[g][:]).then_inc(x1_stored[g], 16)
                both(act, work)
                for g in range(2):
                    act.wait_ge(x1_stored[g], landed(iters - 1))

            @block.vector
            def _(dve):
                start_counts(dve, [Y_done, stat_done, aggr_done, rs_done, x1_done])

                def work(i, row):
                    for g in range(2):
                        dve.wait_ge(product, at2(i, g))
                        dve.tensor_tensor(Y[g][:], rows4(bank[2 + g]), s.br_all[:].rearrange("p (a d) -> p a d", a=1).to_broadcast([P, G, D]), ALU.add).then_inc(Y_done, 1)
                        dve.wait_ge(Y_done, at2(i, g))
                        dve.wait_ge(sd_done, at2(i, g, back=2))
                        rowstats(dve, Y[g], stats[g], mv[g], stat_done, aggr_done, i, g)
                    for g in range(2):
                        dve.wait_ge(sd_done, at2(i, g))
                        dve.reciprocal(rs[g][:], sd[g][:]).then_inc(rs_done, 1)
                        dve.wait_ge(rs_done, at2(i, g))
                        dve.wait_ge(x1_stored[g], landed(i, back=1))
                        for k in range(G):
                            ins = dve.tensor_scalar(x1[g][:, k, :], Y[g][:, k, :], mv[g][:, k, 0:1], rs[g][:, k:k + 1], ALU.subtract, ALU.mult)
                        ins.then_inc(x1_done, 1)
                both(dve, work)


def forward_attention_phase(nc, s, a, layer):
    first = layer == 0
    T, iters = s.T, s.T // (2 * G)
    W, hw, table, rows_out, x_src = (W0, C + 1, s.state0, s.root0, a["x"]) if first else (W2, D + 1, s.state2, s.own2, s.x2)
    A = H * hw
    with Phase(nc, f"fwd{layer}") as ph:
        bank = ph.banks()
        xs, xd, xsT, xdT = (ph.two(n, [P, G, D]) for n in ("xs", "xd", "xsT", "xdT"))
        idx, cut8 = ph.sb("idx", [P, 4 * G], I32), ph.sb("cut8", [P, 2 * G])
        st = ph.two("st", [P, G, W])
        mh = ph.two("mh", [P, G + 1, H])
        diff = ph.two("diff", [P, G, 2, H])
        wt = ph.two("wt", [P, G, 2, A])
        dec = ph.two("dec", [P, A])
        if first:
            qT, prod, root = (ph.two(n, [P, G, D]) for n in ("qT", "prod", "root"))
        else:
            sc, leak = ph.two("sc", [P, G, H]), ph.two("leak", [P, G, H])
        idx_ready, gathered, st_stored, row_stored = ph.sem("idx_ready"), ph.sem2("gathered"), ph.sem2("st_stored"), ph.sem2("row_stored")
        names = (
            "transposed", "xT_copied", "qk_done", "qT_copied", "prod_done", "values_done", "scores_done", "root_copied",
            "sc_copied", "leak_done", "mh_done", "diff_m", "diff_done", "exp_done", "weighted", "m_stored")
        (transposed, xT_copied, qk_done, qT_copied, prod_done, values_done, scores_done, root_copied,
         sc_copied, leak_done, mh_done, diff_m, diff_done, exp_done, weighted, m_stored) = (ph.sem(n) for n in names)
        max_done, scaled, decayed, acc_done, cut_ready, cleared = (ph.sem(n) for n in ("max_done", "scaled", "decayed", "acc_done", "cut_ready", "cleared"))
        score = [v[:] for v in sc] if not first else [bank[6][:, 0:G * H].rearrange("p (k h) -> p k h", k=G)] * 2

        with nc.Block() as block:
            @block.gpsimd
            def _(pool):
                limit = pool.to_reg(s.N - 1)
                with pool.Fori(0, iters) as i:
                    for g in range(2):
                        if g == 0:
                            column, read = now(pool, i * (4 * G)), now(pool, at2(i, 1, back=2))
                            pool.wait_ge(transposed, read)
                            pool.tensor_copy(idx[:], s.gather_idx[:, bass.ds(column, 4 * G)]).then_inc(idx_ready, 1)
                            pool.wait_ge(idx_ready, i + 1)
                        freed, stored = now(pool, at2(i, g, back=2)), now(pool, landed(i, back=1))
                        pool.wait_ge(idx_ready, 1)
                        if not first:
                            pool.wait_ge(row_stored[g], stored)
                        pool.wait_ge(transposed, freed)
                        for k in range(G):
                            kk = g * G + k
                            pool.indirect_dma_start(xs[g][:, k, :], None, x_src, bass.IndirectOffsetOnAxis(ap=idx[:, kk:kk + 1], axis=0),
                                                    bounds_check=limit, oob_is_err=False).then_inc(gathered[g], 16)
                            pool.indirect_dma_start(xd[g][:, k, :], None, x_src, bass.IndirectOffsetOnAxis(ap=idx[:, 2 * G + kk:2 * G + kk + 1], axis=0),
                                                    bounds_check=limit, oob_is_err=False).then_inc(gathered[g], 16)

            @block.tensor
            def _(pe):
                start_counts(pe, [transposed, qk_done, scores_done] + [values_done] * first, [values_done] * (not first))
                with pe.Fori(0, iters) as i:
                    for g in range(2):
                        pe.wait_ge(gathered[g], 16 * 2 * G * i + 16 * 2 * G)
                        pe.wait_ge(xT_copied, at2(i, g, back=1))
                        for k in range(G):
                            pe.transpose(bank[0][:, k * D:(k + 1) * D], xs[g][:, k, :], s.ident[:])
                        for k in range(G):
                            ins = pe.transpose(bank[1][:, k * D:(k + 1) * D], xd[g][:, k, :], s.ident[:])
                        ins.then_inc(transposed, 1)
                        pe.wait_ge(xT_copied, at2(i, g))
                        if first:
                            pe.wait_ge(qT_copied, at2(i, g, back=1))
                            pe.matmul(bank[2][:], s.Wq[:], xdT[g][:], start=True, stop=True)
                            pe.wait_ge(prod_done, at2(i, g, back=1))
                            pe.matmul(bank[3][:], s.Wk[:], xsT[g][:], start=True, stop=True).then_inc(qk_done, 1)
                            pe.wait_ge(weighted, at2(i, g, back=1))
                            for k in range(G):
                                pe.matmul(bank[4][:, k * D:(k + 1) * D], xsT[g][:, k, :], s.Wv[:], start=True, stop=True)
                            pe.wait_ge(root_copied, at2(i, g, back=1))
                            for k in range(G):
                                pe.matmul(bank[5][:, k * D:(k + 1) * D], xdT[g][:, k, :], s.WrI[:], start=True, stop=False)
                                ins = pe.matmul(bank[5][:, k * D:(k + 1) * D], s.ones_row[:], s.brv_row[:], start=False, stop=True)
                            ins.then_inc(values_done, 1)
                            pe.wait_ge(prod_done, at2(i, g))
                            pe.wait_ge(diff_m, at2(i, g, back=1))
                            for k in range(G):
                                ins = pe.matmul(bank[6][:, k * H:(k + 1) * H], prod[g][:, k, :], s.headsel[:], start=True, stop=True)
                            ins.then_inc(scores_done, 1)
                        else:
                            pe.wait_ge(sc_copied, at2(i, g, back=1))
                            for k in range(G):
                                pe.matmul(bank[6][:, k * H:(k + 1) * H], xsT[g][:, k, :], s.att_s[:], start=True, stop=False)
                                ins = pe.matmul(bank[6][:, k * H:(k + 1) * H], xdT[g][:, k, :], s.att_d[:], start=False, stop=True)
                            ins.then_inc(scores_done, 1)
                            for k in range(G):
                                pe.wait_ge(scaled, at8(i, g * G + k, back=4))
                                pe.matmul(bank[2 + k][:], xsT[g][:, k, :], s.Wz[:], start=True, stop=True).then_inc(values_done, 1)

            @block.scalar
            def _(act):
                start_counts(act, [xT_copied, qT_copied, root_copied, exp_done], [scaled])
                with act.Fori(0, iters) as i:
                    for g in range(2):
                        act.wait_ge(transposed, at2(i, g))
                        if first:
                            act.wait_ge(values_done, at2(i, g, back=2))
                        else:
                            act.wait_ge(values_done, at8(i, g * G + 3, back=8))
                        act.activation(xsT[g][:], rows4(bank[0]), ACT.Copy)
                        act.activation(xdT[g][:], rows4(bank[1]), ACT.Copy).then_inc(xT_copied, 1)
                        if first:
                            act.wait_ge(qk_done, at2(i, g))
                            act.wait_ge(prod_done, at2(i, g, back=2))
                            act.activation(qT[g][:], rows4(bank[2]), ACT.Identity, bias=s.bq[:]).then_inc(qT_copied, 1)
                            act.wait_ge(values_done, at2(i, g))
                            act.wait_ge(row_stored[g], landed(i, back=1))
                            act.activation(root[g][:], rows4(bank[5]), ACT.Copy).then_inc(root_copied, 1)
                        act.wait_ge(diff_done, at2(i, g))
                        act.wait_ge(acc_done, at8(i, g * G + 3, back=8))
                        act.activation(wt[g][:].rearrange("p k two (h w) -> p (k two) h w", h=H)[:, :, :, hw - 1],
                                       diff[g][:].rearrange("p k two h -> p (k two) h"), ACT.Exp).then_inc(exp_done, 1)
                        if not first:
                            act.wait_ge(exp_done, at2(i, g))
                            for k in range(G):
                                act.wait_ge(values_done, at8(i, g * G + k))
                                for h in range(H):
                                    ins = act.activation(wt[g][:, k, 1, h * hw:h * hw + D], bank[2 + k][:, h * D:(h + 1) * D], ACT.Copy,
                                                         scale=wt[g][:, k, 1, (h + 1) * hw - 1:(h + 1) * hw])
                                ins.then_inc(scaled, 1)

            @block.vector
            def _(dve):
                start_counts(dve, [prod_done, mh_done, diff_m, diff_done, weighted, m_stored, sc_copied, leak_done], [max_done, decayed, acc_done])
                dve.memset(st[1][:], 0.0).then_inc(cleared, 1)
                dve.memset(mh[1][:], 0.0).then_inc(cleared, 1)
                dve.wait_ge(cleared, 2)
                with dve.Fori(0, iters) as i:
                    for g in range(2):
                        if g == 0:
                            dve.wait_ge(diff_done, at2(i, g, back=1))
                            dve.tensor_copy(cut8[:], s.cut[:, bass.ds(i * (2 * G), 2 * G)]).then_inc(cut_ready, 1)
                            dve.wait_ge(cut_ready, i + 1)
                        if first:
                            dve.wait_ge(qk_done, at2(i, g))
                            dve.wait_ge(qT_copied, at2(i, g))
                            dve.wait_ge(scores_done, at2(i, g, back=2))
                            dve.scalar_tensor_tensor(prod[g][:], rows4(bank[3]), s.bk[:], qT[g][:], ALU.add, ALU.mult).then_inc(prod_done, 1)
                            dve.wait_ge(scores_done, at2(i, g))
                        else:
                            dve.wait_ge(scores_done, at2(i, g))
                            dve.tensor_copy(leak[g][:], bank[6][:, 0:G * H].rearrange("p (k h) -> p k h", k=G)).then_inc(sc_copied, 1)
                            dve.wait_ge(sc_copied, at2(i, g))
                            dve.wait_ge(diff_m, at2(i, g, back=2))
                            dve.scalar_tensor_tensor(sc[g][:], leak[g][:], 0.2, leak[g][:], ALU.mult, ALU.max).then_inc(leak_done, 1)
                            dve.wait_ge(leak_done, at2(i, g))
                        dve.wait_ge(max_done, at8(i, g * G, back=1))
                        dve.wait_ge(m_stored, at2(i, g, back=2))
                        dve.tensor_copy(mh[g][:, 0, :], mh[1 - g][:, G, :]).then_inc(mh_done, 1)
                        dve.wait_ge(mh_done, at2(i, g))
                        for k in range(G):
                            kk = g * G + k
                            dve.scalar_tensor_tensor(mh[g][:, k + 1, :], mh[g][:, k, :], cut8[:, kk:kk + 1], score[g][:, k, :], ALU.add, ALU.max).then_inc(max_done, 1)
                            dve.wait_ge(max_done, at8(i, kk))
                        dve.wait_ge(exp_done, at2(i, g, back=2))
                        dve.tensor_tensor(diff[g][:, :, 0, :], mh[g][:, 0:G, :], mh[g][:, 1:G + 1, :], ALU.subtract)
                        dve.tensor_tensor(diff[g][:, :, 1, :], score[g], mh[g][:, 1:G + 1, :], ALU.subtract).then_inc(diff_m, 1)
                        dve.wait_ge(diff_m, at2(i, g))
                        cuts = cut8[:, g * G:(g + 1) * G].rearrange("p (k a) -> p k a", a=1).to_broadcast([P, G, H])
                        dve.tensor_tensor(diff[g][:, :, 0, :], diff[g][:, :, 0, :], cuts, ALU.add).then_inc(diff_done, 1)
                        dve.wait_ge(st_stored[g], landed(i, back=1))
                        dve.tensor_copy(st[g][:, :, A:A + H], mh[g][:, 1:G + 1, :]).then_inc(m_stored, 1)
                        dve.wait_ge(exp_done, at2(i, g))
                        if first:
                            dve.wait_ge(values_done, at2(i, g))
                            w4 = wt[g][:, :, 1, :].rearrange("p k (h w) -> p k h w", h=H)
                            dve.tensor_tensor(w4[:, :, :, 0:C], bank[4][:].rearrange("p (k h c) -> p k h c", k=G, h=H),
                                              w4[:, :, :, C:C + 1].to_broadcast([P, G, H, C]), ALU.mult).then_inc(weighted, 1)
                            dve.wait_ge(weighted, at2(i, g))
                        for k in range(G):
                            kk = g * G + k
                            prev = st[g][:, k - 1, 0:A] if k else st[1 - g][:, G - 1, 0:A]
                            dve.wait_ge(acc_done, at8(i, kk, back=1))
                            if not first:
                                dve.wait_ge(scaled, at8(i, kk))
                                for h in range(H):
                                    ins = dve.scalar_tensor_tensor(st[g][:, k, h * hw:(h + 1) * hw], prev[:, h * hw:(h + 1) * hw],
                                                                   wt[g][:, k, 0, (h + 1) * hw - 1:(h + 1) * hw], wt[g][:, k, 1, h * hw:(h + 1) * hw],
                                                                   ALU.mult, ALU.add)
                                ins.then_inc(acc_done, 1)
                                continue
                            dve.tensor_tensor(dec[k % 2][:].rearrange("p (h w) -> p h w", h=H), prev.rearrange("p (h w) -> p h w", h=H),
                                              wt[g][:, k, 0, :].rearrange("p (h w) -> p h w", h=H)[:, :, hw - 1:hw].to_broadcast([P, H, hw]), ALU.mult).then_inc(decayed, 1)
                            dve.wait_ge(decayed, at8(i, kk))
                            dve.tensor_tensor(st[g][:, k, 0:A], dec[k % 2][:], wt[g][:, k, 1, :], ALU.add).then_inc(acc_done, 1)

            @block.sync
            def _(sp):
                start_counts(sp, dmas=row_stored + st_stored)
                with sp.Fori(0, iters) as i:
                    for g in range(2):
                        t, group, step = (now(sp, v) for v in (i * (2 * G) + g * G, at2(i, g), at8(i, g * G + 3)))
                        if first:
                            sp.wait_ge(root_copied, group)
                            sp.dma_start(rows_out[:, bass.ds(t, G), :], root[g][:]).then_inc(row_stored[g], 16)
                        else:
                            sp.wait_ge(gathered[g], 16 * 2 * G * i + 16 * 2 * G)
                            sp.dma_start(rows_out[:, bass.ds(t, G), :], xd[g][:]).then_inc(row_stored[g], 16)
                        sp.wait_ge(m_stored, group)
                        sp.wait_ge(acc_done, step)
                        sp.dma_start(table[:, bass.ds(t, G), :], st[g][:]).then_inc(st_stored[g], 16)
                for g in range(2):
                    sp.wait_ge(row_stored[g], landed(iters - 1))
                    sp.wait_ge(st_stored[g], landed(iters - 1))


def patch_phase(nc, s, table, W, hw):
    T = s.T
    A = H * hw if hw else W
    flat = table.rearrange("p t w -> (p t) w")
    halves = [(0, A)] if A <= G * D else [(0, A // 2), (A // 2, A)]
    with Phase(nc, f"patch{W}") as ph:
        bank = ph.banks()
        head, tail, head_out, tail_out = (ph.sb(n, [P, W]) for n in ("head", "tail", "head_out", "tail_out"))
        far = ph.sb("far", [P, G, D])
        red, best = ph.sb("red", [P, 4, H]), ph.sb("best", [P, 2, H])
        diff, wts = ph.sb("diff", [P, 2, H]), ph.sb("wts", [P, 2, H])
        head_loaded, loaded, turned, calc, exp_done, joined, stored = (
            ph.sem(n) for n in ("head_loaded", "loaded", "turned", "calc", "exp_done", "joined", "stored"))
        sums = [0]
        with nc.Block() as block:
            @block.gpsimd
            def _(pool):
                pool.indirect_dma_start(head[:], None, flat, bass.IndirectOffsetOnAxis(ap=s.head_row[:], axis=0),
                                        bounds_check=P * T - 1, oob_is_err=False).then_inc(head_loaded, 16)

            @block.sync
            def _(sp):
                sp.dma_start(tail[:], table[:, T - 1, :]).then_inc(loaded, 16)

            @block.vector
            def _(dve):
                n = [0]

                def done(ins):
                    n[0] += 1
                    ins.then_inc(calc, 1)
                    dve.wait_ge(calc, n[0])

                dve.wait_ge(loaded, 16)
                dve.wait_ge(head_loaded, 16)
                if hw:
                    dve.wait_ge(turned, 1)
                    for j, (src, m) in enumerate(((0, s.far_tt), (1, s.far_th), (0, s.far_ht), (1, s.far_hh))):
                        done(dve.tensor_tensor(far[:], rows4(bank[src]), m[:].rearrange("p (a d) -> p a d", a=1).to_broadcast([P, G, P]), ALU.add))
                        done(dve.tensor_reduce(red[:, j, :], far[:], X, ALU.max))
                    for j in range(2):
                        done(dve.tensor_tensor(best[:, j, :], red[:, 2 * j, :], red[:, 2 * j + 1, :], ALU.max))
                    for j, part in enumerate((tail, head)):
                        done(dve.tensor_tensor(diff[:, j, :], part[:, A:A + H], best[:, j, :], ALU.subtract))
                    sums[0] = n[0]
                    dve.wait_ge(exp_done, 1)
                    for j, part in enumerate((tail, head)):
                        v = part[:, 0:A].rearrange("p (h w) -> p h w", h=H)
                        done(dve.tensor_tensor(v, v, wts[:, j, :].rearrange("p (h a) -> p h a", a=1).to_broadcast([P, H, hw]), ALU.mult))
                        done(dve.tensor_copy((tail_out, head_out)[j][:, A:A + H], best[:, j, :]))
                else:
                    done(dve.tensor_copy(best[:, 0, :], s.trash[:].to_broadcast([P, H])))
                sums.append(n[0])
                dve.wait_ge(joined, 1)
                for j, out in enumerate((tail_out, head_out)):
                    for b, (lo, hi) in enumerate(halves):
                        done(dve.tensor_copy(out[:, lo:hi], bank[2 + 2 * j + b][:, 0:hi - lo]))
                sums.append(n[0])

            @block.scalar
            def _(act):
                if hw:
                    act.wait_ge(calc, sums[0])
                    act.activation(wts[:], diff[:], ACT.Exp).then_inc(exp_done, 1)

            @block.tensor
            def _(pe):
                if hw:
                    pe.wait_ge(loaded, 16)
                    pe.wait_ge(head_loaded, 16)
                    for j, part in enumerate((tail, head)):
                        for h in range(H):
                            ins = pe.transpose(bank[j][:, h * P:(h + 1) * P], part[:, A + h:A + h + 1].to_broadcast([P, P]), s.ident[:])
                    ins.then_inc(turned, 1)
                pe.wait_ge(loaded, 16)
                pe.wait_ge(head_loaded, 16)
                pe.wait_ge(calc, sums[1])
                for j, (from_tail, from_head) in enumerate(((s.tail_tail, s.head_tail), (s.tail_head, s.head_head))):
                    for b, (lo, hi) in enumerate(halves):
                        pe.matmul(bank[2 + 2 * j + b][:, 0:hi - lo], from_tail[:], tail[:, lo:hi], start=True, stop=False)
                        ins = pe.matmul(bank[2 + 2 * j + b][:, 0:hi - lo], from_head[:], head[:, lo:hi], start=False, stop=True)
                ins.then_inc(joined, 1)

        with nc.Block() as block:
            @block.gpsimd
            def _(pool):
                pool.indirect_dma_start(flat, bass.IndirectOffsetOnAxis(ap=s.head_row[:], axis=0), head_out[:], None,
                                        bounds_check=P * T - 1, oob_is_err=False).then_inc(stored, 16)
                pool.wait_ge(stored, 16)
                pool.dma_start(table[:, T - 1, :], tail_out[:]).then_inc(stored, 16)
                pool.wait_ge(stored, 32)


def backward0_phase(nc, s, a):
    T, iters, hw = s.T, s.T // (2 * G), C + 1
    with Phase(nc, "bwd0") as ph:
        bank = ph.banks()
        st, root, edge = ph.two("st", [P, G, W0]), ph.two("root", [P, G, D]), ph.two("edge", [P, G, RBF])
        edgeT, hid, filt = ph.two("edgeT", [RBF, G, P]), ph.two("hid", [P, G, P]), ph.two("filt", [P, G, D])
        inv, Y, x1, x1T, msg, merged, equal = ph.two("inv", [P, G, H]), *(ph.two(n, [P, G, D]) for n in ("Y", "x1", "x1T", "msg", "merged", "equal"))
        stats, mv, sd, rs = ph.two("stats", [P, G, 6]), ph.two("mv", [P, G, 2]), ph.two("sd", [P, G]), ph.two("rs", [P, G])
        earlier, dup, add_f, add_idx = ph.two("earlier", [P, G, D]), ph.two("dup", [P, G]), ph.two("add_f", [P, G]), ph.two("add_idx", [P, G], I32)
        end_idx, inner, srcs, to_trash = ph.two("end_idx", [P, G], I32), ph.two("inner", [P, G], U32), ph.two("srcs", [P, G]), ph.two("to_trash", [P, G])
        loaded, edge_loaded, x1_stored, added, group_before_added = (
            ph.sem2("loaded"), ph.sem2("edge_loaded"), ph.sem2("x1_stored"), ph.sem("added"), ph.sem("group_before_added"))
        names = ("edgeT_done", "edgeT_copied", "hid_done", "hid_copied", "filt_done", "filt_copied", "x1T_done", "x1T_copied", "h_done",
                 "merge_done", "merge_copied", "src_rows", "inv_done", "Y_scaled", "Y_done", "stat_done", "aggr_done", "sd_done", "rs_done",
                 "rows_done", "msg_done", "equal_done", "dup_done", "near_done", "idx_sum", "add_ready", "meta_ready", "end_ready")
        (edgeT_done, edgeT_copied, hid_done, hid_copied, filt_done, filt_copied, x1T_done, x1T_copied, h_done, merge_done,
         merge_copied, src_rows, inv_done, Y_scaled, Y_done, stat_done, aggr_done, sd_done, rs_done, rows_done, msg_done,
         equal_done, dup_done, near_done, idx_sum, add_ready, meta_ready, end_ready) = (ph.sem(n) for n in names)
        spread, cleared = ph.sem("spread"), ph.sem("cleared")

        def last(eng, i):
            return eng.snap(T - 2 * G - (2 * G) * i)

        def step(base, g):
            return base + G * (1 - g)

        with nc.Block() as block:
            @block.sync
            def _(sp):
                start_counts(sp, dmas=edge_loaded)
                start_counts(sp, dmas=loaded, n=2)
                with sp.Fori(0, iters) as i:
                    base = last(sp, i)
                    for g in range(2):
                        t, freed = now(sp, step(base, g)), now(sp, at2(i, g, back=2))
                        sp.wait_ge(hid_done, freed)
                        sp.dma_start(edge[g][:], a["edge2"][:, bass.ds(t, G), :]).then_inc(edge_loaded[g], 16)
                        sp.wait_ge(Y_done, freed)
                        sp.dma_start(st[g][:], s.state0[:, bass.ds(t, G), :]).then_inc(loaded[g], 16)
                        sp.dma_start(root[g][:], s.root0[:, bass.ds(t, G), :]).then_inc(loaded[g], 16)

            @block.gpsimd
            def _(pool):
                first_dma(pool, s, ph, [*x1_stored, added])
                limit, trash_limit = pool.to_reg(s.N - 1), pool.to_reg(s.N + P - 1)
                start_counts(pool, [end_ready, group_before_added])
                with pool.Fori(0, iters) as i:
                    base = last(pool, i)
                    for g in range(2):
                        t, freed, group, spread_all = (now(pool, v) for v in (step(base, g), scattered_at(i, G, back=1), at2(i, g), at8(i, g * G + G - 1)))
                        pool.wait_ge(x1_stored[g], freed)
                        pool.tensor_copy(end_idx[g][:], s.end_idx[:, bass.ds(t, G)]).then_inc(end_ready, 1)
                        befores = [now(pool, 16 * 2 * G * i + 16 * (g * G + k + 1)) for k in range(G)]
                        pool.wait_ge(end_ready, 3)
                        pool.wait_ge(end_ready, group)
                        pool.wait_ge(spread, spread_all)
                        pool.wait_ge(merge_copied, group)
                        pool.wait_ge(add_ready, group)
                        for k in reversed(range(G)):
                            pool.wait_ge(end_ready, 3)
                            pool.wait_ge(added, befores[G - 1 - k])
                            if k == G - 1:
                                pool.sem_inc(group_before_added, 1)
                                pool.wait_ge(end_ready, 3)
                            pool.indirect_dma_start(s.agg1, bass.IndirectOffsetOnAxis(ap=add_idx[g][:, k:k + 1], axis=0), merged[g][:, k, :], None,
                                                    bounds_check=trash_limit, oob_is_err=True, compute_op=ALU.add).then_inc(added, 16)
                            pool.indirect_dma_start(s.x1, bass.IndirectOffsetOnAxis(ap=end_idx[g][:, k:k + 1], axis=0), x1[g][:, k, :], None,
                                                    bounds_check=limit, oob_is_err=False).then_inc(x1_stored[g], 16)
                pool.wait_ge(added, 16 * T + 16)
                for g in range(2):
                    pool.wait_ge(x1_stored[g], scattered_at(iters - 1, G))

            @block.tensor
            def _(pe):
                start_counts(pe, [edgeT_done, hid_done, filt_done, x1T_done, h_done, merge_done, src_rows])
                with pe.Fori(0, iters) as i:
                    for g in range(2):
                        pe.wait_ge(meta_ready, at2(i, g))
                        pe.wait_ge(equal_done, at2(i, g, back=1))
                        for k in range(G):
                            ins = pe.transpose(bank[0][:, k * P:(k + 1) * P], srcs[g][:, k:k + 1].to_broadcast([P, P]), s.ident[:])
                        ins.then_inc(src_rows, 1)
                        arrived, freed = now(pe, landed(i)), now(pe, at2(i, g, back=1))
                        pe.wait_ge(meta_ready, 3)
                        pe.wait_ge(edge_loaded[g], arrived)
                        pe.wait_ge(edgeT_copied, freed)
                        for k in range(G):
                            ins = pe.transpose(bank[1][0:RBF, k * P:(k + 1) * P], edge[g][:, k, :], s.ident[:])
                        ins.then_inc(edgeT_done, 1)
                        pe.wait_ge(edgeT_copied, at2(i, g))
                        pe.wait_ge(hid_copied, at2(i, g, back=1))
                        pe.matmul(bank[2][:], s.W1[:], edgeT[g][:], start=True, stop=True).then_inc(hid_done, 1)
                        pe.wait_ge(hid_copied, at2(i, g))
                        pe.wait_ge(filt_copied, at2(i, g, back=1))
                        for k in range(G):
                            pe.matmul(bank[3][:, k * D:(k + 1) * D], hid[g][:, k, :], s.W2[:], start=True, stop=False)
                            ins = pe.matmul(bank[3][:, k * D:(k + 1) * D], s.ones_row[:], s.b2_row[:], start=False, stop=True)
                        ins.then_inc(filt_done, 1)
                        pe.wait_ge(spread, at8(i, g * G + G - 1))
                        pe.wait_ge(x1T_copied, at2(i, g, back=1))
                        for k in range(G):
                            ins = pe.transpose(bank[4][:, k * D:(k + 1) * D], x1[g][:, k, :], s.ident[:])
                        ins.then_inc(x1T_done, 1)
                        pe.wait_ge(x1T_copied, at2(i, g))
                        pe.wait_ge(msg_done, at2(i, g, back=1))
                        for k in range(G):
                            pe.matmul(bank[5][:, k * D:(k + 1) * D], x1T[g][:, k, :], s.Wl[:], start=True, stop=False)
                            ins = pe.matmul(bank[5][:, k * D:(k + 1) * D], s.ones_row[:], s.bl_row[:], start=False, stop=True)
                        ins.then_inc(h_done, 1)
                        pe.wait_ge(msg_done, at2(i, g))
                        pe.wait_ge(equal_done, at2(i, g))
                        pe.wait_ge(merge_copied, at2(i, g, back=1))
                        for k in range(G):
                            ins = pe.matmul(bank[6][:, k * D:(k + 1) * D], equal[g][:, k, :], msg[g][:, k, :], start=True, stop=True)
                        ins.then_inc(merge_done, 1)

            @block.scalar
            def _(act):
                start_counts(act, [edgeT_copied, hid_copied, filt_copied, x1T_copied, merge_copied, sd_done])
                with act.Fori(0, iters) as i:
                    for g in range(2):
                        act.wait_ge(edgeT_done, at2(i, g))
                        act.wait_ge(hid_done, at2(i, g, back=2))
                        act.activation(edgeT[g][:], bank[1][0:RBF, :].rearrange("p (k d) -> p k d", k=G), ACT.Copy).then_inc(edgeT_copied, 1)
                        act.wait_ge(hid_done, at2(i, g))
                        act.wait_ge(filt_done, at2(i, g, back=2))
                        act.activation(hid[g][:], rows4(bank[2]), ACT.Relu, bias=s.b1[:]).then_inc(hid_copied, 1)
                        act.wait_ge(aggr_done, at2(i, g))
                        act.wait_ge(rs_done, at2(i, g, back=2))
                        act.activation(sd[g][:], mv[g][:, :, 1], ACT.Sqrt, bias=s.eps[:]).then_inc(sd_done, 1)
                        act.wait_ge(filt_done, at2(i, g))
                        act.wait_ge(msg_done, at2(i, g, back=2))
                        act.activation(filt[g][:], rows4(bank[3]), ACT.Copy).then_inc(filt_copied, 1)
                        act.wait_ge(x1T_done, at2(i, g))
                        act.wait_ge(h_done, at2(i, g, back=2))
                        act.activation(x1T[g][:], rows4(bank[4]), ACT.Copy).then_inc(x1T_copied, 1)
                        act.wait_ge(merge_done, at2(i, g))
                        act.wait_ge(group_before_added, at2(i, g, back=1))
                        act.activation(merged[g][:], rows4(bank[6]), ACT.Copy).then_inc(merge_copied, 1)

            @block.vector
            def _(dve):
                start_counts(dve, [meta_ready, inv_done, Y_scaled, Y_done, stat_done, aggr_done, rs_done, rows_done,
                                   msg_done, equal_done, dup_done, near_done, idx_sum, add_ready], [spread])
                dve.memset(x1[1][:], 0.0).then_inc(cleared, 1)
                dve.wait_ge(cleared, 1)
                with dve.Fori(0, iters) as i:
                    base = last(dve, i)
                    for g in range(2):
                        t = dve.snap(step(base, g))
                        dve.wait_ge(src_rows, at2(i, g, back=2))
                        dve.tensor_copy(srcs[g][:], s.src_f[:, bass.ds(t, G)])
                        dve.tensor_copy(to_trash[g][:], s.to_trash[:, bass.ds(t, G)])
                        dve.tensor_copy(inner[g][:], s.inner[:, bass.ds(t, G)]).then_inc(meta_ready, 1)
                        dve.wait_ge(loaded[g], landed(i, 2))
                        sums = st[g][:, :, 0:H * hw].rearrange("p k (h w) -> p k h w", h=H)
                        dve.reciprocal(inv[g][:], sums[:, :, :, C]).then_inc(inv_done, 1)
                        dve.wait_ge(inv_done, at2(i, g))
                        y4 = Y[g][:].rearrange("p k (h c) -> p k h c", h=H)
                        dve.tensor_tensor(y4, sums[:, :, :, 0:C], inv[g][:].rearrange("p k (h a) -> p k h a", a=1).to_broadcast([P, G, H, C]), ALU.mult).then_inc(Y_scaled, 1)
                        dve.wait_ge(Y_scaled, at2(i, g))
                        dve.tensor_tensor(Y[g][:], Y[g][:], root[g][:], ALU.add).then_inc(Y_done, 1)
                        dve.wait_ge(Y_done, at2(i, g))
                        dve.wait_ge(sd_done, at2(i, g, back=2))
                        rowstats(dve, Y[g], stats[g], mv[g], stat_done, aggr_done, i, g)
                        dve.wait_ge(meta_ready, at2(i, g))
                        dve.wait_ge(src_rows, at2(i, g))
                        dve.wait_ge(merge_done, at2(i, g, back=2))
                        dve.tensor_tensor(equal[g][:], rows4(bank[0]), srcs[g][:].rearrange("p (k a) -> p k a", a=1).to_broadcast([P, G, P]), ALU.is_equal).then_inc(equal_done, 1)
                        dve.wait_ge(equal_done, at2(i, g))
                        for k in range(G):
                            ins = dve.tensor_tensor_reduce(out=earlier[g][:, k, :], in0=equal[g][:, k, :], in1=s.lower[:], scale=1.0, scalar=0.0,
                                                           op0=ALU.mult, op1=ALU.add, accum_out=dup[g][:, k:k + 1])
                        ins.then_inc(dup_done, 1)
                        dve.wait_ge(dup_done, at2(i, g))
                        dve.scalar_tensor_tensor(add_f[g][:], dup[g][:], 1.0, to_trash[g][:], ALU.min, ALU.mult).then_inc(idx_sum, 1)
                        dve.wait_ge(idx_sum, at2(i, g))
                        dve.wait_ge(group_before_added, at2(i, g, back=1))
                        dve.tensor_tensor(add_idx[g][:], add_f[g][:], srcs[g][:], ALU.add).then_inc(add_ready, 1)
                        dve.wait_ge(sd_done, at2(i, g))
                        dve.reciprocal(rs[g][:], sd[g][:]).then_inc(rs_done, 1)
                        dve.wait_ge(rs_done, at2(i, g))
                        dve.wait_ge(x1_stored[g], scattered_at(i, G, back=1))
                        dve.wait_ge(x1T_done, at2(i, g, back=2))
                        for k in range(G):
                            ins = dve.tensor_scalar(x1[g][:, k, :], Y[g][:, k, :], mv[g][:, k, 0:1], rs[g][:, k:k + 1], ALU.subtract, ALU.mult)
                        ins.then_inc(rows_done, 1)
                        dve.wait_ge(rows_done, at2(i, g))
                        for k in reversed(range(G)):
                            later = x1[g][:, k + 1, :] if k < G - 1 else x1[1 - g][:, 0, :]
                            n = g * G + G - 1 - k
                            before = now(dve, at8(i, n, back=1))
                            dve.wait_ge(cleared, 1)
                            dve.wait_ge(spread, before)
                            ins = dve.copy_predicated(x1[g][:, k, :], inner[g][:, k:k + 1].to_broadcast([P, D]), later)
                            ins.then_inc(spread, 1)
                        dve.wait_ge(h_done, at2(i, g))
                        dve.wait_ge(filt_copied, at2(i, g))
                        dve.wait_ge(merge_done, at2(i, g, back=2))
                        dve.tensor_tensor(msg[g][:], rows4(bank[5]), filt[g][:], ALU.mult).then_inc(msg_done, 1)


def norm_rows(dve, act_sd, Y, out, mv, sd, rs, rs_done, out_done, i, g):
    dve.wait_ge(act_sd, at2(i, g))
    dve.reciprocal(rs[:], sd[:]).then_inc(rs_done, 1)
    dve.wait_ge(rs_done, at2(i, g))
    for k in range(G):
        ins = dve.tensor_scalar(out[:, k, :], Y[:, k, :], mv[:, k, 0:1], rs[:, k:k + 1], ALU.subtract, ALU.mult)
    ins.then_inc(out_done, 1)


def dense1_phase(nc, s, a):
    iters = s.blocks // 2
    with Phase(nc, "dense1") as ph:
        xin, agg = ph.two("xin", [P, G, D]), ph.two("agg", [P, G, D])
        Y = [ph.two(f"Y{j}", [P, G, D]) for j in range(3)]
        out = [ph.two(f"out{j}", [P, G, D]) for j in range(3)]
        stats, mv, sd, rs = ([ph.two(f"{n}{j}", [P, G] + w) for j in range(3)] for n, w in (("stats", [6]), ("mv", [2]), ("sd", []), ("rs", [])))
        loaded, stored = ph.sem2("loaded"), [ph.sem2(f"stored{j}") for j in range(3)]
        Y_done, stat_done, aggr_done, sd_done, rs_done, out_done = ([ph.sem(f"{n}{j}") for j in range(3)] for n in ("Y_done", "stat_done", "aggr_done", "sd_done", "rs_done", "out_done"))
        tables = (s.x2, s.x3, s.out)

        def both(eng, work):
            with eng.Fori(0, iters - 1) as i:
                work(i, [i * (2 * s.block), i * (2 * s.block) + s.block])
            work(iters - 1, [(2 * iters - 2) * s.block, s.N - s.block])

        def row_of(eng, r):
            return r if isinstance(r, int) else eng.snap(r)

        with nc.Block() as block:
            @block.sync
            def _(sp):
                start_counts(sp, dmas=loaded, n=2)
                def work(i, row):
                    rows = [row_of(sp, r) for r in row]
                    for g in range(2):
                        sp.wait_ge(Y_done[0], at2(i, g, back=2))
                        sp.dma_start(xin[g][:], s.x1[bass.ds(rows[g], s.block), :].rearrange("(p k) d -> p k d", k=G)).then_inc(loaded[g], 16)
                        sp.dma_start(agg[g][:], s.agg1[bass.ds(rows[g], s.block), :].rearrange("(p k) d -> p k d", k=G)).then_inc(loaded[g], 16)
                both(sp, work)

            @block.gpsimd
            def _(pool):
                start_counts(pool, Y_done)
                biases = [None, s.bt_all, s.rbn_all]

                def work(i, row):
                    for j in range(3):
                        for g in range(2):
                            if j == 0:
                                pool.wait_ge(loaded[g], landed(i, 2))
                                one, two = xin[g][:], agg[g][:]
                            else:
                                pool.wait_ge(out_done[j - 1], at2(i, g))
                                one, two = out[j - 1][g][:], biases[j][:].rearrange("p (a d) -> p a d", a=1).to_broadcast([P, G, D])
                            pool.wait_ge(out_done[j], at2(i, g, back=2))
                            pool.tensor_tensor(Y[j][g][:], one, two, ALU.add).then_inc(Y_done[j], 1)
                both(pool, work)

            @block.vector
            def _(dve):
                start_counts(dve, [*stat_done, *aggr_done, *rs_done, *out_done])

                def work(i, row):
                    for j in range(3):
                        for g in range(2):
                            dve.wait_ge(Y_done[j], at2(i, g))
                            dve.wait_ge(sd_done[j], at2(i, g, back=2))
                            rowstats(dve, Y[j][g], stats[j][g], mv[j][g], stat_done[j], aggr_done[j], i, g)
                        for g in range(2):
                            dve.wait_ge(stored[j][g], landed(i, back=1))
                            if j < 2:
                                dve.wait_ge(Y_done[j + 1], at2(i, g, back=2))
                            norm_rows(dve, sd_done[j], Y[j][g], out[j][g], mv[j][g], sd[j][g], rs[j][g], rs_done[j], out_done[j], i, g)
                both(dve, work)

            @block.scalar
            def _(act):
                start_counts(act, dmas=stored[0] + stored[1] + stored[2])
                start_counts(act, sd_done)

                def work(i, row):
                    rows = [row_of(act, r) for r in row]
                    for j in range(3):
                        for g in range(2):
                            act.wait_ge(aggr_done[j], at2(i, g))
                            act.wait_ge(rs_done[j], at2(i, g, back=2))
                            act.activation(sd[j][g][:], mv[j][g][:, :, 1], ACT.Sqrt, bias=s.eps[:]).then_inc(sd_done[j], 1)
                        for g in range(2):
                            act.wait_ge(out_done[j], at2(i, g))
                            if isinstance(i, int) and g == 1:
                                act.wait_ge(stored[j][0], landed(i))
                                act.wait_ge(stored[j][1], landed(i, back=1))
                            act.dma_start(tables[j][bass.ds(rows[g], s.block), :].rearrange("(p k) d -> p k d", k=G), out[j][g][:]).then_inc(stored[j][g], 16)
                both(act, work)
                for j in range(3):
                    for g in range(2):
                        act.wait_ge(stored[j][g], landed(iters - 1))


def backward2_phase(nc, s, a):
    T, iters, hw = s.T, s.T // (2 * G), D + 1
    with Phase(nc, "bwd2") as ph:
        bank = ph.banks()
        st, own, inv = ph.two("st", [P, G, W2]), ph.two("own", [P, G, D]), ph.two("inv", [P, G, H])
        part, x3 = ph.two("part", [P, G, H, D]), ph.two("x3", [P, G, D])
        stats, mv, sd, rs = ph.two("stats", [P, G, 6]), ph.two("mv", [P, G, 2]), ph.two("sd", [P, G]), ph.two("rs", [P, G])
        end_idx, inner = ph.two("end_idx", [P, G], I32), ph.two("inner", [P, G], U32)
        loaded, scattered, x3_stored = ph.sem2("loaded"), ph.sem2("scattered"), ph.sem2("x3_stored")
        names = ("inv_done", "part_done", "sum_done", "stat_done", "aggr_done", "sd_done", "rs_done", "rows_done", "end_ready", "meta_ready")
        (inv_done, part_done, sum_done, stat_done, aggr_done, sd_done, rs_done, rows_done, end_ready, meta_ready) = (ph.sem(n) for n in names)
        spread, cleared = ph.sem("spread"), ph.sem("cleared")

        def last(eng, i):
            return eng.snap(T - 2 * G - (2 * G) * i)

        def step(base, g):
            return base + G * (1 - g)

        with nc.Block() as block:
            @block.sync
            def _(sp):
                start_counts(sp, dmas=loaded, n=2)
                with sp.Fori(0, iters) as i:
                    base = last(sp, i)
                    for g in range(2):
                        t, freed = now(sp, step(base, g)), now(sp, at2(i, g, back=2))
                        sp.wait_ge(sum_done, freed)
                        sp.dma_start(st[g][:], s.state2[:, bass.ds(t, G), :]).then_inc(loaded[g], 16)
                        sp.dma_start(own[g][:], s.own2[:, bass.ds(t, G), :]).then_inc(loaded[g], 16)

            @block.gpsimd
            def _(pool):
                first_dma(pool, s, ph, scattered)
                limit = pool.to_reg(s.N - 1)
                start_counts(pool, [end_ready])
                with pool.Fori(0, iters) as i:
                    base = last(pool, i)
                    for g in range(2):
                        t, freed, group, ready = (now(pool, v) for v in (step(base, g), scattered_at(i, G, back=1), at2(i, g), at8(i, g * G + G - 1)))
                        pool.wait_ge(scattered[g], freed)
                        pool.tensor_copy(end_idx[g][:], s.end_idx[:, bass.ds(t, G)]).then_inc(end_ready, 1)
                        pool.wait_ge(end_ready, 3)
                        pool.wait_ge(end_ready, group)
                        pool.wait_ge(spread, ready)
                        for k in reversed(range(G)):
                            pool.indirect_dma_start(s.x3, bass.IndirectOffsetOnAxis(ap=end_idx[g][:, k:k + 1], axis=0), x3[g][:, k, :], None,
                                                    bounds_check=limit, oob_is_err=False).then_inc(scattered[g], 16)
                for g in range(2):
                    pool.wait_ge(scattered[g], scattered_at(iters - 1, G))

            @block.tensor
            def _(pe):
                start_counts(pe, [sum_done])
                with pe.Fori(0, iters) as i:
                    for g in range(2):
                        pe.wait_ge(loaded[g], landed(i, 2))
                        pe.wait_ge(part_done, at2(i, g))
                        pe.wait_ge(rows_done, at2(i, g, back=2))
                        pe.matmul(bank[g][:], s.ident[:], own[g][:], start=True, stop=False)
                        pe.matmul(bank[g][:], s.ident[:], s.bt_all[:].rearrange("p (a d) -> p a d", a=1).to_broadcast([P, G, D]), start=False, stop=False)
                        for h in range(H):
                            ins = pe.matmul(bank[g][:], s.ident[:], part[g][:, :, h, :], start=False, stop=(h == H - 1))
                        ins.then_inc(sum_done, 1)

            @block.scalar
            def _(act):
                start_counts(act, dmas=x3_stored)
                start_counts(act, [sd_done])
                with act.Fori(0, iters) as i:
                    base = last(act, i)
                    for g in range(2):
                        act.wait_ge(aggr_done, at2(i, g))
                        act.wait_ge(rs_done, at2(i, g, back=2))
                        act.activation(sd[g][:], mv[g][:, :, 1], ACT.Sqrt, bias=s.eps[:]).then_inc(sd_done, 1)
                        t = act.snap(step(base, g))
                        act.wait_ge(spread, at8(i, g * G + G - 1))
                        act.dma_start(s.dst3[:, bass.ds(t, G), :], x3[g][:]).then_inc(x3_stored[g], 16)
                for g in range(2):
                    act.wait_ge(x3_stored[g], landed(iters - 1))

            @block.vector
            def _(dve):
                start_counts(dve, [meta_ready, inv_done, part_done, stat_done, aggr_done, rs_done, rows_done], [spread])
                dve.memset(x3[1][:], 0.0).then_inc(cleared, 1)
                dve.wait_ge(cleared, 1)
                with dve.Fori(0, iters) as i:
                    base = last(dve, i)
                    for g in range(2):
                        dve.tensor_copy(inner[g][:], s.inner[:, bass.ds(step(base, g), G)]).then_inc(meta_ready, 1)
                        dve.wait_ge(loaded[g], landed(i, 2))
                        sums = st[g][:, :, 0:H * hw].rearrange("p k (h w) -> p k h w", h=H)
                        dve.reciprocal(inv[g][:], sums[:, :, :, D]).then_inc(inv_done, 1)
                        dve.wait_ge(inv_done, at2(i, g))
                        dve.wait_ge(sum_done, at2(i, g, back=2))
                        for k in range(G):
                            ins = dve.tensor_tensor(part[g][:, k], sums[:, k, :, 0:D], inv[g][:, k, :].rearrange("p (h a) -> p h a", a=1).to_broadcast([P, H, D]), ALU.mult)
                        ins.then_inc(part_done, 1)
                        dve.wait_ge(sum_done, at2(i, g))
                        dve.wait_ge(sd_done, at2(i, g, back=2))
                        rowstats(dve, rows4(bank[g]), stats[g], mv[g], stat_done, aggr_done, i, g)
                        dve.wait_ge(scattered[g], scattered_at(i, G, back=1))
                        dve.wait_ge(x3_stored[g], landed(i, back=1))
                        norm_rows(dve, sd_done, rows4(bank[g]), x3[g], mv[g], sd[g], rs[g], rs_done, rows_done, i, g)
                        dve.wait_ge(rows_done, at2(i, g))
                        dve.wait_ge(meta_ready, at2(i, g))
                        for k in reversed(range(G)):
                            later = x3[g][:, k + 1, :] if k < G - 1 else x3[1 - g][:, 0, :]
                            n = g * G + G - 1 - k
                            before = now(dve, at8(i, n, back=1))
                            dve.wait_ge(cleared, 1)
                            dve.wait_ge(spread, before)
                            dve.copy_predicated(x3[g][:, k, :], inner[g][:, k:k + 1].to_broadcast([P, D]), later).then_inc(spread, 1)


def forward3_phase(nc, s, a):
    T, iters = s.T, s.T // (2 * G)
    with Phase(nc, "fwd3") as ph:
        bank = ph.banks()
        xs, xd, xsT, xdT, old = (ph.two(n, [P, G, D]) for n in ("xs", "xd", "xsT", "xdT", "old"))
        idx, same8, st = ph.sb("idx", [P, 4 * G], I32), ph.sb("same8", [P, 2 * G]), ph.two("st", [P, G, W3])
        idx_ready, gathered, own_loaded, st_stored = ph.sem("idx_ready"), ph.sem2("gathered"), ph.sem2("own_loaded"), ph.sem2("st_stored")
        transposed, xT_copied, rows_done, same_ready, decayed, acc_done, cnt_done, cleared = (
            ph.sem(n) for n in ("transposed", "xT_copied", "rows_done", "same_ready", "decayed", "acc_done", "cnt_done", "cleared"))
        with nc.Block() as block:
            @block.gpsimd
            def _(pool):
                limit = pool.to_reg(s.N - 1)
                with pool.Fori(0, iters) as i:
                    for g in range(2):
                        if g == 0:
                            column, read = now(pool, i * (4 * G)), now(pool, at2(i, 1, back=2))
                            pool.wait_ge(transposed, read)
                            pool.tensor_copy(idx[:], s.gather_idx[:, bass.ds(column, 4 * G)]).then_inc(idx_ready, 1)
                            pool.wait_ge(idx_ready, i + 1)
                        freed = now(pool, at2(i, g, back=2))
                        pool.wait_ge(idx_ready, 1)
                        pool.wait_ge(transposed, freed)
                        for k in range(G):
                            kk = g * G + k
                            pool.indirect_dma_start(xs[g][:, k, :], None, s.x3, bass.IndirectOffsetOnAxis(ap=idx[:, kk:kk + 1], axis=0),
                                                    bounds_check=limit, oob_is_err=False).then_inc(gathered[g], 16)

            @block.sync
            def _(sp):
                start_counts(sp, dmas=own_loaded)
                with sp.Fori(0, iters) as i:
                    for g in range(2):
                        t = sp.snap(i * (2 * G) + g * G)
                        sp.wait_ge(transposed, at2(i, g, back=2))
                        sp.dma_start(xd[g][:], s.dst3[:, bass.ds(t, G), :]).then_inc(own_loaded[g], 16)

            @block.tensor
            def _(pe):
                start_counts(pe, [transposed, rows_done])
                with pe.Fori(0, iters) as i:
                    for g in range(2):
                        pe.wait_ge(gathered[g], 16 * G * i + 16 * G)
                        pe.wait_ge(own_loaded[g], landed(i))
                        pe.wait_ge(xT_copied, at2(i, g, back=2))
                        for k in range(G):
                            pe.transpose(bank[g][:, k * D:(k + 1) * D], xs[g][:, k, :], s.ident[:])
                        for k in range(G):
                            ins = pe.transpose(bank[2 + g][:, k * D:(k + 1) * D], xd[g][:, k, :], s.ident[:])
                        ins.then_inc(transposed, 1)
                        pe.wait_ge(xT_copied, at2(i, g))
                        pe.wait_ge(acc_done, at8(i, g * G + 3, back=8))
                        for k in range(G):
                            pe.matmul(bank[4 + g][:, k * D:(k + 1) * D], xsT[g][:, k, :], s.WeT[:, 0, :], start=True, stop=False)
                            ins = pe.matmul(bank[4 + g][:, k * D:(k + 1) * D], xdT[g][:, k, :], s.WeT[:, 1, :], start=False, stop=True)
                        ins.then_inc(rows_done, 1)

            @block.scalar
            def _(act):
                start_counts(act, dmas=st_stored)
                start_counts(act, [xT_copied])
                with act.Fori(0, iters) as i:
                    for g in range(2):
                        act.wait_ge(transposed, at2(i, g))
                        act.wait_ge(rows_done, at2(i, g, back=2))
                        act.activation(xsT[g][:], rows4(bank[g]), ACT.Copy)
                        act.activation(xdT[g][:], rows4(bank[2 + g]), ACT.Copy).then_inc(xT_copied, 1)
                        t = act.snap(i * (2 * G) + g * G)
                        act.wait_ge(acc_done, at8(i, g * G + 3))
                        act.wait_ge(cnt_done, at8(i, g * G + 3))
                        act.dma_start(s.state3[:, bass.ds(t, G), :], st[g][:]).then_inc(st_stored[g], 16)
                for g in range(2):
                    act.wait_ge(st_stored[g], landed(iters - 1))

            @block.vector
            def _(dve):
                start_counts(dve, [], [decayed, acc_done, cnt_done])
                dve.memset(st[1][:], 0.0).then_inc(cleared, 1)
                dve.wait_ge(cleared, 1)
                with dve.Fori(0, iters) as i:
                    dve.wait_ge(acc_done, at8(i, 0, back=1))
                    dve.wait_ge(cnt_done, at8(i, 0, back=1))
                    dve.tensor_copy(same8[:], s.same[:, bass.ds(i * (2 * G), 2 * G)]).then_inc(same_ready, 1)
                    dve.wait_ge(same_ready, i + 1)
                    for g in range(2):
                        dve.wait_ge(rows_done, at2(i, g))
                        dve.wait_ge(st_stored[g], landed(i, back=1))
                        for k in range(G):
                            kk = g * G + k
                            prev = st[g][:, k - 1, :] if k else st[1 - g][:, G - 1, :]
                            dve.wait_ge(acc_done, at8(i, kk, back=1))
                            dve.wait_ge(cnt_done, at8(i, kk, back=1))
                            dve.tensor_scalar(old[g][:, k, :], prev[:, 0:D], same8[:, kk:kk + 1], None, ALU.mult).then_inc(decayed, 1)
                            dve.tensor_scalar(st[g][:, k, D:W3], prev[:, D:W3], same8[:, kk:kk + 1], 1.0, ALU.mult, ALU.add).then_inc(cnt_done, 1)
                            dve.wait_ge(decayed, at8(i, kk))
                            dve.scalar_tensor_tensor(st[g][:, k, 0:D], bank[4 + g][:, k * D:(k + 1) * D], 0.0, old[g][:, k, :], ALU.max, ALU.add).then_inc(acc_done, 1)


def backward3_phase(nc, s, a):
    T, iters = s.T, s.T // (2 * G)
    with Phase(nc, "bwd3") as ph:
        bank = ph.banks()
        st, own, inv = ph.two("st", [P, G, W3]), ph.two("own", [P, G, D]), ph.two("inv", [P, G])
        mean, meanT, Y, out = (ph.two(n, [P, G, D]) for n in ("mean", "meanT", "Y", "out"))
        stats, mv, sd, rs = ph.two("stats", [P, G, 6]), ph.two("mv", [P, G, 2]), ph.two("sd", [P, G]), ph.two("rs", [P, G])
        end_idx = ph.two("end_idx", [P, G], I32)
        loaded, scattered = ph.sem2("loaded"), ph.sem2("scattered")
        names = ("inv_done", "mean_done", "meanT_done", "meanT_copied", "node_done", "Y_done", "stat_done", "aggr_done", "sd_done", "rs_done", "out_done", "end_ready")
        (inv_done, mean_done, meanT_done, meanT_copied, node_done, Y_done, stat_done, aggr_done, sd_done, rs_done, out_done,
         end_ready) = (ph.sem(n) for n in names)
        with nc.Block() as block:
            @block.sync
            def _(sp):
                start_counts(sp, dmas=loaded, n=2)
                with sp.Fori(0, iters) as i:
                    for g in range(2):
                        t = sp.snap(i * (2 * G) + g * G)
                        sp.wait_ge(mean_done, at2(i, g, back=2))
                        sp.wait_ge(Y_done, at2(i, g, back=2))
                        sp.dma_start(st[g][:], s.state3[:, bass.ds(t, G), :]).then_inc(loaded[g], 16)
                        sp.dma_start(own[g][:], s.dst3[:, bass.ds(t, G), :]).then_inc(loaded[g], 16)

            @block.gpsimd
            def _(pool):
                first_dma(pool, s, ph, scattered)
                limit = pool.to_reg(s.N - 1)
                start_counts(pool, [end_ready])
                with pool.Fori(0, iters) as i:
                    for g in range(2):
                        t, freed, group = (now(pool, v) for v in (i * (2 * G) + g * G, scattered_at(i, G, back=1), at2(i, g)))
                        pool.wait_ge(scattered[g], freed)
                        pool.tensor_copy(end_idx[g][:], s.end_idx[:, bass.ds(t, G)]).then_inc(end_ready, 1)
                        pool.wait_ge(end_ready, 3)
                        pool.wait_ge(end_ready, group)
                        pool.wait_ge(out_done, group)
                        for k in range(G):
                            pool.indirect_dma_start(s.out, bass.IndirectOffsetOnAxis(ap=end_idx[g][:, k:k + 1], axis=0), out[g][:, k, :], None,
                                                    bounds_check=limit, oob_is_err=False).then_inc(scattered[g], 16)
                for g in range(2):
                    pool.wait_ge(scattered[g], scattered_at(iters - 1, G))

            @block.tensor
            def _(pe):
                start_counts(pe, [meanT_done, node_done])
                with pe.Fori(0, iters) as i:
                    for g in range(2):
                        pe.wait_ge(mean_done, at2(i, g))
                        pe.wait_ge(meanT_copied, at2(i, g, back=2))
                        for k in range(G):
                            ins = pe.transpose(bank[g][:, k * D:(k + 1) * D], mean[g][:, k, :], s.ident[:])
                        ins.then_inc(meanT_done, 1)
                        pe.wait_ge(meanT_copied, at2(i, g))
                        pe.wait_ge(Y_done, at2(i, g, back=2))
                        for k in range(G):
                            pe.matmul(bank[2 + g][:, k * D:(k + 1) * D], meanT[g][:, k, :], s.WnT[:], start=True, stop=False)
                            ins = pe.matmul(bank[2 + g][:, k * D:(k + 1) * D], s.ones_row[:], s.bn_row[:], start=False, stop=True)
                        ins.then_inc(node_done, 1)

            @block.scalar
            def _(act):
                start_counts(act, [mean_done, meanT_copied, sd_done])
                with act.Fori(0, iters) as i:
                    for g in range(2):
                        act.wait_ge(inv_done, at2(i, g))
                        act.wait_ge(meanT_done, at2(i, g, back=2))
                        for k in range(G):
                            ins = act.activation(mean[g][:, k, :], st[g][:, k, 0:D], ACT.Copy, scale=inv[g][:, k:k + 1])
                        ins.then_inc(mean_done, 1)
                        act.wait_ge(meanT_done, at2(i, g))
                        act.wait_ge(node_done, at2(i, g, back=2))
                        act.activation(meanT[g][:], rows4(bank[g]), ACT.Copy).then_inc(meanT_copied, 1)
                        act.wait_ge(aggr_done, at2(i, g))
                        act.wait_ge(rs_done, at2(i, g, back=2))
                        act.activation(sd[g][:], mv[g][:, :, 1], ACT.Sqrt, bias=s.eps[:]).then_inc(sd_done, 1)

            @block.vector
            def _(dve):
                start_counts(dve, [inv_done, Y_done, stat_done, aggr_done, rs_done, out_done])
                with dve.Fori(0, iters) as i:
                    for g in range(2):
                        dve.wait_ge(loaded[g], landed(i, 2))
                        dve.wait_ge(mean_done, at2(i, g, back=2))
                        dve.reciprocal(inv[g][:], st[g][:, :, D]).then_inc(inv_done, 1)
                    for g in range(2):
                        dve.wait_ge(node_done, at2(i, g))
                        dve.scalar_tensor_tensor(Y[g][:], rows4(bank[2 + g]), 0.0, own[g][:], ALU.max, ALU.add).then_inc(Y_done, 1)
                        dve.wait_ge(Y_done, at2(i, g))
                        dve.wait_ge(sd_done, at2(i, g, back=2))
                        rowstats(dve, Y[g], stats[g], mv[g], stat_done, aggr_done, i, g)
                        dve.wait_ge(scattered[g], scattered_at(i, G, back=1))
                        norm_rows(dve, sd_done, Y[g], out[g], mv[g], sd[g], rs[g], rs_done, out_done, i, g)


def build(nc, a, out):
    N, T = a["x"].shape[0], a["src2"].shape[1]
    s = Kept()
    s.N, s.T, s.block = N, T, P * G
    s.blocks = -(-N // s.block)
    assert s.blocks % 2 == 0 and T % (2 * G) == 0
    s.zrows = 64 if N > 64 * P else 4
    s.zchunks = (N + P) // (P * s.zrows)
    rest = N + P - s.zchunks * P * s.zrows
    s.zrest = next((r for r in range(s.zrows, 0, -1) if rest % r == 0 and rest // r <= P), 1)

    def table(name, shape):
        return nc.dram_tensor(name, shape, F32, kind="Internal").ap()

    s.x1, s.x2, s.x3 = (table(f"x{j}", (N, D)) for j in (1, 2, 3))
    s.agg1 = table("agg1", (N + P, D))
    s.state0, s.state2, s.state3 = table("state0", (P, T, W0)), table("state2", (P, T, W2)), table("state3", (P, T, W3))
    s.root0, s.own2, s.dst3 = table("root0", (P, T, D)), table("own2", (P, T, D)), table("dst3", (P, T, D))
    s.out = out
    with ExitStack() as c:
        def sb(names, shape, dt=F32):
            return [c.enter_context(nc.sbuf_tensor(n, shape, dt)) for n in names.split()]

        s.ident, s.lower, s.Wq, s.Wk, s.Wv, s.WrI, s.W2, s.Wl, s.WnT = sb("ident lower Wq Wk Wv WrI W2 Wl WnT", [P, D])
        s.br_all, s.bt_all, s.bn_all, s.rbn_all = sb("br_all bt_all bn_all rbn_all", [P, D])
        s.tail_tail, s.tail_head, s.head_tail, s.head_head = sb("tail_tail tail_head head_tail head_head", [P, P])
        s.far_tt, s.far_th, s.far_ht, s.far_hh = sb("far_tt far_th far_ht far_hh", [P, P])
        s.brv_row, s.b2_row, s.bl_row, s.bn_row, s.ones_row = sb("brv_row b2_row bl_row bn_row ones_row", [1, D])
        s.bq, s.bk, s.b1, s.eps, s.trash = sb("bq bk b1 eps trash", [P, 1])
        [s.W1], [s.WeT], [s.Wz] = sb("W1", [RBF, D]), sb("WeT", [P, 2, D]), sb("Wz", [P, H, D])
        s.headsel, s.att_s, s.att_d = sb("headsel att_s att_d", [P, H])
        s.src_f, s.dst_f, s.same, s.cut, s.to_trash = sb("src_f dst_f same cut to_trash", [P, T])
        [s.inner], [s.end_idx], [s.gather_idx] = sb("inner", [P, T], U32), sb("end_idx", [P, T], I32), sb("gather_idx", [P, 2 * T], I32)
        [s.head_row], [s.zeros] = sb("head_row", [P, 1], I32), sb("zeros", [P, s.zrows * D])
        setup_phase(nc, s, a)
        dense0_phase(nc, s, a)
        forward_attention_phase(nc, s, a, 0)
        patch_phase(nc, s, s.state0, W0, C + 1)
        backward0_phase(nc, s, a)
        dense1_phase(nc, s, a)
        forward_attention_phase(nc, s, a, 2)
        patch_phase(nc, s, s.state2, W2, D + 1)
        backward2_phase(nc, s, a)
        forward3_phase(nc, s, a)
        patch_phase(nc, s, s.state3, W3, 0)
        backward3_phase(nc, s, a)


def laid_out(inputs):
    g = {k: np.asarray(v) for k, v in inputs.items()}
    N, E = g["x"].shape[0], g["src"].shape[0]
    T = steps_of(E)
    pad = P * T - E

    def per_partition(v, fill):
        return np.concatenate([v, np.full(P * T - v.shape[0], fill, v.dtype)]).reshape(P, T)

    flip = np.ascontiguousarray
    out = {
        "x": g["x"],
        "src2": per_partition(g["src"], N + P - 1), "dst2": per_partition(g["dst"], N), "next_dst2": per_partition(g["dst"][1:], N + 1),
        "edge2": np.concatenate([g["edge_attr_64"], np.zeros((pad, RBF), g["edge_attr_64"].dtype)]).reshape(P, T, RBF),
        "Wq": g["L0_gnn_Wq"], "Wk": g["L0_gnn_Wk"], "Wv": g["L0_gnn_Wv"], "Wr": g["L0_gnn_Wr"],
        "bq": g["L0_gnn_bq"], "bk": g["L0_gnn_bk"], "bv": g["L0_gnn_bv"], "br": g["L0_gnn_br"],
        "W1": g["L1_gnn_W1"], "b1": g["L1_gnn_b1"], "W2": g["L1_gnn_W2"], "b2": g["L1_gnn_b2"], "Wl": g["L1_gnn_Wl"], "bl": g["L1_gnn_bl"],
        "WfcT": flip(g["L2_gnn_W_fc"].T), "Wtr": g["L2_gnn_W_trans"], "bt": g["L2_gnn_b_trans"],
        "att2": flip(np.stack([g["L2_gnn_att_ns"][0].T, g["L2_gnn_att_nd"][0].T], axis=2)),
        "WeT": flip(g["L3_gnn_W_edge"].T), "WnT": flip(g["L3_gnn_W_node"].T), "bn": g["L3_gnn_b_node"],
        "c_ident": np.eye(P, dtype=np.float32), "c_lower": np.tri(P, k=-1, dtype=np.float32),
        "c_headsel": flip(np.repeat(np.eye(H, dtype=np.float32), C, axis=0) / np.float32(np.sqrt(C))),
        "c_trash": np.arange(N, N + P, dtype=np.float32).reshape(P, 1),
    }
    return out


def kernel(**inputs):
    import concourse.bacc as bacc
    from concourse.bass_utils import run_bass_kernel_spmd

    arrays = laid_out(inputs)
    nc = bacc.Bacc("TRN2", target_bir_lowering=False, num_devices=1)
    a = {name: nc.dram_tensor(f"in_{name}", v.shape, mybir.dt.from_np(v.dtype), kind="ExternalInput").ap() for name, v in arrays.items()}
    out = nc.dram_tensor("out", inputs["x"].shape, F32, kind="ExternalOutput").ap()
    build(nc, a, out)
    r = run_bass_kernel_spmd(nc, [{f"in_{name}": v for name, v in arrays.items()}], core_ids=[0])
    return r.results[0]["out"]
```

```python
from contextlib import ExitStack

import numpy as np
import concourse.bass as bass
import concourse.mybir as mybir

P = 128
D = 128
H = 4
C = D // H
RBF = 64
G = 4
R = 8
W0 = H * (C + 1) + H
W2 = H * (D + 1) + H
W3 = D + 1
FAR = 1.0e30
SKIP = float(1 << 22)
EPS = 1e-5

F32 = mybir.dt.float32
BF16 = mybir.dt.bfloat16
I32 = mybir.dt.int32
U32 = mybir.dt.uint32
ALU = mybir.AluOpType
ACT = mybir.ActivationFunctionType
X = mybir.AxisListType.X


def steps_of(edges):
    return -(-edges // (P * 2 * G)) * 2 * G


def at2(i, g, back=0):
    return 2 * i + (g + 3 - back)


def at8(i, k, back=0):
    return 8 * i + (k + 9 - back)


def landed(i, n=1, back=0):
    return (16 * n) * i + (16 * n) * (2 - back)


def start_counts(eng, groups=(), steps=(), dmas=(), n=1):
    for s in groups:
        eng.sem_inc(s, 2)
    for s in steps:
        eng.sem_inc(s, 8)
    for s in dmas:
        eng.sem_inc(s, 16 * n)


def scattered_at(i, n, back=0):
    return (16 * n) * i + (16 * n * (1 - back) + 16)


def first_dma(pool, s, ph, sems):
    for n, sem in enumerate(sems):
        pool.dma_start(ph.sb(f"first{n}", [P, 1])[:], s.eps[:]).then_inc(sem, 16)


def in_rounds(eng, iters, *stages, apart=0):
    lead, lag = max(o for _, o in stages), max(-o for _, o in stages)
    first, last = (lag + 1) // 2, iters - (lead + apart + 1) // 2
    last = max(first, last)

    def one(i, r):
        for stage, o in stages:
            g = (r + o) % 2
            di = (r + o - g) // 2
            if not isinstance(i, int) or 0 <= i + di < iters:
                stage(i + di if di else i, g)

    for n in range(-lead, 2 * first):
        one(n // 2, n % 2)
    if first < last:
        with eng.Fori(first, last) as i:
            one(i, 0)
            one(i, 1)
    for n in range(2 * last, 2 * iters + lag):
        one(n // 2, n % 2)


def now(eng, value):
    return value if isinstance(value, int) else eng.snap(eng.to_reg(value))


class Kept:
    pass


class Phase:

    def __init__(self, nc, name):
        self.nc, self.name, self.ctx, self.sems = nc, name, ExitStack(), []

    def __enter__(self):
        return self

    def __exit__(self, *a):
        self.nc.clear_and_free_semaphores(self.sems)
        self.nc.all_engine_barrier()
        self.ctx.close()

    def sb(self, name, shape, dt=F32):
        return self.ctx.enter_context(self.nc.sbuf_tensor(f"{self.name}_{name}", shape, dt))

    def two(self, name, shape, dt=F32):
        return [self.sb(f"{name}{g}", shape, dt) for g in range(2)]

    def banks(self):
        return [self.ctx.enter_context(self.nc.psum_tensor(f"{self.name}_bank{j}", [P, G * D], F32)) for j in range(8)]

    def sem(self, name):
        self.sems.append(self.nc.alloc_semaphore(f"{self.name}_{name}"))
        return self.sems[-1]

    def sem2(self, name):
        return [self.sem(f"{name}{g}") for g in range(2)]


def rows4(bank):
    return bank[:].rearrange("p (k d) -> p k d", k=G)


def setup_phase(nc, s, a):
    T, N = s.T, s.N
    with Phase(nc, "setup") as ph:
        loaded, made, mult, moved, calc = (ph.sem(n) for n in ("loaded", "made", "multiplied", "moved", "calc"))
        src_i, dst_i, nxt_i = (ph.sb(n, [P, T], I32) for n in ("src_i", "dst_i", "nxt_i"))
        nxt_f, t0 = ph.sb("nxt_f", [P, T]), ph.sb("t0", [P, T])
        wfcT = ph.sb("wfcT", [P, H, D])
        wtr = ph.sb("wtr", [P, H, D + 2])
        bias3, left, chosen = (ph.sb(n, [3, 5, D]) for n in ("bias3", "left", "chosen"))
        part16 = ph.sb("part16", [3, 5, D], BF16)
        cnt = ph.sb("cnt", [P, 1])
        bank = ph.banks()
        flagged = []
        loads = [
            (src_i[:], a["src2"]), (dst_i[:], a["dst2"]), (nxt_i[:], a["next_dst2"]),
            (s.ident[:], a["c_ident"]), (s.lower[:], a["c_lower"]), (s.headsel[:], a["c_headsel"]), (s.trash[:], a["c_trash"]),
            (s.Wq[:], a["Wq"]), (s.Wk[:], a["Wk"]), (s.Wv[:], a["Wv"]), (s.WrI[:], a["Wr"]),
            (s.W1[:], a["W1"]), (s.W2[:], a["W2"]), (s.Wl[:], a["Wl"]),
            (s.WeT[:], a["WeT"].rearrange("(h p) d -> p h d", p=P)), (s.WnT[:], a["WnT"]),
            (wfcT[:], a["WfcT"].rearrange("(h p) d -> p h d", p=P)),
            (wtr[:, :, 0:D], a["Wtr"].rearrange("(h p) d -> p h d", p=P)),
            (wtr[:, :, D:D + 2], a["att2"]),
            (s.bq[:], a["bq"].rearrange("(p a) -> p a", a=1)), (s.bk[:], a["bk"].rearrange("(p a) -> p a", a=1)),
            (s.b1[:], a["b1"].rearrange("(p a) -> p a", a=1)),
            *((bias3[:, j, :], a[n].rearrange("(a n) -> a n", a=1).to_broadcast([3, D])) for j, n in enumerate(("br", "b2", "bl", "bn", "bv"))),
            (s.br_all[:], a["br"].rearrange("(a n) -> a n", a=1).to_broadcast([P, D])),
            (s.bt_all[:], a["bt"].rearrange("(a n) -> a n", a=1).to_broadcast([P, D])),
            (s.bn_all[:], a["bn"].rearrange("(a n) -> a n", a=1).to_broadcast([P, D])),
        ]
        with nc.Block() as block:
            @block.sync
            def _(sp):
                for out, in_ in loads:
                    sp.dma_start(out, in_, allow_slow_non_contiguous=True).then_inc(loaded, 16)

            @block.gpsimd
            def _(pool):
                pool.memset(s.ones3[:], 1.0).then_inc(made, 1)
                pool.memset(s.eps[:], EPS).then_inc(made, 1)
                pool.memset(s.zeros[:], 0.0).then_inc(made, 1)

            @block.vector
            def _(dve):
                n = [0]

                def done(ins):
                    n[0] += 1
                    ins.then_inc(calc, 1)
                    dve.wait_ge(calc, n[0])

                dve.wait_ge(loaded, 16 * len(loads))
                done(dve.tensor_tensor(s.WrI[:], s.WrI[:], s.ident[:], ALU.add))
                done(dve.tensor_tensor(bias3[:, 0, :], bias3[:, 0, :], bias3[:, 4, :], ALU.add))
                done(dve.tensor_copy(left[:], bias3[:]))
                done(dve.memset(chosen[:], 0.0))
                for part in range(3):
                    done(dve.tensor_copy(part16[:], left[:]))
                    done(dve.scalar_tensor_tensor(chosen[:], part16[:], s.ident[0:3, part:part + 1], chosen[:], ALU.mult, ALU.add))
                    done(dve.tensor_tensor(left[:], left[:], part16[:], ALU.subtract))
                for j, parts in enumerate((s.brv_parts, s.b2_parts, s.bl_parts, s.bn_parts)):
                    done(dve.tensor_copy(parts[:], chosen[:, j, :]))
                done(dve.tensor_scalar(s.rbn_all[:], s.bn_all[:], 0.0, None, ALU.max))
                done(dve.tensor_copy(s.src_f[:], src_i[:]))
                done(dve.tensor_copy(s.dst_f[:], dst_i[:]))
                flagged.append(n[0])
                done(dve.tensor_copy(nxt_f[:], nxt_i[:]))
                done(dve.memset(s.same[:], 0.0))
                done(dve.tensor_tensor(s.same[:, 1:T], s.dst_f[:, 1:T], s.dst_f[:, 0:T - 1], ALU.is_equal))
                done(dve.tensor_scalar(s.cut[:], s.same[:], -1.0, FAR, ALU.add, ALU.mult))
                done(dve.tensor_tensor(t0[:], nxt_f[:], s.dst_f[:], ALU.is_equal))
                done(dve.tensor_copy(s.inner[:], t0[:]))
                done(dve.memset(s.inner[:, T - 1:T], 0))
                done(dve.scalar_tensor_tensor(t0[:], t0[:], SKIP, s.dst_f[:], ALU.mult, ALU.add))
                done(dve.tensor_copy(s.end_idx[:], t0[:]))
                ga = s.gather_idx[:].rearrange("p (n two k) -> p n two k", two=2, k=G)
                done(dve.tensor_scalar(t0[:], s.src_f[:], float(N - 1), None, ALU.min))
                done(dve.tensor_copy(ga[:, :, 0, :], t0[:].rearrange("p (n k) -> p n k", k=G)))
                done(dve.tensor_scalar(t0[:], s.dst_f[:], float(N - 1), None, ALU.min))
                done(dve.tensor_copy(ga[:, :, 1, :], t0[:].rearrange("p (n k) -> p n k", k=G)))
                done(dve.tensor_scalar(s.to_trash[:], s.src_f[:], s.trash[:], -1.0, ALU.subtract, ALU.mult))
                done(dve.tensor_scalar(s.to_trash[:, 1::2], s.to_trash[:, 1::2], float(P), None, ALU.add))
                head, tail = s.dst_f[:, 0:1], s.dst_f[:, T - 1:T]
                done(dve.tensor_scalar(t0[:], s.dst_f[:], head, None, ALU.is_equal))
                done(dve.tensor_reduce(cnt[:], t0[:], X, ALU.add))
                done(dve.tensor_scalar(t0[:, 0:1], s.trash[:], -float(N), float(T), ALU.add, ALU.mult))
                done(dve.scalar_tensor_tensor(t0[:, 1:2], cnt[:], -1.0, t0[:, 0:1], ALU.add, ALU.add))
                done(dve.tensor_copy(s.head_row[:], t0[:, 1:2]))
                dve.wait_ge(mult, 1)
                rowT, rowH = bank[0][:, 0:P], bank[0][:, P:2 * P]
                done(dve.tensor_scalar(s.tail_tail[:], rowT, tail, None, ALU.is_equal))
                done(dve.tensor_scalar(s.tail_head[:], rowH, tail, None, ALU.is_equal))
                done(dve.tensor_scalar(s.head_tail[:], rowT, head, None, ALU.is_equal))
                done(dve.tensor_scalar(s.head_head[:], rowH, head, None, ALU.is_equal))
                for far, m in ((s.far_tt, s.tail_tail), (s.far_th, s.tail_head), (s.far_ht, s.head_tail), (s.far_hh, s.head_head)):
                    done(dve.tensor_scalar(far[:], m[:], -1.0, FAR, ALU.add, ALU.mult))
                done(dve.tensor_tensor(t0[:, 0:1], head, tail, ALU.not_equal))
                done(dve.tensor_scalar(s.head_tail[:], s.head_tail[:], t0[:, 0:1], None, ALU.mult))
                done(dve.tensor_scalar(s.head_head[:], s.head_head[:], t0[:, 0:1], None, ALU.mult))
                for h in range(H):
                    dve.wait_ge(mult, 2 + h)
                    done(dve.tensor_copy(s.Wz[:, h, :], bank[1 + h][:, 0:D]))
                    done(dve.tensor_copy(s.att_s[:, h:h + 1], bank[1 + h][:, D:D + 1]))
                    done(dve.tensor_copy(s.att_d[:, h:h + 1], bank[1 + h][:, D + 1:D + 2]))
                dve.wait_ge(made, 3)

            @block.tensor
            def _(pe):
                pe.wait_ge(loaded, 16 * len(loads))
                pe.wait_ge(calc, flagged[0])
                pe.transpose(bank[0][:, 0:P], s.dst_f[:, T - 1:T].to_broadcast([P, P]), s.ident[:])
                pe.transpose(bank[0][:, P:2 * P], s.dst_f[:, 0:1].to_broadcast([P, P]), s.ident[:]).then_inc(mult, 1)
                for h in range(H):
                    pe.matmul(bank[1 + h][:, 0:D + 2], wfcT[:, h, :], wtr[:, h, :], start=True, stop=True).then_inc(mult, 1)


def rowstats(dve, Y, stats, mv, stat_done, aggr_done, i, g):
    for k in range(Y.shape[1]):
        ins = dve.bn_stats(stats[:, k, :], Y[:, k, :])
    ins.then_inc(stat_done, 1)
    four = now(dve, at2(i, g))
    dve.wait_ge(stat_done, 2)
    dve.wait_ge(stat_done, four)
    for k in range(Y.shape[1]):
        ins = dve.bn_aggr(mv[:, k, :], stats[:, k, :])
    ins.then_inc(aggr_done, 1)


def dense_row(s, i, g):
    if isinstance(i, int) and (i, g) == (s.blocks // 2 - 1, 1):
        return s.N - s.block
    return (2 * s.block) * i + s.block * g


def of_block(table, row, s):
    return table[bass.ds(row, s.block), :].rearrange("(p k) d -> p k d", k=R)


def store_block(sp, s, table, rows, ready, stored, i, g):
    row, done = now(sp, dense_row(s, i, g)), now(sp, at2(i, g))
    sp.wait_ge(ready, done)
    if isinstance(i, int) and (i, g) == (s.blocks // 2 - 1, 1):
        sp.wait_ge(stored[0], landed(i))
    sp.dma_start(of_block(table, row, s), rows[g][:]).then_inc(stored[g], 16)


def scales(dve, mv, sd, rs, nb, sd_done, rs_done, nb_done, i, g):
    dve.wait_ge(sd_done, at2(i, g))
    dve.wait_ge(nb_done, at2(i, g, back=2))
    dve.reciprocal(rs[:], sd[:]).then_inc(rs_done, 1)
    dve.wait_ge(rs_done, at2(i, g))
    dve.scalar_tensor_tensor(nb[:], mv[:, :, 0], -1.0, rs[:], ALU.mult, ALU.mult).then_inc(nb_done, 1)


def scale_rows(act, Y, out, rs, nb, nb_done, out_done, i, g):
    act.wait_ge(nb_done, at2(i, g))
    for k in range(R):
        ins = act.activation(out[:, k, :], Y[:, k, :], ACT.Identity, scale=rs[:, k:k + 1], bias=nb[:, k:k + 1])
    ins.then_inc(out_done, 1)


def dense0_phase(nc, s, a):
    with Phase(nc, "dense0") as ph:
        xT_bank, Y_bank = ([ph.ctx.enter_context(nc.psum_tensor(f"dense0_{n}{g}", [P, R, D], F32)) for g in range(2)] for n in ("xT_bank", "Y_bank"))
        x_in, xT, Y, x1 = (ph.two(n, [P, R, D]) for n in ("x_in", "xT", "Y", "x1"))
        stats, mv = ph.two("stats", [P, R, 6]), ph.two("mv", [P, R, 2])
        sd, rs, nb = ph.two("sd", [P, R]), ph.two("rs", [P, R]), ph.two("nb", [P, R])
        x_loaded, x1_stored, zeroed = ph.sem2("x_loaded"), ph.sem2("x1_stored"), ph.sem("zeroed")
        transposed, xT_copied, product, Y_done, stat_done, aggr_done, sd_done, rs_done, nb_done, x1_done = (ph.sem(n) for n in (
            "transposed", "xT_copied", "product", "Y_done", "stat_done", "aggr_done", "sd_done", "rs_done", "nb_done", "x1_done"))
        iters = s.blocks // 2
        zero_rows = P * s.zrows
        with nc.Block() as block:
            @block.sync
            def _(sp):
                start_counts(sp, dmas=x_loaded + x1_stored)

                def load(i, g):
                    row, freed = now(sp, dense_row(s, i, g)), now(sp, at2(i, g, back=2))
                    sp.wait_ge(transposed, freed)
                    sp.dma_start(x_in[g][:], of_block(a["x"], row, s)).then_inc(x_loaded[g], 16)

                def store(i, g):
                    store_block(sp, s, s.x1, x1, x1_done, x1_stored, i, g)

                in_rounds(sp, iters, (load, 2), (store, -1), apart=1)
                for g in range(2):
                    sp.wait_ge(x1_stored[g], landed(iters - 1))

            @block.gpsimd
            def _(pool):
                agg = s.agg1
                for j in range(s.zchunks):
                    pool.dma_start(agg[bass.ds(j * zero_rows, zero_rows), :].rearrange("(p r) d -> p (r d)", p=P), s.zeros[:]).then_inc(zeroed, 16)
                rest = s.agg_rows - s.zchunks * zero_rows
                if rest:
                    pool.dma_start(agg[s.zchunks * zero_rows:s.agg_rows, :].rearrange("(p r) d -> p (r d)", p=rest // s.zrest), s.zeros[0:rest // s.zrest, 0:s.zrest * D]).then_inc(zeroed, 16)
                pool.wait_ge(zeroed, 16 * (s.zchunks + (1 if rest else 0)))

            @block.tensor
            def _(pe):
                start_counts(pe, [transposed, product])

                def turn(i, g):
                    pe.wait_ge(x_loaded[g], landed(i))
                    pe.wait_ge(xT_copied, at2(i, g, back=2))
                    for k in range(R):
                        ins = pe.transpose(xT_bank[g][:, k, :], x_in[g][:, k, :], s.ident[:])
                    ins.then_inc(transposed, 1)

                def multiply(i, g):
                    pe.wait_ge(xT_copied, at2(i, g))
                    pe.wait_ge(Y_done, at2(i, g, back=2))
                    for k in range(R):
                        ins = pe.matmul(Y_bank[g][:, k, :], xT[g][:, k, :], s.WrI[:], start=True, stop=True)
                    ins.then_inc(product, 1)

                in_rounds(pe, iters, (multiply, 0), (turn, 1))

            @block.scalar
            def _(act):
                start_counts(act, [xT_copied, sd_done, x1_done])

                def copy_turned(i, g):
                    act.wait_ge(transposed, at2(i, g))
                    act.wait_ge(product, at2(i, g, back=2))
                    act.activation(xT[g][:], xT_bank[g][:], ACT.Copy).then_inc(xT_copied, 1)

                def root_of_variance(i, g):
                    act.wait_ge(aggr_done, at2(i, g))
                    act.wait_ge(rs_done, at2(i, g, back=2))
                    act.activation(sd[g][:], mv[g][:, :, 1], ACT.Sqrt, bias=s.eps[:]).then_inc(sd_done, 1)

                def normalise(i, g):
                    act.wait_ge(x1_stored[g], landed(i, back=1))
                    scale_rows(act, Y[g], x1[g], rs[g], nb[g], nb_done, x1_done, i, g)

                act.activation(ph.sb("warm", [P, 1])[:], s.eps[:], ACT.Sqrt)
                in_rounds(act, iters, (normalise, -1), (copy_turned, 1), (root_of_variance, 0))

            @block.vector
            def _(dve):
                start_counts(dve, [Y_done, stat_done, aggr_done, rs_done, nb_done])

                def rows(i, g):
                    dve.wait_ge(product, at2(i, g))
                    dve.wait_ge(x1_done, at2(i, g, back=2))
                    dve.tensor_tensor(Y[g][:], Y_bank[g][:], s.br_all[:].rearrange("p (a d) -> p a d", a=1).to_broadcast([P, R, D]), ALU.add).then_inc(Y_done, 1)
                    dve.wait_ge(Y_done, at2(i, g))
                    dve.wait_ge(nb_done, at2(i, g, back=2))
                    rowstats(dve, Y[g], stats[g], mv[g], stat_done, aggr_done, i, g)

                def scale(i, g):
                    dve.wait_ge(x1_done, at2(i, g, back=2))
                    scales(dve, mv[g], sd[g], rs[g], nb[g], sd_done, rs_done, nb_done, i, g)

                in_rounds(dve, iters, (scale, -1), (rows, 0))


def forward_attention_phase(nc, s, a, layer):
    first = layer == 0
    T, iters = s.T, s.T // (2 * G)
    W, hw, table, rows_out, x_src = (W0, C + 1, s.state0, s.root0, a["x"]) if first else (W2, D + 1, s.state2, s.own2, s.x2)
    A = H * hw
    with Phase(nc, f"fwd{layer}") as ph:
        bank = ph.banks()
        value_bank = (bank[4], bank[7])
        xs, xd, xsT, xdT = (ph.two(n, [P, G, D]) for n in ("xs", "xd", "xsT", "xdT"))
        idx, cut4, warm = ph.two("idx", [P, 2 * G], I32), ph.two("cut4", [P, G]), ph.sb("warm", [P, 1])
        st = ph.two("st", [P, G, W])
        mh = ph.two("mh", [P, G + 1, H])
        diff = ph.two("diff", [P, G, 2, H])
        wt = ph.two("wt", [P, G, 2, A])
        dec = ph.two("dec", [P, A])
        if first:
            qT, prod, root = (ph.two(n, [P, G, D]) for n in ("qT", "prod", "root"))
        else:
            sc, leak = ph.two("sc", [P, G, H]), ph.two("leak", [P, G, H])
        idx_ready, gathered, st_stored, row_stored = ph.sem("idx_ready"), ph.sem2("gathered"), ph.sem2("st_stored"), ph.sem2("row_stored")
        names = (
            "transposed", "xT_copied", "qk_done", "qT_copied", "prod_done", "values_done", "scores_done", "root_copied",
            "sc_copied", "leak_done", "mh_done", "diff_m", "diff_done", "exp_done", "weighted", "m_stored")
        (transposed, xT_copied, qk_done, qT_copied, prod_done, values_done, scores_done, root_copied,
         sc_copied, leak_done, mh_done, diff_m, diff_done, exp_done, weighted, m_stored) = (ph.sem(n) for n in names)
        max_done, scaled, decayed, acc_done, cut_ready, cleared = (ph.sem(n) for n in ("max_done", "scaled", "decayed", "acc_done", "cut_ready", "cleared"))
        score = [v[:] for v in sc] if not first else [bank[6][:, 0:G * H].rearrange("p (k h) -> p k h", k=G)] * 2

        def store_state(eng, i, g):
            t, group, step = (now(eng, v) for v in (i * (2 * G) + g * G, at2(i, g), at8(i, g * G + 3)))
            eng.wait_ge(m_stored, group)
            eng.wait_ge(acc_done, step)
            eng.dma_start(table[:, bass.ds(t, G), :], st[g][:]).then_inc(st_stored[g], 16)

        with nc.Block() as block:
            @block.gpsimd
            def _(pool):
                limit = pool.to_reg(s.N - 1)
                with pool.Fori(0, iters) as i:
                    for g in range(2):
                        column, freed, stored, ready = (now(pool, v) for v in (i * (4 * G) + g * 2 * G, at2(i, g, back=2), landed(i, back=1), 2 * i + (g + 1)))
                        pool.wait_ge(transposed, freed)
                        pool.tensor_copy(idx[g][:], s.gather_idx[:, bass.ds(column, 2 * G)]).then_inc(idx_ready, 1)
                        pool.wait_ge(idx_ready, 1)
                        pool.wait_ge(idx_ready, ready)
                        if not first:
                            pool.wait_ge(row_stored[g], stored)
                        for k in range(G):
                            pool.indirect_dma_start(xs[g][:, k, :], None, x_src, bass.IndirectOffsetOnAxis(ap=idx[g][:, k:k + 1], axis=0),
                                                    bounds_check=limit, oob_is_err=False).then_inc(gathered[g], 16)
                            pool.indirect_dma_start(xd[g][:, k, :], None, x_src, bass.IndirectOffsetOnAxis(ap=idx[g][:, G + k:G + k + 1], axis=0),
                                                    bounds_check=limit, oob_is_err=False).then_inc(gathered[g], 16)

            @block.tensor
            def _(pe):
                start_counts(pe, [transposed, qk_done, scores_done] + [values_done] * first, [values_done] * (not first))

                def turn(i, g):
                    pe.wait_ge(gathered[g], 16 * 2 * G * i + 16 * 2 * G)
                    pe.wait_ge(xT_copied, at2(i, g, back=1))
                    for k in range(G):
                        pe.transpose(bank[0][:, k * D:(k + 1) * D], xs[g][:, k, :], s.ident[:])
                    for k in range(G):
                        ins = pe.transpose(bank[1][:, k * D:(k + 1) * D], xd[g][:, k, :], s.ident[:])
                    ins.then_inc(transposed, 1)

                def project(i, g):
                    pe.wait_ge(xT_copied, at2(i, g))
                    pe.wait_ge(qT_copied, at2(i, g, back=1))
                    pe.matmul(bank[2][:], s.Wq[:], xdT[g][:], start=True, stop=True)
                    pe.wait_ge(prod_done, at2(i, g, back=1))
                    pe.matmul(bank[3][:], s.Wk[:], xsT[g][:], start=True, stop=True).then_inc(qk_done, 1)
                    pe.wait_ge(weighted, at2(i, g, back=2))
                    for k in range(G):
                        ins = pe.matmul(value_bank[g][:, k * D:(k + 1) * D], xsT[g][:, k, :], s.Wv[:], start=True, stop=True)
                    pe.wait_ge(root_copied, at2(i, g, back=1))
                    for k in range(G):
                        pe.matmul(bank[5][:, k * D:(k + 1) * D], xdT[g][:, k, :], s.WrI[:], start=True, stop=False)
                        ins = pe.matmul(bank[5][:, k * D:(k + 1) * D], s.ones3[:], s.brv_parts[:], start=False, stop=True)
                    ins.then_inc(values_done, 1)

                def score_products(i, g):
                    pe.wait_ge(prod_done, at2(i, g))
                    pe.wait_ge(diff_m, at2(i, g, back=1))
                    for k in range(G):
                        ins = pe.matmul(bank[6][:, k * H:(k + 1) * H], prod[g][:, k, :], s.headsel[:], start=True, stop=True)
                    ins.then_inc(scores_done, 1)

                def score_rows(i, g):
                    pe.wait_ge(xT_copied, at2(i, g))
                    pe.wait_ge(sc_copied, at2(i, g, back=1))
                    for k in range(G):
                        pe.matmul(bank[6][:, k * H:(k + 1) * H], xsT[g][:, k, :], s.att_s[:], start=True, stop=False)
                        ins = pe.matmul(bank[6][:, k * H:(k + 1) * H], xdT[g][:, k, :], s.att_d[:], start=False, stop=True)
                    ins.then_inc(scores_done, 1)

                def values(i, g):
                    for k in range(G):
                        pe.wait_ge(scaled, at8(i, g * G + k, back=4))
                        pe.matmul(bank[2 + k][:], xsT[g][:, k, :], s.Wz[:], start=True, stop=True).then_inc(values_done, 1)

                if first:
                    in_rounds(pe, iters, (project, 0), (turn, 1), (score_products, 0))
                else:
                    in_rounds(pe, iters, (score_rows, 0), (turn, 1), (values, 0))

            @block.scalar
            def _(act):
                start_counts(act, [xT_copied, qT_copied, root_copied, exp_done], [scaled])
                act.activation(warm[:], s.eps[:], ACT.Exp)

                def copy_rows(i, g):
                    act.wait_ge(transposed, at2(i, g))
                    if first:
                        act.wait_ge(values_done, at2(i, g, back=2))
                    else:
                        act.wait_ge(values_done, at8(i, g * G + 3, back=8))
                    act.activation(xsT[g][:], rows4(bank[0]), ACT.Copy)
                    act.activation(xdT[g][:], rows4(bank[1]), ACT.Copy).then_inc(xT_copied, 1)

                def queries(i, g):
                    act.wait_ge(qk_done, at2(i, g))
                    act.wait_ge(prod_done, at2(i, g, back=2))
                    act.activation(qT[g][:], rows4(bank[2]), ACT.Identity, bias=s.bq[:]).then_inc(qT_copied, 1)

                def roots(i, g):
                    act.wait_ge(values_done, at2(i, g))
                    act.wait_ge(row_stored[g], landed(i, back=1))
                    act.activation(root[g][:], rows4(bank[5]), ACT.Copy).then_inc(root_copied, 1)

                def weights(i, g):
                    act.wait_ge(diff_done, at2(i, g))
                    act.wait_ge(acc_done, at8(i, g * G + 3, back=8))
                    act.activation(wt[g][:].rearrange("p k two (h w) -> p (k two) h w", h=H)[:, :, :, hw - 1],
                                   diff[g][:].rearrange("p k two h -> p (k two) h"), ACT.Exp).then_inc(exp_done, 1)

                def weigh(i, g):
                    weights(i, g)
                    act.wait_ge(exp_done, at2(i, g))
                    for k in range(G):
                        act.wait_ge(values_done, at8(i, g * G + k))
                        for h in range(H):
                            ins = act.activation(wt[g][:, k, 1, h * hw:h * hw + D], bank[2 + k][:, h * D:(h + 1) * D], ACT.Copy,
                                                 scale=wt[g][:, k, 1, (h + 1) * hw - 1:(h + 1) * hw])
                        ins.then_inc(scaled, 1)

                if first:
                    in_rounds(act, iters, (queries, 0), (weights, -1), (roots, 0), (copy_rows, 1))
                else:
                    start_counts(act, dmas=st_stored)
                    in_rounds(act, iters, (copy_rows, 1), (weigh, 0), (lambda i, g: store_state(act, i, g), -1))

            @block.vector
            def _(dve):
                start_counts(dve, [prod_done, mh_done, diff_m, diff_done, weighted, m_stored, sc_copied, leak_done, cut_ready], [max_done, decayed, acc_done])
                dve.memset(st[1][:], 0.0).then_inc(cleared, 1)
                dve.memset(mh[1][:], 0.0).then_inc(cleared, 1)
                dve.wait_ge(cleared, 2)

                def products(i, g):
                    dve.wait_ge(qk_done, at2(i, g))
                    dve.wait_ge(qT_copied, at2(i, g))
                    dve.wait_ge(scores_done, at2(i, g, back=2))
                    dve.scalar_tensor_tensor(prod[g][:], rows4(bank[3]), s.bk[:], qT[g][:], ALU.add, ALU.mult).then_inc(prod_done, 1)

                def maxima(i, g):
                    dve.wait_ge(diff_done, at2(i, g, back=2))
                    dve.tensor_copy(cut4[g][:], s.cut[:, bass.ds(i * (2 * G) + g * G, G)]).then_inc(cut_ready, 1)
                    if first:
                        dve.wait_ge(scores_done, at2(i, g))
                    else:
                        dve.wait_ge(scores_done, at2(i, g))
                        dve.tensor_copy(leak[g][:], bank[6][:, 0:G * H].rearrange("p (k h) -> p k h", k=G)).then_inc(sc_copied, 1)
                        dve.wait_ge(sc_copied, at2(i, g))
                        dve.wait_ge(diff_m, at2(i, g, back=2))
                        dve.scalar_tensor_tensor(sc[g][:], leak[g][:], 0.2, leak[g][:], ALU.mult, ALU.max).then_inc(leak_done, 1)
                        dve.wait_ge(leak_done, at2(i, g))
                    dve.wait_ge(max_done, at8(i, g * G, back=1))
                    dve.wait_ge(m_stored, at2(i, g, back=2))
                    dve.tensor_copy(mh[g][:, 0, :], mh[1 - g][:, G, :]).then_inc(mh_done, 1)
                    dve.wait_ge(mh_done, at2(i, g))
                    dve.wait_ge(cut_ready, at2(i, g))
                    for k in range(G):
                        dve.scalar_tensor_tensor(mh[g][:, k + 1, :], mh[g][:, k, :], cut4[g][:, k:k + 1], score[g][:, k, :], ALU.add, ALU.max).then_inc(max_done, 1)
                        dve.wait_ge(max_done, at8(i, g * G + k))
                    dve.wait_ge(exp_done, at2(i, g, back=2))
                    dve.tensor_tensor(diff[g][:, :, 0, :], mh[g][:, 0:G, :], mh[g][:, 1:G + 1, :], ALU.subtract)
                    dve.tensor_tensor(diff[g][:, :, 1, :], score[g], mh[g][:, 1:G + 1, :], ALU.subtract).then_inc(diff_m, 1)
                    dve.wait_ge(diff_m, at2(i, g))
                    cuts = cut4[g][:].rearrange("p (k a) -> p k a", a=1).to_broadcast([P, G, H])
                    dve.tensor_tensor(diff[g][:, :, 0, :], diff[g][:, :, 0, :], cuts, ALU.add).then_inc(diff_done, 1)

                def sums(i, g):
                    dve.wait_ge(st_stored[g], landed(i, back=1))
                    dve.tensor_copy(st[g][:, :, A:A + H], mh[g][:, 1:G + 1, :]).then_inc(m_stored, 1)
                    dve.wait_ge(exp_done, at2(i, g))
                    if first:
                        dve.wait_ge(values_done, at2(i, g))
                        w4 = wt[g][:, :, 1, :].rearrange("p k (h w) -> p k h w", h=H)
                        dve.tensor_tensor(w4[:, :, :, 0:C], value_bank[g][:].rearrange("p (k h c) -> p k h c", k=G, h=H),
                                          w4[:, :, :, C:C + 1].to_broadcast([P, G, H, C]), ALU.mult).then_inc(weighted, 1)
                        dve.wait_ge(weighted, at2(i, g))
                    for k in range(G):
                        kk = g * G + k
                        prev = st[g][:, k - 1, 0:A] if k else st[1 - g][:, G - 1, 0:A]
                        dve.wait_ge(acc_done, at8(i, kk, back=1))
                        if not first:
                            dve.wait_ge(scaled, at8(i, kk))
                            for h in range(H):
                                ins = dve.scalar_tensor_tensor(st[g][:, k, h * hw:(h + 1) * hw], prev[:, h * hw:(h + 1) * hw],
                                                               wt[g][:, k, 0, (h + 1) * hw - 1:(h + 1) * hw], wt[g][:, k, 1, h * hw:(h + 1) * hw],
                                                               ALU.mult, ALU.add)
                            ins.then_inc(acc_done, 1)
                            continue
                        dve.tensor_tensor(dec[k % 2][:].rearrange("p (h w) -> p h w", h=H), prev.rearrange("p (h w) -> p h w", h=H),
                                          wt[g][:, k, 0, :].rearrange("p (h w) -> p h w", h=H)[:, :, hw - 1:hw].to_broadcast([P, H, hw]), ALU.mult).then_inc(decayed, 1)
                        dve.wait_ge(decayed, at8(i, kk))
                        dve.tensor_tensor(st[g][:, k, 0:A], dec[k % 2][:], wt[g][:, k, 1, :], ALU.add).then_inc(acc_done, 1)

                if first:
                    in_rounds(dve, iters, (products, 0), (sums, -1), (maxima, 0))
                else:
                    in_rounds(dve, iters, (maxima, 1), (sums, 0))

            @block.sync
            def _(sp):
                start_counts(sp, dmas=row_stored)
                if first:
                    start_counts(sp, dmas=st_stored)

                def store_rows(i, g):
                    t, group = now(sp, i * (2 * G) + g * G), now(sp, at2(i, g))
                    if first:
                        sp.wait_ge(root_copied, group)
                        sp.dma_start(rows_out[:, bass.ds(t, G), :], root[g][:]).then_inc(row_stored[g], 16)
                    else:
                        sp.wait_ge(gathered[g], 16 * 2 * G * i + 16 * 2 * G)
                        sp.dma_start(rows_out[:, bass.ds(t, G), :], xd[g][:]).then_inc(row_stored[g], 16)

                if first:
                    in_rounds(sp, iters, (store_rows, 0), (lambda i, g: store_state(sp, i, g), -1))
                else:
                    in_rounds(sp, iters, (store_rows, 0))
                for g in range(2):
                    sp.wait_ge(row_stored[g], landed(iters - 1))
                    sp.wait_ge(st_stored[g], landed(iters - 1))


def patch_phase(nc, s, table, W, hw):
    T = s.T
    A = H * hw if hw else W
    flat = table.rearrange("p t w -> (p t) w")
    halves = [(0, A)] if A <= G * D else [(0, A // 2), (A // 2, A)]
    with Phase(nc, f"patch{W}") as ph:
        bank = ph.banks()
        head, tail, head_out, tail_out = (ph.sb(n, [P, W]) for n in ("head", "tail", "head_out", "tail_out"))
        far = ph.sb("far", [P, G, D])
        red, best = ph.sb("red", [P, 4, H]), ph.sb("best", [P, 2, H])
        diff, wts = ph.sb("diff", [P, 2, H]), ph.sb("wts", [P, 2, H])
        head_loaded, loaded, turned, calc, exp_done, joined, stored = (
            ph.sem(n) for n in ("head_loaded", "loaded", "turned", "calc", "exp_done", "joined", "stored"))
        sums = [0]
        with nc.Block() as block:
            @block.gpsimd
            def _(pool):
                pool.indirect_dma_start(head[:], None, flat, bass.IndirectOffsetOnAxis(ap=s.head_row[:], axis=0),
                                        bounds_check=P * T - 1, oob_is_err=False).then_inc(head_loaded, 16)

            @block.sync
            def _(sp):
                sp.dma_start(tail[:], table[:, T - 1, :]).then_inc(loaded, 16)

            @block.vector
            def _(dve):
                n = [0]

                def done(ins):
                    n[0] += 1
                    ins.then_inc(calc, 1)
                    dve.wait_ge(calc, n[0])

                dve.wait_ge(loaded, 16)
                dve.wait_ge(head_loaded, 16)
                if hw:
                    dve.wait_ge(turned, 1)
                    for j, (src, m) in enumerate(((0, s.far_tt), (1, s.far_th), (0, s.far_ht), (1, s.far_hh))):
                        done(dve.tensor_tensor(far[:], rows4(bank[src]), m[:].rearrange("p (a d) -> p a d", a=1).to_broadcast([P, G, P]), ALU.add))
                        done(dve.tensor_reduce(red[:, j, :], far[:], X, ALU.max))
                    for j in range(2):
                        done(dve.tensor_tensor(best[:, j, :], red[:, 2 * j, :], red[:, 2 * j + 1, :], ALU.max))
                    for j, part in enumerate((tail, head)):
                        done(dve.tensor_tensor(diff[:, j, :], part[:, A:A + H], best[:, j, :], ALU.subtract))
                    sums[0] = n[0]
                    dve.wait_ge(exp_done, 1)
                    for j, part in enumerate((tail, head)):
                        v = part[:, 0:A].rearrange("p (h w) -> p h w", h=H)
                        done(dve.tensor_tensor(v, v, wts[:, j, :].rearrange("p (h a) -> p h a", a=1).to_broadcast([P, H, hw]), ALU.mult))
                        done(dve.tensor_copy((tail_out, head_out)[j][:, A:A + H], best[:, j, :]))
                else:
                    done(dve.tensor_copy(best[:, 0, :], s.trash[:].to_broadcast([P, H])))
                sums.append(n[0])
                dve.wait_ge(joined, 1)
                for j, out in enumerate((tail_out, head_out)):
                    for b, (lo, hi) in enumerate(halves):
                        done(dve.tensor_copy(out[:, lo:hi], bank[2 + 2 * j + b][:, 0:hi - lo]))
                sums.append(n[0])

            @block.scalar
            def _(act):
                if hw:
                    act.wait_ge(calc, sums[0])
                    act.activation(wts[:], diff[:], ACT.Exp).then_inc(exp_done, 1)

            @block.tensor
            def _(pe):
                if hw:
                    pe.wait_ge(loaded, 16)
                    pe.wait_ge(head_loaded, 16)
                    for j, part in enumerate((tail, head)):
                        for h in range(H):
                            ins = pe.transpose(bank[j][:, h * P:(h + 1) * P], part[:, A + h:A + h + 1].to_broadcast([P, P]), s.ident[:])
                    ins.then_inc(turned, 1)
                pe.wait_ge(loaded, 16)
                pe.wait_ge(head_loaded, 16)
                pe.wait_ge(calc, sums[1])
                for j, (from_tail, from_head) in enumerate(((s.tail_tail, s.head_tail), (s.tail_head, s.head_head))):
                    for b, (lo, hi) in enumerate(halves):
                        pe.matmul(bank[2 + 2 * j + b][:, 0:hi - lo], from_tail[:], tail[:, lo:hi], start=True, stop=False)
                        ins = pe.matmul(bank[2 + 2 * j + b][:, 0:hi - lo], from_head[:], head[:, lo:hi], start=False, stop=True)
                ins.then_inc(joined, 1)

        with nc.Block() as block:
            @block.gpsimd
            def _(pool):
                pool.indirect_dma_start(flat, bass.IndirectOffsetOnAxis(ap=s.head_row[:], axis=0), head_out[:], None,
                                        bounds_check=P * T - 1, oob_is_err=False).then_inc(stored, 16)
                pool.wait_ge(stored, 16)
                pool.dma_start(table[:, T - 1, :], tail_out[:]).then_inc(stored, 16)
                pool.wait_ge(stored, 32)


def backward0_phase(nc, s, a):
    T, iters, hw = s.T, s.T // (2 * G), C + 1
    with Phase(nc, "bwd0") as ph:
        bank = ph.banks()
        st, root, src_rows = ph.two("st", [P, G, W0]), ph.two("root", [P, G, D]), ph.two("src_rows", [P, G, P], I32)
        edgeT, hid, filt = ph.two("edgeT", [RBF, G, P]), ph.two("hid", [P, G, P]), ph.two("filt", [P, G, D])
        inv, Y, x1, x1T, msg, merged, equal, cross = ph.two("inv", [P, G, H]), *(
            ph.two(n, [P, G, D]) for n in ("Y", "x1", "x1T", "msg", "merged", "equal", "cross"))
        stats, mv, sd, rs = ph.two("stats", [P, G, 6]), ph.two("mv", [P, G, 2]), ph.two("sd", [P, G]), ph.two("rs", [P, G])
        earlier, dup, add_f, add_idx = ph.two("earlier", [P, G, D]), ph.two("dup", [P, G]), ph.two("add_f", [P, G]), ph.two("add_idx", [P, G], I32)
        dup_pair, warm = ph.two("dup_pair", [P, G // 2]), ph.sb("warm", [P, 1])
        end_idx, inner, srcs, to_trash = ph.two("end_idx", [P, G], I32), ph.two("inner", [P, G], U32), ph.two("srcs", [P, G]), ph.two("to_trash", [P, G])
        loaded, edge_loaded, src_loaded, x1_stored = (ph.sem2(n) for n in ("loaded", "edge_loaded", "src_loaded", "x1_stored"))
        added, group_before_added = ph.sem("added"), ph.sem("group_before_added")
        names = ("hid_done", "hid_copied", "filt_done", "filt_copied", "x1T_done", "x1T_copied", "h_done",
                 "merge_done", "merge_copied", "inv_done", "Y_scaled", "Y_done", "stat_done", "aggr_done", "sd_done", "rs_done",
                 "rows_done", "msg_done", "equal_done", "dup_done", "dup_summed", "idx_sum", "add_ready", "meta_ready", "end_ready")
        (hid_done, hid_copied, filt_done, filt_copied, x1T_done, x1T_copied, h_done,
         merge_done, merge_copied, inv_done, Y_scaled, Y_done, stat_done, aggr_done, sd_done, rs_done,
         rows_done, msg_done, equal_done, dup_done, dup_summed, idx_sum, add_ready, meta_ready, end_ready) = (ph.sem(n) for n in names)
        spread, cleared = ph.sem("spread"), ph.sem("cleared")

        def first_step(i, g):
            return (T - G - g * G) - (2 * G) * i

        with nc.Block() as block:
            @block.sync
            def _(sp):
                start_counts(sp, dmas=edge_loaded + src_loaded)
                start_counts(sp, dmas=loaded, n=2)

                def load(i, g):
                    t, freed = now(sp, first_step(i, g)), now(sp, at2(i, g, back=2))
                    sp.wait_ge(Y_done, freed)
                    sp.dma_start(st[g][:], s.state0[:, bass.ds(t, G), :]).then_inc(loaded[g], 16)
                    sp.dma_start(root[g][:], s.root0[:, bass.ds(t, G), :]).then_inc(loaded[g], 16)
                    sp.wait_ge(equal_done, freed)
                    src_of_steps = a["src_steps"][bass.ds(t, G), :].rearrange("k p -> (k p)").rearrange("(a n) -> a n", a=1)
                    sp.dma_start(src_rows[g][:].rearrange("q k p -> q (k p)"), src_of_steps.to_broadcast([P, G * P])).then_inc(src_loaded[g], 16)
                    sp.wait_ge(hid_done, freed)
                    sp.dma_start(edgeT[g][:], a["edge_steps"][:, bass.ds(t, G), :]).then_inc(edge_loaded[g], 16)

                in_rounds(sp, iters, (load, 0))

            @block.gpsimd
            def _(pool):
                limit, trash_limit = pool.to_reg(s.N - 1), pool.to_reg(s.agg_rows - 1)
                start_counts(pool, [end_ready, group_before_added])
                first_dma(pool, s, ph, [*x1_stored, added])

                def scatter(i, g):
                    t, freed, group, spread_all = (now(pool, v) for v in (first_step(i, g), scattered_at(i, G, back=1), at2(i, g), at8(i, g * G + G - 1)))
                    pool.wait_ge(x1_stored[g], freed)
                    pool.tensor_copy(end_idx[g][:], s.end_idx[:, bass.ds(t, G)]).then_inc(end_ready, 1)
                    before_pair = [now(pool, 16 * 2 * G * i + 16 * (g * G + k + 1)) for k in (0, 2)]
                    pool.wait_ge(end_ready, 3)
                    pool.wait_ge(end_ready, group)
                    pool.wait_ge(spread, spread_all)
                    for j, pair in enumerate(((3, 2), (1, 0))):
                        pool.wait_ge(end_ready, 3)
                        pool.wait_ge(added, before_pair[j])
                        if j == 0:
                            pool.sem_inc(group_before_added, 1)
                            pool.wait_ge(end_ready, 3)
                            pool.wait_ge(merge_copied, group)
                            pool.wait_ge(add_ready, group)
                        for k in pair:
                            pool.indirect_dma_start(s.agg1, bass.IndirectOffsetOnAxis(ap=add_idx[g][:, k:k + 1], axis=0), merged[g][:, k, :], None,
                                                    bounds_check=trash_limit, oob_is_err=True, compute_op=ALU.add).then_inc(added, 16)
                        for k in pair:
                            pool.indirect_dma_start(s.x1, bass.IndirectOffsetOnAxis(ap=end_idx[g][:, k:k + 1], axis=0), x1[g][:, k, :], None,
                                                    bounds_check=limit, oob_is_err=False).then_inc(x1_stored[g], 16)

                in_rounds(pool, iters, (scatter, 0))
                pool.wait_ge(added, 16 * T + 16)
                for g in range(2):
                    pool.wait_ge(x1_stored[g], scattered_at(iters - 1, G))

            @block.tensor
            def _(pe):
                start_counts(pe, [hid_done, filt_done, x1T_done, h_done, merge_done])

                def hidden(i, g):
                    pe.wait_ge(edge_loaded[g], landed(i))
                    pe.wait_ge(hid_copied, at2(i, g, back=1))
                    pe.matmul(bank[2][:], s.W1[:], edgeT[g][:], start=True, stop=True).then_inc(hid_done, 1)

                def filters(i, g):
                    pe.wait_ge(hid_copied, at2(i, g))
                    pe.wait_ge(filt_copied, at2(i, g, back=1))
                    for k in range(G):
                        pe.matmul(bank[3][:, k * D:(k + 1) * D], hid[g][:, k, :], s.W2[:], start=True, stop=False)
                        ins = pe.matmul(bank[3][:, k * D:(k + 1) * D], s.ones3[:], s.b2_parts[:], start=False, stop=True)
                    ins.then_inc(filt_done, 1)

                def turn(i, g):
                    pe.wait_ge(spread, at8(i, g * G + G - 1))
                    pe.wait_ge(x1T_copied, at2(i, g, back=1))
                    for k in range(G):
                        ins = pe.transpose(bank[4][:, k * D:(k + 1) * D], x1[g][:, k, :], s.ident[:])
                    ins.then_inc(x1T_done, 1)

                def project(i, g):
                    pe.wait_ge(x1T_copied, at2(i, g))
                    pe.wait_ge(msg_done, at2(i, g, back=1))
                    for k in range(G):
                        pe.matmul(bank[5][:, k * D:(k + 1) * D], x1T[g][:, k, :], s.Wl[:], start=True, stop=False)
                        ins = pe.matmul(bank[5][:, k * D:(k + 1) * D], s.ones3[:], s.bl_parts[:], start=False, stop=True)
                    ins.then_inc(h_done, 1)

                def merge(i, g):
                    pe.wait_ge(msg_done, at2(i, g))
                    pe.wait_ge(equal_done, at2(i, g))
                    pe.wait_ge(merge_copied, at2(i, g, back=1))
                    for k in range(G):
                        other = k ^ 1
                        pe.matmul(bank[6][:, k * D:(k + 1) * D], equal[g][:, k, :], msg[g][:, k, :], start=True, stop=False)
                        ins = pe.matmul(bank[6][:, k * D:(k + 1) * D], cross[g][:, other, :], msg[g][:, other, :], start=False, stop=True)
                    ins.then_inc(merge_done, 1)

                in_rounds(pe, iters, (merge, -1), (turn, 0), (hidden, 1), (project, 0), (filters, 1))

            @block.scalar
            def _(act):
                start_counts(act, [hid_copied, filt_copied, x1T_copied, merge_copied, sd_done])
                act.activation(warm[:], s.eps[:], ACT.Sqrt)

                def copy_hidden(i, g):
                    act.wait_ge(hid_done, at2(i, g))
                    act.wait_ge(filt_done, at2(i, g, back=2))
                    act.activation(hid[g][:], rows4(bank[2]), ACT.Relu, bias=s.b1[:]).then_inc(hid_copied, 1)

                def root_of_variance(i, g):
                    act.wait_ge(aggr_done, at2(i, g))
                    act.wait_ge(rs_done, at2(i, g, back=2))
                    act.activation(sd[g][:], mv[g][:, :, 1], ACT.Sqrt, bias=s.eps[:]).then_inc(sd_done, 1)

                def copy_filters(i, g):
                    act.wait_ge(filt_done, at2(i, g))
                    act.wait_ge(msg_done, at2(i, g, back=2))
                    act.activation(filt[g][:], rows4(bank[3]), ACT.Copy).then_inc(filt_copied, 1)

                def copy_turned(i, g):
                    act.wait_ge(x1T_done, at2(i, g))
                    act.wait_ge(h_done, at2(i, g, back=2))
                    act.activation(x1T[g][:], rows4(bank[4]), ACT.Copy).then_inc(x1T_copied, 1)

                def copy_merged(i, g):
                    act.wait_ge(merge_done, at2(i, g))
                    act.wait_ge(group_before_added, at2(i, g, back=1))
                    act.activation(merged[g][:], rows4(bank[6]), ACT.Copy).then_inc(merge_copied, 1)

                in_rounds(act, iters, (copy_merged, -1), (copy_turned, 0), (copy_hidden, 1), (root_of_variance, 1), (copy_filters, 1))

            @block.vector
            def _(dve):
                start_counts(dve, [meta_ready, inv_done, Y_scaled, Y_done, stat_done, aggr_done, rs_done, rows_done,
                                   msg_done, equal_done, dup_done, dup_summed, idx_sum, add_ready], [spread])
                dve.memset(x1[1][:], 0.0).then_inc(cleared, 1)
                dve.wait_ge(cleared, 1)

                def rows(i, g):
                    t, index_read, spread_read = now(dve, first_step(i, g)), now(dve, at2(i, g, back=2)), now(dve, at8(i, g * G + G - 1, back=2 * G))
                    dve.wait_ge(add_ready, index_read)
                    dve.wait_ge(spread, spread_read)
                    dve.tensor_copy(srcs[g][:], s.src_f[:, bass.ds(t, G)])
                    dve.tensor_copy(to_trash[g][:], s.to_trash[:, bass.ds(t, G)])
                    dve.tensor_copy(inner[g][:], s.inner[:, bass.ds(t, G)]).then_inc(meta_ready, 1)
                    dve.wait_ge(loaded[g], landed(i, 2))
                    sums = st[g][:, :, 0:H * hw].rearrange("p k (h w) -> p k h w", h=H)
                    dve.reciprocal(inv[g][:], sums[:, :, :, C]).then_inc(inv_done, 1)
                    dve.wait_ge(inv_done, at2(i, g))
                    y4 = Y[g][:].rearrange("p k (h c) -> p k h c", h=H)
                    dve.tensor_tensor(y4, sums[:, :, :, 0:C], inv[g][:].rearrange("p k (h a) -> p k h a", a=1).to_broadcast([P, G, H, C]), ALU.mult).then_inc(Y_scaled, 1)
                    dve.wait_ge(Y_scaled, at2(i, g))
                    dve.tensor_tensor(Y[g][:], Y[g][:], root[g][:], ALU.add).then_inc(Y_done, 1)
                    dve.wait_ge(Y_done, at2(i, g))
                    dve.wait_ge(sd_done, at2(i, g, back=2))
                    rowstats(dve, Y[g], stats[g], mv[g], stat_done, aggr_done, i, g)

                def targets(i, g):
                    dve.wait_ge(meta_ready, at2(i, g))
                    dve.wait_ge(src_loaded[g], landed(i))
                    dve.wait_ge(merge_done, at2(i, g, back=2))
                    own = srcs[g][:].rearrange("p (k a) -> p k a", a=1).to_broadcast([P, G, P])
                    dve.tensor_tensor(equal[g][:], src_rows[g][:], own, ALU.is_equal)
                    dve.tensor_tensor(cross[g][:, 0::2, :], src_rows[g][:, 1::2, :], own[:, 0::2, :], ALU.is_equal)
                    dve.tensor_tensor(cross[g][:, 1::2, :], src_rows[g][:, 0::2, :], own[:, 1::2, :], ALU.is_equal).then_inc(equal_done, 1)
                    dve.wait_ge(equal_done, at2(i, g))
                    for k in range(G):
                        dve.tensor_tensor_reduce(out=earlier[g][:, k, :], in0=equal[g][:, k, :], in1=s.lower[:], scale=1.0, scalar=0.0,
                                                 op0=ALU.mult, op1=ALU.add, accum_out=dup[g][:, k:k + 1])
                    dve.tensor_reduce(dup_pair[g][:], cross[g][:, 0::2, :], X, ALU.add).then_inc(dup_done, 1)
                    dve.wait_ge(dup_done, at2(i, g))
                    dve.tensor_tensor(dup[g][:, 0::2], dup[g][:, 0::2], dup_pair[g][:], ALU.add).then_inc(dup_summed, 1)
                    dve.wait_ge(dup_summed, at2(i, g))
                    dve.scalar_tensor_tensor(add_f[g][:], dup[g][:], 1.0, to_trash[g][:], ALU.min, ALU.mult).then_inc(idx_sum, 1)

                def indices(i, g):
                    dve.wait_ge(idx_sum, at2(i, g))
                    dve.wait_ge(group_before_added, at2(i, g, back=1))
                    dve.tensor_tensor(add_idx[g][:], add_f[g][:], srcs[g][:], ALU.add).then_inc(add_ready, 1)

                def normalise(i, g):
                    dve.wait_ge(x1_stored[g], scattered_at(i, G, back=1))
                    dve.wait_ge(x1T_done, at2(i, g, back=2))
                    norm_rows(dve, sd_done, Y[g], x1[g], mv[g], sd[g], rs[g], rs_done, rows_done, i, g)
                    spread_rows(dve, x1, inner, spread, cleared, rows_done, meta_ready, i, g)

                def messages(i, g):
                    dve.wait_ge(h_done, at2(i, g))
                    dve.wait_ge(filt_copied, at2(i, g))
                    dve.wait_ge(merge_done, at2(i, g, back=2))
                    dve.tensor_tensor(msg[g][:], rows4(bank[5]), filt[g][:], ALU.mult).then_inc(msg_done, 1)

                in_rounds(dve, iters, (messages, -1), (normalise, 0), (indices, 0), (rows, 1), (targets, 1))


def spread_rows(dve, x, inner, spread, cleared, rows_done, meta_ready, i, g):
    group, before = now(dve, at2(i, g)), [now(dve, at8(i, g * G + k, back=1)) for k in range(G)]
    for k in reversed(range(G)):
        later = x[g][:, k + 1, :] if k < G - 1 else x[1 - g][:, 0, :]
        dve.wait_ge(cleared, 1)
        if k == G - 1:
            dve.wait_ge(rows_done, group)
            dve.wait_ge(meta_ready, group)
        dve.wait_ge(spread, before[G - 1 - k])
        dve.copy_predicated(x[g][:, k, :], inner[g][:, k:k + 1].to_broadcast([P, D]), later).then_inc(spread, 1)


def norm_rows(dve, act_sd, Y, out, mv, sd, rs, rs_done, out_done, i, g):
    dve.wait_ge(act_sd, at2(i, g))
    dve.reciprocal(rs[:], sd[:]).then_inc(rs_done, 1)
    dve.wait_ge(rs_done, at2(i, g))
    for k in range(G):
        ins = dve.tensor_scalar(out[:, k, :], Y[:, k, :], mv[:, k, 0:1], rs[:, k:k + 1], ALU.subtract, ALU.mult)
    ins.then_inc(out_done, 1)


def dense1_phase(nc, s, a):
    iters = s.blocks // 2
    with Phase(nc, "dense1") as ph:
        xin, agg = ph.two("xin", [P, R, D]), ph.two("agg", [P, R, D])
        Y = [ph.two(f"Y{j}", [P, R, D]) for j in range(3)]
        out = [ph.two(f"out{j}", [P, R, D]) for j in range(3)]
        stats, mv, sd, rs, nb = ([ph.two(f"{n}{j}", [P, R] + w) for j in range(3)] for n, w in (("stats", [6]), ("mv", [2]), ("sd", []), ("rs", []), ("nb", [])))
        loaded, stored = ph.sem2("loaded"), [ph.sem2(f"stored{j}") for j in range(3)]
        Y_done, stat_done, aggr_done, sd_done, rs_done, nb_done, out_done = ([ph.sem(f"{n}{j}") for j in range(3)] for n in (
            "Y_done", "stat_done", "aggr_done", "sd_done", "rs_done", "nb_done", "out_done"))
        tables = (s.x2, s.x3, s.out)

        with nc.Block() as block:
            @block.sync
            def _(sp):
                start_counts(sp, dmas=loaded, n=2)
                start_counts(sp, dmas=stored[0] + stored[1] + stored[2])

                def load(i, g):
                    row, freed = now(sp, dense_row(s, i, g)), now(sp, at2(i, g, back=2))
                    sp.wait_ge(Y_done[0], freed)
                    sp.dma_start(xin[g][:], of_block(s.x1, row, s)).then_inc(loaded[g], 16)
                    sp.dma_start(agg[g][:], of_block(s.agg1, row, s)).then_inc(loaded[g], 16)

                def store(j):
                    return lambda i, g: store_block(sp, s, tables[j], out[j], out_done[j], stored[j], i, g)

                in_rounds(sp, iters, (store(0), -2), (store(1), -4), (store(2), -6), (load, 2), apart=1)
                for j in range(3):
                    for g in range(2):
                        sp.wait_ge(stored[j][g], landed(iters - 1))

            @block.gpsimd
            def _(pool):
                start_counts(pool, Y_done)
                biases = [None, s.bt_all, s.rbn_all]

                def add(j):
                    def work(i, g):
                        if j == 0:
                            pool.wait_ge(loaded[g], landed(i, 2))
                            one, two = xin[g][:], agg[g][:]
                        else:
                            pool.wait_ge(out_done[j - 1], at2(i, g))
                            one, two = out[j - 1][g][:], biases[j][:].rearrange("p (a d) -> p a d", a=1).to_broadcast([P, R, D])
                        pool.wait_ge(out_done[j], at2(i, g, back=2))
                        pool.tensor_tensor(Y[j][g][:], one, two, ALU.add).then_inc(Y_done[j], 1)
                    return work

                in_rounds(pool, iters, (add(0), 0), (add(1), -2), (add(2), -4))

            @block.vector
            def _(dve):
                start_counts(dve, [*stat_done, *aggr_done, *rs_done, *nb_done])

                def statistics(j):
                    def work(i, g):
                        dve.wait_ge(Y_done[j], at2(i, g))
                        dve.wait_ge(nb_done[j], at2(i, g, back=2))
                        rowstats(dve, Y[j][g], stats[j][g], mv[j][g], stat_done[j], aggr_done[j], i, g)
                    return work

                def scale(j):
                    def work(i, g):
                        dve.wait_ge(out_done[j], at2(i, g, back=2))
                        scales(dve, mv[j][g], sd[j][g], rs[j][g], nb[j][g], sd_done[j], rs_done[j], nb_done[j], i, g)
                    return work

                in_rounds(dve, iters, (scale(0), -1), (scale(1), -3), (scale(2), -5), (statistics(0), 0), (statistics(1), -2), (statistics(2), -4))

            @block.scalar
            def _(act):
                start_counts(act, [*sd_done, *out_done])

                def root_of_variance(j):
                    def work(i, g):
                        act.wait_ge(aggr_done[j], at2(i, g))
                        act.wait_ge(rs_done[j], at2(i, g, back=2))
                        act.activation(sd[j][g][:], mv[j][g][:, :, 1], ACT.Sqrt, bias=s.eps[:]).then_inc(sd_done[j], 1)
                    return work

                def normalise(j):
                    def work(i, g):
                        act.wait_ge(stored[j][g], landed(i, back=1))
                        if j < 2:
                            act.wait_ge(Y_done[j + 1], at2(i, g, back=2))
                        scale_rows(act, Y[j][g], out[j][g], rs[j][g], nb[j][g], nb_done[j], out_done[j], i, g)
                    return work

                act.activation(ph.sb("warm", [P, 1])[:], s.eps[:], ACT.Sqrt)
                in_rounds(act, iters, (normalise(0), -1), (normalise(1), -3), (normalise(2), -5),
                          (root_of_variance(0), 0), (root_of_variance(1), -2), (root_of_variance(2), -4))


def backward2_phase(nc, s, a):
    T, iters, hw = s.T, s.T // (2 * G), D + 1
    with Phase(nc, "bwd2") as ph:
        bank = ph.banks()
        st, own, inv = ph.two("st", [P, G, W2]), ph.two("own", [P, G, D]), ph.two("inv", [P, G, H])
        base = ph.two("base", [P, G, D])
        part, x3, warm = ph.two("part", [P, G, H, D]), ph.two("x3", [P, G, D]), ph.sb("warm", [P, 1])
        stats, mv, sd, rs = ph.two("stats", [P, G, 6]), ph.two("mv", [P, G, 2]), ph.two("sd", [P, G]), ph.two("rs", [P, G])
        end_idx, inner = ph.two("end_idx", [P, G], I32), ph.two("inner", [P, G], U32)
        loaded, scattered, x3_stored = ph.sem2("loaded"), ph.sem2("scattered"), ph.sem2("x3_stored")
        inv_done, base_done, part_done, sum_done, stat_done, aggr_done, sd_done, rs_done, rows_done, end_ready, meta_ready, spread, cleared = (ph.sem(n) for n in (
            "inv_done", "base_done", "part_done", "sum_done", "stat_done", "aggr_done", "sd_done", "rs_done", "rows_done", "end_ready", "meta_ready", "spread", "cleared"))

        def first_step(i, g):
            return (T - G - g * G) - (2 * G) * i

        with nc.Block() as block:
            @block.sync
            def _(sp):
                start_counts(sp, dmas=loaded, n=2)

                def load(i, g):
                    t, freed = now(sp, first_step(i, g)), now(sp, at2(i, g, back=2))
                    sp.wait_ge(part_done, freed)
                    sp.dma_start(st[g][:], s.state2[:, bass.ds(t, G), :]).then_inc(loaded[g], 16)
                    sp.wait_ge(base_done, freed)
                    sp.dma_start(own[g][:], s.own2[:, bass.ds(t, G), :]).then_inc(loaded[g], 16)

                in_rounds(sp, iters, (load, 0))

            @block.gpsimd
            def _(pool):
                limit = pool.to_reg(s.N - 1)
                start_counts(pool, [end_ready, base_done])
                first_dma(pool, s, ph, scattered)

                def add_bias(i, g):
                    pool.wait_ge(loaded[g], landed(i, 2))
                    pool.wait_ge(sum_done, at2(i, g, back=2))
                    pool.tensor_tensor(base[g][:], own[g][:], s.bt_all[:].rearrange("p (a d) -> p a d", a=1).to_broadcast([P, G, D]), ALU.add).then_inc(base_done, 1)

                def scatter(i, g):
                    t, freed, group, ready = (now(pool, v) for v in (first_step(i, g), scattered_at(i, G, back=1), at2(i, g), at8(i, g * G + G - 1)))
                    pool.wait_ge(scattered[g], freed)
                    pool.tensor_copy(end_idx[g][:], s.end_idx[:, bass.ds(t, G)]).then_inc(end_ready, 1)
                    pool.wait_ge(end_ready, 3)
                    pool.wait_ge(end_ready, group)
                    pool.wait_ge(spread, ready)
                    for k in reversed(range(G)):
                        pool.indirect_dma_start(s.x3, bass.IndirectOffsetOnAxis(ap=end_idx[g][:, k:k + 1], axis=0), x3[g][:, k, :], None,
                                                bounds_check=limit, oob_is_err=False).then_inc(scattered[g], 16)

                in_rounds(pool, iters, (scatter, -1), (add_bias, 1))
                for g in range(2):
                    pool.wait_ge(scattered[g], scattered_at(iters - 1, G))

            @block.tensor
            def _(pe):
                start_counts(pe, [sum_done])

                def total(i, g):
                    pe.wait_ge(base_done, at2(i, g))
                    pe.wait_ge(part_done, at2(i, g))
                    pe.wait_ge(rows_done, at2(i, g, back=2))
                    pe.matmul(bank[g][:], s.ident[:], base[g][:], start=True, stop=False)
                    for h in range(H):
                        ins = pe.matmul(bank[g][:], s.ident[:], part[g][:, :, h, :], start=False, stop=(h == H - 1))
                    ins.then_inc(sum_done, 1)

                in_rounds(pe, iters, (total, 0))

            @block.scalar
            def _(act):
                start_counts(act, [sd_done])
                start_counts(act, dmas=x3_stored)
                act.activation(warm[:], s.eps[:], ACT.Sqrt)

                def root_of_variance(i, g):
                    act.wait_ge(aggr_done, at2(i, g))
                    act.wait_ge(rs_done, at2(i, g, back=2))
                    act.activation(sd[g][:], mv[g][:, :, 1], ACT.Sqrt, bias=s.eps[:]).then_inc(sd_done, 1)

                def store(i, g):
                    t, ready = now(act, first_step(i, g)), now(act, at8(i, g * G + G - 1))
                    act.wait_ge(spread, ready)
                    act.dma_start(s.dst3[:, bass.ds(t, G), :], x3[g][:]).then_inc(x3_stored[g], 16)

                in_rounds(act, iters, (store, -1), (root_of_variance, 0))
                for g in range(2):
                    act.wait_ge(x3_stored[g], landed(iters - 1))

            @block.vector
            def _(dve):
                start_counts(dve, [meta_ready, inv_done, part_done, stat_done, aggr_done, rs_done, rows_done], [spread])
                dve.memset(x3[1][:], 0.0).then_inc(cleared, 1)
                dve.wait_ge(cleared, 1)

                def parts(i, g):
                    t, spread_read = now(dve, first_step(i, g)), now(dve, at8(i, g * G + G - 1, back=2 * G))
                    dve.wait_ge(spread, spread_read)
                    dve.tensor_copy(inner[g][:], s.inner[:, bass.ds(t, G)]).then_inc(meta_ready, 1)
                    dve.wait_ge(loaded[g], landed(i, 2))
                    sums = st[g][:, :, 0:H * hw].rearrange("p k (h w) -> p k h w", h=H)
                    dve.reciprocal(inv[g][:], sums[:, :, :, D]).then_inc(inv_done, 1)
                    dve.wait_ge(inv_done, at2(i, g))
                    dve.wait_ge(sum_done, at2(i, g, back=2))
                    for k in range(G):
                        ins = dve.tensor_tensor(part[g][:, k], sums[:, k, :, 0:D], inv[g][:, k, :].rearrange("p (h a) -> p h a", a=1).to_broadcast([P, H, D]), ALU.mult)
                    ins.then_inc(part_done, 1)

                def statistics(i, g):
                    dve.wait_ge(sum_done, at2(i, g))
                    dve.wait_ge(sd_done, at2(i, g, back=2))
                    rowstats(dve, rows4(bank[g]), stats[g], mv[g], stat_done, aggr_done, i, g)

                def normalise(i, g):
                    dve.wait_ge(scattered[g], scattered_at(i, G, back=1))
                    dve.wait_ge(x3_stored[g], landed(i, back=1))
                    norm_rows(dve, sd_done, rows4(bank[g]), x3[g], mv[g], sd[g], rs[g], rs_done, rows_done, i, g)
                    spread_rows(dve, x3, inner, spread, cleared, rows_done, meta_ready, i, g)

                in_rounds(dve, iters, (normalise, -1), (parts, 1), (statistics, 0))


def forward3_phase(nc, s, a):
    T, iters = s.T, s.T // (2 * G)
    with Phase(nc, "fwd3") as ph:
        bank = ph.banks()
        xs, xd, xsT, xdT, old = (ph.two(n, [P, G, D]) for n in ("xs", "xd", "xsT", "xdT", "old"))
        idx, same4, st = ph.two("idx", [P, 2 * G], I32), ph.two("same4", [P, G]), ph.two("st", [P, G, W3])
        idx_ready, gathered, own_loaded, st_stored = ph.sem("idx_ready"), ph.sem2("gathered"), ph.sem2("own_loaded"), ph.sem2("st_stored")
        transposed, xT_copied, rows_done, same_ready, decayed, acc_done, cnt_done, cleared = (
            ph.sem(n) for n in ("transposed", "xT_copied", "rows_done", "same_ready", "decayed", "acc_done", "cnt_done", "cleared"))
        with nc.Block() as block:
            @block.gpsimd
            def _(pool):
                limit = pool.to_reg(s.N - 1)

                def gather(i, g):
                    column, freed, ready = (now(pool, v) for v in (i * (4 * G) + g * 2 * G, at2(i, g, back=2), 2 * i + (g + 1)))
                    pool.wait_ge(transposed, freed)
                    pool.tensor_copy(idx[g][:], s.gather_idx[:, bass.ds(column, 2 * G)]).then_inc(idx_ready, 1)
                    pool.wait_ge(idx_ready, 1)
                    pool.wait_ge(idx_ready, ready)
                    for k in range(G):
                        pool.indirect_dma_start(xs[g][:, k, :], None, s.x3, bass.IndirectOffsetOnAxis(ap=idx[g][:, k:k + 1], axis=0),
                                                bounds_check=limit, oob_is_err=False).then_inc(gathered[g], 16)

                in_rounds(pool, iters, (gather, 0))

            @block.sync
            def _(sp):
                start_counts(sp, dmas=own_loaded)

                def load(i, g):
                    t, freed = now(sp, i * (2 * G) + g * G), now(sp, at2(i, g, back=2))
                    sp.wait_ge(transposed, freed)
                    sp.dma_start(xd[g][:], s.dst3[:, bass.ds(t, G), :]).then_inc(own_loaded[g], 16)

                in_rounds(sp, iters, (load, 0))

            @block.tensor
            def _(pe):
                start_counts(pe, [transposed, rows_done])

                def turn(i, g):
                    pe.wait_ge(gathered[g], 16 * G * i + 16 * G)
                    pe.wait_ge(own_loaded[g], landed(i))
                    pe.wait_ge(xT_copied, at2(i, g, back=2))
                    for k in range(G):
                        pe.transpose(bank[g][:, k * D:(k + 1) * D], xs[g][:, k, :], s.ident[:])
                    for k in range(G):
                        ins = pe.transpose(bank[2 + g][:, k * D:(k + 1) * D], xd[g][:, k, :], s.ident[:])
                    ins.then_inc(transposed, 1)

                def edge_rows(i, g):
                    pe.wait_ge(xT_copied, at2(i, g))
                    pe.wait_ge(acc_done, at8(i, g * G + 3, back=8))
                    for k in range(G):
                        pe.matmul(bank[4 + g][:, k * D:(k + 1) * D], xsT[g][:, k, :], s.WeT[:, 0, :], start=True, stop=False)
                        ins = pe.matmul(bank[4 + g][:, k * D:(k + 1) * D], xdT[g][:, k, :], s.WeT[:, 1, :], start=False, stop=True)
                    ins.then_inc(rows_done, 1)

                in_rounds(pe, iters, (turn, 1), (edge_rows, 0))

            @block.scalar
            def _(act):
                start_counts(act, [xT_copied])
                start_counts(act, dmas=st_stored)

                def copy_rows(i, g):
                    act.wait_ge(transposed, at2(i, g))
                    act.wait_ge(rows_done, at2(i, g, back=2))
                    act.activation(xsT[g][:], rows4(bank[g]), ACT.Copy)
                    act.activation(xdT[g][:], rows4(bank[2 + g]), ACT.Copy).then_inc(xT_copied, 1)

                def store(i, g):
                    t, step = now(act, i * (2 * G) + g * G), now(act, at8(i, g * G + 3))
                    act.wait_ge(acc_done, step)
                    act.wait_ge(cnt_done, step)
                    act.dma_start(s.state3[:, bass.ds(t, G), :], st[g][:]).then_inc(st_stored[g], 16)

                in_rounds(act, iters, (copy_rows, 0), (store, -1))
                for g in range(2):
                    act.wait_ge(st_stored[g], landed(iters - 1))

            @block.vector
            def _(dve):
                start_counts(dve, [same_ready], [decayed, acc_done, cnt_done])
                dve.memset(st[1][:], 0.0).then_inc(cleared, 1)
                dve.wait_ge(cleared, 1)

                def sums(i, g):
                    t, read = now(dve, i * (2 * G) + g * G), now(dve, at8(i, g * G + 3, back=8))
                    dve.wait_ge(acc_done, read)
                    dve.wait_ge(cnt_done, read)
                    dve.tensor_copy(same4[g][:], s.same[:, bass.ds(t, G)]).then_inc(same_ready, 1)
                    dve.wait_ge(same_ready, at2(i, g))
                    dve.wait_ge(rows_done, at2(i, g))
                    dve.wait_ge(st_stored[g], landed(i, back=1))
                    for k in range(G):
                        kk = g * G + k
                        prev = st[g][:, k - 1, :] if k else st[1 - g][:, G - 1, :]
                        dve.wait_ge(acc_done, at8(i, kk, back=1))
                        dve.wait_ge(cnt_done, at8(i, kk, back=1))
                        dve.tensor_scalar(old[g][:, k, :], prev[:, 0:D], same4[g][:, k:k + 1], None, ALU.mult).then_inc(decayed, 1)
                        dve.tensor_scalar(st[g][:, k, D:W3], prev[:, D:W3], same4[g][:, k:k + 1], 1.0, ALU.mult, ALU.add).then_inc(cnt_done, 1)
                        dve.wait_ge(decayed, at8(i, kk))
                        dve.scalar_tensor_tensor(st[g][:, k, 0:D], bank[4 + g][:, k * D:(k + 1) * D], 0.0, old[g][:, k, :], ALU.max, ALU.add).then_inc(acc_done, 1)

                in_rounds(dve, iters, (sums, 0))


def backward3_phase(nc, s, a):
    T, iters = s.T, s.T // (2 * G)
    with Phase(nc, "bwd3") as ph:
        bank = ph.banks()
        st, own, inv = ph.two("st", [P, G, W3]), ph.two("own", [P, G, D]), ph.two("inv", [P, G])
        mean, meanT, Y, out = (ph.two(n, [P, G, D]) for n in ("mean", "meanT", "Y", "out"))
        stats, mv, sd, rs = ph.two("stats", [P, G, 6]), ph.two("mv", [P, G, 2]), ph.two("sd", [P, G]), ph.two("rs", [P, G])
        end_idx, warm = ph.two("end_idx", [P, G], I32), ph.sb("warm", [P, 1])
        loaded, scattered = ph.sem2("loaded"), ph.sem2("scattered")
        inv_done, mean_done, meanT_done, meanT_copied, node_done, Y_done, stat_done, aggr_done, sd_done, rs_done, out_done, end_ready = (ph.sem(n) for n in (
            "inv_done", "mean_done", "meanT_done", "meanT_copied", "node_done", "Y_done", "stat_done", "aggr_done", "sd_done", "rs_done", "out_done", "end_ready"))
        with nc.Block() as block:
            @block.sync
            def _(sp):
                start_counts(sp, dmas=loaded, n=2)

                def load(i, g):
                    t, freed = now(sp, i * (2 * G) + g * G), now(sp, at2(i, g, back=2))
                    sp.wait_ge(mean_done, freed)
                    sp.wait_ge(Y_done, freed)
                    sp.dma_start(st[g][:], s.state3[:, bass.ds(t, G), :]).then_inc(loaded[g], 16)
                    sp.dma_start(own[g][:], s.dst3[:, bass.ds(t, G), :]).then_inc(loaded[g], 16)

                in_rounds(sp, iters, (load, 0))

            @block.gpsimd
            def _(pool):
                limit = pool.to_reg(s.N - 1)
                start_counts(pool, [end_ready])
                first_dma(pool, s, ph, scattered)

                def scatter(i, g):
                    t, freed, group = (now(pool, v) for v in (i * (2 * G) + g * G, scattered_at(i, G, back=1), at2(i, g)))
                    pool.wait_ge(scattered[g], freed)
                    pool.tensor_copy(end_idx[g][:], s.end_idx[:, bass.ds(t, G)]).then_inc(end_ready, 1)
                    pool.wait_ge(end_ready, 3)
                    pool.wait_ge(end_ready, group)
                    pool.wait_ge(out_done, group)
                    for k in range(G):
                        pool.indirect_dma_start(s.out, bass.IndirectOffsetOnAxis(ap=end_idx[g][:, k:k + 1], axis=0), out[g][:, k, :], None,
                                                bounds_check=limit, oob_is_err=False).then_inc(scattered[g], 16)

                in_rounds(pool, iters, (scatter, 0))
                for g in range(2):
                    pool.wait_ge(scattered[g], scattered_at(iters - 1, G))

            @block.tensor
            def _(pe):
                start_counts(pe, [meanT_done, node_done])

                def turn(i, g):
                    pe.wait_ge(mean_done, at2(i, g))
                    pe.wait_ge(meanT_copied, at2(i, g, back=2))
                    for k in range(G):
                        ins = pe.transpose(bank[g][:, k * D:(k + 1) * D], mean[g][:, k, :], s.ident[:])
                    ins.then_inc(meanT_done, 1)

                def node_rows(i, g):
                    pe.wait_ge(meanT_copied, at2(i, g))
                    pe.wait_ge(Y_done, at2(i, g, back=2))
                    for k in range(G):
                        pe.matmul(bank[2 + g][:, k * D:(k + 1) * D], meanT[g][:, k, :], s.WnT[:], start=True, stop=False)
                        ins = pe.matmul(bank[2 + g][:, k * D:(k + 1) * D], s.ones3[:], s.bn_parts[:], start=False, stop=True)
                    ins.then_inc(node_done, 1)

                in_rounds(pe, iters, (node_rows, 0), (turn, 1))

            @block.scalar
            def _(act):
                start_counts(act, [mean_done, meanT_copied, sd_done])
                act.activation(warm[:], s.eps[:], ACT.Sqrt)

                def means(i, g):
                    act.wait_ge(inv_done, at2(i, g))
                    act.wait_ge(meanT_done, at2(i, g, back=2))
                    for k in range(G):
                        ins = act.activation(mean[g][:, k, :], st[g][:, k, 0:D], ACT.Copy, scale=inv[g][:, k:k + 1])
                    ins.then_inc(mean_done, 1)

                def copy_turned(i, g):
                    act.wait_ge(meanT_done, at2(i, g))
                    act.wait_ge(node_done, at2(i, g, back=2))
                    act.activation(meanT[g][:], rows4(bank[g]), ACT.Copy).then_inc(meanT_copied, 1)

                def root_of_variance(i, g):
                    act.wait_ge(aggr_done, at2(i, g))
                    act.wait_ge(rs_done, at2(i, g, back=2))
                    act.activation(sd[g][:], mv[g][:, :, 1], ACT.Sqrt, bias=s.eps[:]).then_inc(sd_done, 1)

                in_rounds(act, iters, (means, 1), (copy_turned, 1), (root_of_variance, 0))

            @block.vector
            def _(dve):
                start_counts(dve, [inv_done, Y_done, stat_done, aggr_done, rs_done, out_done])

                def inverses(i, g):
                    dve.wait_ge(loaded[g], landed(i, 2))
                    dve.wait_ge(mean_done, at2(i, g, back=2))
                    dve.reciprocal(inv[g][:], st[g][:, :, D]).then_inc(inv_done, 1)

                def rows(i, g):
                    dve.wait_ge(node_done, at2(i, g))
                    dve.scalar_tensor_tensor(Y[g][:], rows4(bank[2 + g]), 0.0, own[g][:], ALU.max, ALU.add).then_inc(Y_done, 1)
                    dve.wait_ge(Y_done, at2(i, g))
                    dve.wait_ge(sd_done, at2(i, g, back=2))
                    rowstats(dve, Y[g], stats[g], mv[g], stat_done, aggr_done, i, g)

                def normalise(i, g):
                    dve.wait_ge(scattered[g], scattered_at(i, G, back=1))
                    norm_rows(dve, sd_done, Y[g], out[g], mv[g], sd[g], rs[g], rs_done, out_done, i, g)

                in_rounds(dve, iters, (inverses, 1), (normalise, -1), (rows, 0))


def build(nc, a, out):
    N, T = a["x"].shape[0], a["src2"].shape[1]
    s = Kept()
    s.N, s.T, s.block = N, T, P * R
    s.blocks = -(-N // (2 * s.block)) * 2
    assert T % (2 * G) == 0 and N > (s.blocks - 1) * s.block
    s.agg_rows = N + 3 * P
    s.zrows = 64 if N > 64 * P else 4
    s.zchunks = s.agg_rows // (P * s.zrows)
    rest = s.agg_rows - s.zchunks * P * s.zrows
    s.zrest = next((r for r in range(s.zrows, 0, -1) if rest % r == 0 and rest // r <= P), 1)

    def table(name, shape):
        return nc.dram_tensor(name, shape, F32, kind="Internal").ap()

    s.x1, s.x2, s.x3 = (table(f"x{j}", (N, D)) for j in (1, 2, 3))
    s.agg1 = table("agg1", (s.agg_rows, D))
    s.state0, s.state2, s.state3 = table("state0", (P, T, W0)), table("state2", (P, T, W2)), table("state3", (P, T, W3))
    s.root0, s.own2, s.dst3 = table("root0", (P, T, D)), table("own2", (P, T, D)), table("dst3", (P, T, D))
    s.out = out
    with ExitStack() as c:
        def sb(names, shape, dt=F32):
            return [c.enter_context(nc.sbuf_tensor(n, shape, dt)) for n in names.split()]

        s.ident, s.lower, s.Wq, s.Wk, s.Wv, s.WrI, s.W2, s.Wl, s.WnT = sb("ident lower Wq Wk Wv WrI W2 Wl WnT", [P, D])
        s.br_all, s.bt_all, s.bn_all, s.rbn_all = sb("br_all bt_all bn_all rbn_all", [P, D])
        s.tail_tail, s.tail_head, s.head_tail, s.head_head = sb("tail_tail tail_head head_tail head_head", [P, P])
        s.far_tt, s.far_th, s.far_ht, s.far_hh = sb("far_tt far_th far_ht far_hh", [P, P])
        s.brv_parts, s.b2_parts, s.bl_parts, s.bn_parts, s.ones3 = sb("brv_parts b2_parts bl_parts bn_parts ones3", [3, D], BF16)
        s.bq, s.bk, s.b1, s.eps, s.trash = sb("bq bk b1 eps trash", [P, 1])
        [s.W1], [s.WeT], [s.Wz] = sb("W1", [RBF, D]), sb("WeT", [P, 2, D]), sb("Wz", [P, H, D])
        s.headsel, s.att_s, s.att_d = sb("headsel att_s att_d", [P, H])
        s.src_f, s.dst_f, s.same, s.cut, s.to_trash = sb("src_f dst_f same cut to_trash", [P, T])
        [s.inner], [s.end_idx], [s.gather_idx] = sb("inner", [P, T], U32), sb("end_idx", [P, T], I32), sb("gather_idx", [P, 2 * T], I32)
        [s.head_row], [s.zeros] = sb("head_row", [P, 1], I32), sb("zeros", [P, s.zrows * D])
        setup_phase(nc, s, a)
        dense0_phase(nc, s, a)
        forward_attention_phase(nc, s, a, 0)
        patch_phase(nc, s, s.state0, W0, C + 1)
        backward0_phase(nc, s, a)
        dense1_phase(nc, s, a)
        forward_attention_phase(nc, s, a, 2)
        patch_phase(nc, s, s.state2, W2, D + 1)
        backward2_phase(nc, s, a)
        forward3_phase(nc, s, a)
        patch_phase(nc, s, s.state3, W3, 0)
        backward3_phase(nc, s, a)


def laid_out(inputs):
    g = {k: np.asarray(v) for k, v in inputs.items()}
    N, E = g["x"].shape[0], g["src"].shape[0]
    T = steps_of(E)
    pad = P * T - E

    def per_partition(v, fill):
        return np.concatenate([v, np.full(P * T - v.shape[0], fill, v.dtype)]).reshape(P, T)

    flip = np.ascontiguousarray
    src2 = per_partition(g["src"], N + 2 * P)
    out = {
        "x": g["x"],
        "src2": src2, "dst2": per_partition(g["dst"], N), "next_dst2": per_partition(g["dst"][1:], N + 1),
        "src_steps": flip(src2.T),
        "edge_steps": flip(np.concatenate([g["edge_attr_64"], np.zeros((pad, RBF), g["edge_attr_64"].dtype)]).reshape(P, T, RBF).transpose(2, 1, 0)),
        "Wq": g["L0_gnn_Wq"], "Wk": g["L0_gnn_Wk"], "Wv": g["L0_gnn_Wv"], "Wr": g["L0_gnn_Wr"],
        "bq": g["L0_gnn_bq"], "bk": g["L0_gnn_bk"], "bv": g["L0_gnn_bv"], "br": g["L0_gnn_br"],
        "W1": g["L1_gnn_W1"], "b1": g["L1_gnn_b1"], "W2": g["L1_gnn_W2"], "b2": g["L1_gnn_b2"], "Wl": g["L1_gnn_Wl"], "bl": g["L1_gnn_bl"],
        "WfcT": flip(g["L2_gnn_W_fc"].T), "Wtr": g["L2_gnn_W_trans"], "bt": g["L2_gnn_b_trans"],
        "att2": flip(np.stack([g["L2_gnn_att_ns"][0].T, g["L2_gnn_att_nd"][0].T], axis=2)),
        "WeT": flip(g["L3_gnn_W_edge"].T), "WnT": flip(g["L3_gnn_W_node"].T), "bn": g["L3_gnn_b_node"],
        "c_ident": np.eye(P, dtype=np.float32), "c_lower": np.tri(P, k=-1, dtype=np.float32),
        "c_headsel": flip(np.repeat(np.eye(H, dtype=np.float32), C, axis=0) / np.float32(np.sqrt(C))),
        "c_trash": np.arange(N, N + P, dtype=np.float32).reshape(P, 1),
    }
    return out


def kernel(**inputs):
    import concourse.bacc as bacc
    from concourse.bass_utils import run_bass_kernel_spmd

    arrays = laid_out(inputs)
    nc = bacc.Bacc("TRN2", target_bir_lowering=False, num_devices=1)
    a = {name: nc.dram_tensor(f"in_{name}", v.shape, mybir.dt.from_np(v.dtype), kind="ExternalInput").ap() for name, v in arrays.items()}
    out = nc.dram_tensor("out", inputs["x"].shape, F32, kind="ExternalOutput").ap()
    build(nc, a, out)
    r = run_bass_kernel_spmd(nc, [{f"in_{name}": v for name, v in arrays.items()}], core_ids=[0])
    return r.results[0]["out"]
```

```python
from contextlib import ExitStack

import numpy as np
import concourse.bass as bass
import concourse.mybir as mybir

P = 128
D = 128
H = 4
C = D // H
RBF = 64
G = 4
R = 8
VR = 1
W0 = H * (C + 1) + H
W2 = H * (D + 1) + H
W3 = D + 1
FAR = 1.0e30
SKIP = float(1 << 22)
EPS = 1e-5

F32 = mybir.dt.float32
BF16 = mybir.dt.bfloat16
I32 = mybir.dt.int32
U32 = mybir.dt.uint32
ALU = mybir.AluOpType
ACT = mybir.ActivationFunctionType
X = mybir.AxisListType.X


def steps_of(edges):
    return -(-edges // (P * 2 * G)) * 2 * G


def at2(i, g, back=0):
    return 2 * i + (g + 3 - back)


def at8(i, k, back=0):
    return 8 * i + (k + 9 - back)


def at4(i, k, back=0):
    return 4 * i + (k + 5 - back)


def landed(i, n=1, back=0):
    return (16 * n) * i + (16 * n) * (2 - back)


def start_counts(eng, groups=(), steps=(), quarters=(), dmas=(), n=1):
    for s in quarters:
        eng.sem_inc(s, 4)
    for s in groups:
        eng.sem_inc(s, 2)
    for s in steps:
        eng.sem_inc(s, 8)
    for s in dmas:
        eng.sem_inc(s, 16 * n)


def scattered_at(i, n, back=0):
    return (16 * n) * i + (16 * n * (1 - back) + 16)


def first_dma(pool, s, ph, sems):
    for n, sem in enumerate(sems):
        pool.dma_start(ph.sb(f"first{n}", [P, 1])[:], s.eps[:]).then_inc(sem, 16)


def in_rounds(eng, iters, *stages, apart=0):
    lead, lag = max(o for _, o in stages), max(-o for _, o in stages)
    first, last = (lag + 1) // 2, iters - (lead + apart + 1) // 2
    last = max(first, last)

    def one(i, r):
        for stage, o in stages:
            g = (r + o) % 2
            di = (r + o - g) // 2
            if not isinstance(i, int) or 0 <= i + di < iters:
                stage(i + di if di else i, g)

    for n in range(-lead, 2 * first):
        one(n // 2, n % 2)
    if first < last:
        with eng.Fori(first, last) as i:
            one(i, 0)
            one(i, 1)
    for n in range(2 * last, 2 * iters + lag):
        one(n // 2, n % 2)


def now(eng, value):
    return value if isinstance(value, int) else eng.snap(eng.to_reg(value))


class Kept:
    pass


class Phase:

    def __init__(self, nc, name):
        self.nc, self.name, self.ctx, self.sems = nc, name, ExitStack(), []

    def __enter__(self):
        return self

    def __exit__(self, *a):
        self.nc.clear_and_free_semaphores(self.sems)
        self.nc.all_engine_barrier()
        self.ctx.close()

    def sb(self, name, shape, dt=F32):
        return self.ctx.enter_context(self.nc.sbuf_tensor(f"{self.name}_{name}", shape, dt))

    def two(self, name, shape, dt=F32):
        return [self.sb(f"{name}{g}", shape, dt) for g in range(2)]

    def banks(self):
        return [self.ctx.enter_context(self.nc.psum_tensor(f"{self.name}_bank{j}", [P, G * D], F32)) for j in range(8)]

    def sem(self, name):
        self.sems.append(self.nc.alloc_semaphore(f"{self.name}_{name}"))
        return self.sems[-1]

    def sem2(self, name):
        return [self.sem(f"{name}{g}") for g in range(2)]


def rows4(bank):
    return bank[:].rearrange("p (k d) -> p k d", k=G)


def setup_phase(nc, s, a):
    T, N = s.T, s.N
    with Phase(nc, "setup") as ph:
        loaded, made, mult, moved, calc = (ph.sem(n) for n in ("loaded", "made", "multiplied", "moved", "calc"))
        src_i, dst_i, nxt_i = (ph.sb(n, [P, T], I32) for n in ("src_i", "dst_i", "nxt_i"))
        nxt_f, t0 = ph.sb("nxt_f", [P, T]), ph.sb("t0", [P, T])
        wfcT = ph.sb("wfcT", [P, H, D])
        wtr = ph.sb("wtr", [P, H, D + 2])
        bias3, left, chosen = (ph.sb(n, [3, 5, D]) for n in ("bias3", "left", "chosen"))
        part16 = ph.sb("part16", [3, 5, D], BF16)
        cnt = ph.sb("cnt", [P, 1])
        bank = ph.banks()
        flagged = []
        loads = [
            (src_i[:], a["src2"]), (dst_i[:], a["dst2"]), (nxt_i[:], a["next_dst2"]),
            (s.ident[:], a["c_ident"]), (s.lower[:], a["c_lower"]), (s.headsel[:], a["c_headsel"]), (s.trash[:], a["c_trash"]),
            (s.Wq[:], a["Wq"]), (s.Wk[:], a["Wk"]), (s.Wv[:], a["Wv"]), (s.WrI[:], a["Wr"]),
            (s.W1[:], a["W1"]), (s.W2[:], a["W2"]), (s.Wl[:], a["Wl"]),
            (s.WeT[:], a["WeT"].rearrange("(h p) d -> p h d", p=P)), (s.WnT[:], a["WnT"]),
            (wfcT[:], a["WfcT"].rearrange("(h p) d -> p h d", p=P)),
            (wtr[:, :, 0:D], a["Wtr"].rearrange("(h p) d -> p h d", p=P)),
            (wtr[:, :, D:D + 2], a["att2"]),
            (s.bq[:], a["bq"].rearrange("(p a) -> p a", a=1)), (s.bk[:], a["bk"].rearrange("(p a) -> p a", a=1)),
            (s.b1[:], a["b1"].rearrange("(p a) -> p a", a=1)),
            *((bias3[:, j, :], a[n].rearrange("(a n) -> a n", a=1).to_broadcast([3, D])) for j, n in enumerate(("br", "b2", "bl", "bn", "bv"))),
            (s.br_all[:], a["br"].rearrange("(a n) -> a n", a=1).to_broadcast([P, D])),
            (s.bt_all[:], a["bt"].rearrange("(a n) -> a n", a=1).to_broadcast([P, D])),
            (s.bn_all[:], a["bn"].rearrange("(a n) -> a n", a=1).to_broadcast([P, D])),
        ]
        with nc.Block() as block:
            @block.sync
            def _(sp):
                for out, in_ in loads:
                    sp.dma_start(out, in_, allow_slow_non_contiguous=True).then_inc(loaded, 16)

            @block.gpsimd
            def _(pool):
                pool.memset(s.ones3[:], 1.0).then_inc(made, 1)
                pool.memset(s.eps[:], EPS).then_inc(made, 1)
                pool.memset(s.zeros[:], 0.0).then_inc(made, 1)

            @block.vector
            def _(dve):
                n = [0]

                def done(ins):
                    n[0] += 1
                    ins.then_inc(calc, 1)
                    dve.wait_ge(calc, n[0])

                dve.wait_ge(loaded, 16 * len(loads))
                done(dve.tensor_tensor(s.WrI[:], s.WrI[:], s.ident[:], ALU.add))
                done(dve.tensor_tensor(bias3[:, 0, :], bias3[:, 0, :], bias3[:, 4, :], ALU.add))
                done(dve.tensor_copy(left[:], bias3[:]))
                done(dve.memset(chosen[:], 0.0))
                for part in range(3):
                    done(dve.tensor_copy(part16[:], left[:]))
                    done(dve.scalar_tensor_tensor(chosen[:], part16[:], s.ident[0:3, part:part + 1], chosen[:], ALU.mult, ALU.add))
                    done(dve.tensor_tensor(left[:], left[:], part16[:], ALU.subtract))
                for j, parts in enumerate((s.brv_parts, s.b2_parts, s.bl_parts, s.bn_parts)):
                    done(dve.tensor_copy(parts[:], chosen[:, j, :]))
                done(dve.tensor_scalar(s.rbn_all[:], s.bn_all[:], 0.0, None, ALU.max))
                done(dve.tensor_copy(s.src_f[:], src_i[:]))
                done(dve.tensor_copy(s.dst_f[:], dst_i[:]))
                flagged.append(n[0])
                done(dve.tensor_copy(nxt_f[:], nxt_i[:]))
                done(dve.memset(s.same[:], 0.0))
                done(dve.tensor_tensor(s.same[:, 1:T], s.dst_f[:, 1:T], s.dst_f[:, 0:T - 1], ALU.is_equal))
                done(dve.tensor_scalar(s.cut[:], s.same[:], -1.0, FAR, ALU.add, ALU.mult))
                done(dve.tensor_tensor(t0[:], nxt_f[:], s.dst_f[:], ALU.is_equal))
                done(dve.tensor_copy(s.inner[:], t0[:]))
                done(dve.memset(s.inner[:, T - 1:T], 0))
                done(dve.scalar_tensor_tensor(t0[:], t0[:], SKIP, s.dst_f[:], ALU.mult, ALU.add))
                done(dve.tensor_copy(s.end_idx[:], t0[:]))
                ga = s.gather_idx[:].rearrange("p (n two k) -> p n two k", two=2, k=G)
                done(dve.tensor_scalar(t0[:], s.src_f[:], float(N - 1), None, ALU.min))
                done(dve.tensor_copy(ga[:, :, 0, :], t0[:].rearrange("p (n k) -> p n k", k=G)))
                done(dve.tensor_scalar(t0[:], s.dst_f[:], float(N - 1), None, ALU.min))
                done(dve.tensor_copy(ga[:, :, 1, :], t0[:].rearrange("p (n k) -> p n k", k=G)))
                done(dve.tensor_scalar(s.to_trash[:], s.src_f[:], s.trash[:], -1.0, ALU.subtract, ALU.mult))
                done(dve.tensor_scalar(s.to_trash[:, 1::2], s.to_trash[:, 1::2], float(P), None, ALU.add))
                head, tail = s.dst_f[:, 0:1], s.dst_f[:, T - 1:T]
                done(dve.tensor_scalar(t0[:], s.dst_f[:], head, None, ALU.is_equal))
                done(dve.tensor_reduce(cnt[:], t0[:], X, ALU.add))
                done(dve.tensor_scalar(t0[:, 0:1], s.trash[:], -float(N), float(T), ALU.add, ALU.mult))
                done(dve.scalar_tensor_tensor(t0[:, 1:2], cnt[:], -1.0, t0[:, 0:1], ALU.add, ALU.add))
                done(dve.tensor_copy(s.head_row[:], t0[:, 1:2]))
                dve.wait_ge(mult, 1)
                rowT, rowH = bank[0][:, 0:P], bank[0][:, P:2 * P]
                done(dve.tensor_scalar(s.tail_tail[:], rowT, tail, None, ALU.is_equal))
                done(dve.tensor_scalar(s.tail_head[:], rowH, tail, None, ALU.is_equal))
                done(dve.tensor_scalar(s.head_tail[:], rowT, head, None, ALU.is_equal))
                done(dve.tensor_scalar(s.head_head[:], rowH, head, None, ALU.is_equal))
                for far, m in ((s.far_tt, s.tail_tail), (s.far_th, s.tail_head), (s.far_ht, s.head_tail), (s.far_hh, s.head_head)):
                    done(dve.tensor_scalar(far[:], m[:], -1.0, FAR, ALU.add, ALU.mult))
                done(dve.tensor_tensor(t0[:, 0:1], head, tail, ALU.not_equal))
                done(dve.tensor_scalar(s.head_tail[:], s.head_tail[:], t0[:, 0:1], None, ALU.mult))
                done(dve.tensor_scalar(s.head_head[:], s.head_head[:], t0[:, 0:1], None, ALU.mult))
                for h in range(H):
                    dve.wait_ge(mult, 2 + h)
                    done(dve.tensor_copy(s.Wz[:, h, :], bank[1 + h][:, 0:D]))
                    done(dve.tensor_copy(s.att_s[:, h:h + 1], bank[1 + h][:, D:D + 1]))
                    done(dve.tensor_copy(s.att_d[:, h:h + 1], bank[1 + h][:, D + 1:D + 2]))
                dve.wait_ge(made, 3)

            @block.tensor
            def _(pe):
                pe.wait_ge(loaded, 16 * len(loads))
                pe.wait_ge(calc, flagged[0])
                pe.transpose(bank[0][:, 0:P], s.dst_f[:, T - 1:T].to_broadcast([P, P]), s.ident[:])
                pe.transpose(bank[0][:, P:2 * P], s.dst_f[:, 0:1].to_broadcast([P, P]), s.ident[:]).then_inc(mult, 1)
                for h in range(H):
                    pe.matmul(bank[1 + h][:, 0:D + 2], wfcT[:, h, :], wtr[:, h, :], start=True, stop=True).then_inc(mult, 1)


def rowstats(dve, Y, stats, mv, stat_done, aggr_done, i, g):
    for k in range(Y.shape[1]):
        ins = dve.bn_stats(stats[:, k, :], Y[:, k, :])
    ins.then_inc(stat_done, 1)
    four = now(dve, at2(i, g))
    dve.wait_ge(stat_done, 2)
    dve.wait_ge(stat_done, four)
    for k in range(Y.shape[1]):
        ins = dve.bn_aggr(mv[:, k, :], stats[:, k, :])
    ins.then_inc(aggr_done, 1)


def dense_row(s, i, g):
    if isinstance(i, int) and (i, g) == (s.blocks // 2 - 1, 1):
        return s.N - s.block
    return (2 * s.block) * i + s.block * g


def of_block(table, row, s):
    return table[bass.ds(row, s.block), :].rearrange("(p k) d -> p k d", k=R)


def store_block(sp, s, table, rows, ready, stored, i, g):
    row, done = now(sp, dense_row(s, i, g)), now(sp, at2(i, g))
    for sem in ready:
        sp.wait_ge(sem, done)
    if isinstance(i, int) and (i, g) == (s.blocks // 2 - 1, 1):
        sp.wait_ge(stored[0], landed(i))
    sp.dma_start(of_block(table, row, s), rows[g][:]).then_inc(stored[g], 16)


def scales(dve, mv, sd, rs, nb, sd_done, rs_done, nb_done, i, g):
    dve.wait_ge(sd_done, at2(i, g))
    dve.wait_ge(nb_done, at2(i, g, back=2))
    dve.reciprocal(rs[:], sd[:]).then_inc(rs_done, 1)
    dve.wait_ge(rs_done, at2(i, g))
    dve.scalar_tensor_tensor(nb[:], mv[:, :, 0], -1.0, rs[:], ALU.mult, ALU.mult).then_inc(nb_done, 1)


def scale_rows(act, Y, out, rs, nb, nb_done, out_done, i, g, rows):
    act.wait_ge(nb_done, at2(i, g))
    for k in range(rows):
        ins = act.activation(out[:, k, :], Y[:, k, :], ACT.Identity, scale=rs[:, k:k + 1], bias=nb[:, k:k + 1])
    ins.then_inc(out_done, 1)


def forward_attention_phase(nc, s, a, layer):
    first = layer == 0
    T, iters = s.T, s.T // (2 * G)
    W, hw, table, rows_out, x_src = (W0, C + 1, s.state0, s.root0, a["x"]) if first else (W2, D + 1, s.state2, s.own2, s.x2)
    A = H * hw
    with Phase(nc, f"fwd{layer}") as ph:
        bank = ph.banks()
        value_bank, root_bank, score_bank = (bank[2], bank[3]), bank[4], bank[5 if first else 6]
        xs, xd, xsT, xdT = (ph.two(n, [P, G, D]) for n in ("xs", "xd", "xsT", "xdT"))
        idx, cut4, warm = ph.two("idx", [P, 2 * G], I32), ph.two("cut4", [P, G]), ph.sb("warm", [P, 1])
        st = ph.two("st", [P, G, W])
        mh = ph.two("mh", [P, G + 1, H])
        diff = ph.two("diff", [P, G, 2, H])
        wt = ph.two("wt", [P, G, 2, A])
        dec = ph.two("dec", [P, A])
        if first:
            qT, prod, root = (ph.two(n, [P, G, D]) for n in ("qT", "prod", "root"))
            x_in, Y, x1, node_xT = *(ph.two(n, [P, R, D]) for n in ("x_in", "Y", "x1")), ph.two("node_xT", [P, G, D])
            stats, mv = ph.two("stats", [P, R, 6]), ph.two("mv", [P, R, 2])
            log_var, rs, nb = (ph.two(n, [P, R]) for n in ("log_var", "rs", "nb"))
            x_loaded, x1_stored, zeroed = ph.sem2("x_loaded"), ph.sem2("x1_stored"), ph.sem2("zeroed")
            node_transposed, node_xT_copied, node_product, node_added, stat_done, aggr_done, log_done, rs_done, nb_done, x1_done, trash_zeroed = (ph.sem(n) for n in (
                "node_transposed", "node_xT_copied", "node_product", "node_added", "stat_done", "aggr_done", "log_done", "rs_done", "nb_done", "x1_done", "trash_zeroed"))
        else:
            sc, leak = ph.two("sc", [P, G, H]), ph.two("leak", [P, G, H])
        idx_ready, gathered, st_stored, row_stored = ph.sem("idx_ready"), ph.sem2("gathered"), ph.sem2("st_stored"), ph.sem2("row_stored")
        names = (
            "transposed", "xT_copied", "qk_done", "qT_copied", "prod_done", "values_done", "scores_done", "root_copied",
            "sc_copied", "leak_done", "mh_done", "diff_m", "diff_done", "exp_done", "weighted", "m_stored")
        (transposed, xT_copied, qk_done, qT_copied, prod_done, values_done, scores_done, root_copied,
         sc_copied, leak_done, mh_done, diff_m, diff_done, exp_done, weighted, m_stored) = (ph.sem(n) for n in names)
        max_done, scaled, decayed, acc_done, cut_ready, cleared = (ph.sem(n) for n in ("max_done", "scaled", "decayed", "acc_done", "cut_ready", "cleared"))
        score = [v[:] for v in sc] if not first else [score_bank[:, 0:G * H].rearrange("p (k h) -> p k h", k=G)] * 2

        def store_state(eng, i, g):
            t, group, step = (now(eng, v) for v in (i * (2 * G) + g * G, at2(i, g), at8(i, g * G + 3)))
            eng.wait_ge(m_stored, group)
            eng.wait_ge(acc_done, step)
            eng.dma_start(table[:, bass.ds(t, G), :], st[g][:]).then_inc(st_stored[g], 16)

        with nc.Block() as block:
            @block.gpsimd
            def _(pool):
                limit = pool.to_reg(s.N - 1)
                with pool.Fori(0, iters) as i:
                    for g in range(2):
                        column, freed, stored, ready = (now(pool, v) for v in (i * (4 * G) + g * 2 * G, at2(i, g, back=2), landed(i, back=1), 2 * i + (g + 1)))
                        pool.wait_ge(transposed, freed)
                        pool.tensor_copy(idx[g][:], s.gather_idx[:, bass.ds(column, 2 * G)]).then_inc(idx_ready, 1)
                        pool.wait_ge(idx_ready, 1)
                        pool.wait_ge(idx_ready, ready)
                        if not first:
                            pool.wait_ge(row_stored[g], stored)
                        for k in range(G):
                            pool.indirect_dma_start(xs[g][:, k, :], None, x_src, bass.IndirectOffsetOnAxis(ap=idx[g][:, k:k + 1], axis=0),
                                                    bounds_check=limit, oob_is_err=False).then_inc(gathered[g], 16)
                            pool.indirect_dma_start(xd[g][:, k, :], None, x_src, bass.IndirectOffsetOnAxis(ap=idx[g][:, G + k:G + k + 1], axis=0),
                                                    bounds_check=limit, oob_is_err=False).then_inc(gathered[g], 16)

            @block.tensor
            def _(pe):
                start_counts(pe, [transposed, qk_done, scores_done] + [values_done] * first, [values_done] * (not first))

                def turn(i, g):
                    pe.wait_ge(gathered[g], 16 * 2 * G * i + 16 * 2 * G)
                    pe.wait_ge(xT_copied, at2(i, g, back=1))
                    if first:
                        pe.wait_ge(qT_copied, at2(i, g, back=1))
                        pe.wait_ge(prod_done, at2(i, g, back=1))
                    for k in range(G):
                        pe.transpose(bank[0][:, k * D:(k + 1) * D], xs[g][:, k, :], s.ident[:])
                    for k in range(G):
                        ins = pe.transpose(bank[1][:, k * D:(k + 1) * D], xd[g][:, k, :], s.ident[:])
                    ins.then_inc(transposed, 1)

                def project(i, g):
                    pe.wait_ge(xT_copied, at2(i, g))
                    pe.matmul(bank[0][:], s.Wq[:], xdT[g][:], start=True, stop=True)
                    pe.matmul(bank[1][:], s.Wk[:], xsT[g][:], start=True, stop=True).then_inc(qk_done, 1)
                    pe.wait_ge(weighted, at2(i, g, back=2))
                    for k in range(G):
                        ins = pe.matmul(value_bank[g][:, k * D:(k + 1) * D], xsT[g][:, k, :], s.Wv[:], start=True, stop=True)
                    pe.wait_ge(root_copied, at2(i, g, back=1))
                    for k in range(G):
                        pe.matmul(root_bank[:, k * D:(k + 1) * D], xdT[g][:, k, :], s.WrI[:], start=True, stop=False)
                        ins = pe.matmul(root_bank[:, k * D:(k + 1) * D], s.ones3[:], s.brv_parts[:], start=False, stop=True)
                    ins.then_inc(values_done, 1)

                def node_turn(half):
                    def work(i, g):
                        pe.wait_ge(x_loaded[g], landed(i))
                        pe.wait_ge(node_xT_copied, at4(i, 2 * g + half, back=1))
                        for k in range(G):
                            ins = pe.transpose(bank[6][:, k * D:(k + 1) * D], x_in[g][:, half * G + k, :], s.ident[:])
                        ins.then_inc(node_transposed, 1)
                    return work

                def node_multiply(half):
                    def work(i, g):
                        pe.wait_ge(node_xT_copied, at4(i, 2 * g + half))
                        pe.wait_ge(node_added, at4(i, 2 * g + half, back=1))
                        for k in range(G):
                            ins = pe.matmul(bank[7][:, k * D:(k + 1) * D], node_xT[half][:, k, :], s.WrI[:], start=True, stop=True)
                        ins.then_inc(node_product, 1)
                    return work

                def score_products(i, g):
                    pe.wait_ge(prod_done, at2(i, g))
                    pe.wait_ge(diff_m, at2(i, g, back=1))
                    for k in range(G):
                        ins = pe.matmul(score_bank[:, k * H:(k + 1) * H], prod[g][:, k, :], s.headsel[:], start=True, stop=True)
                    ins.then_inc(scores_done, 1)

                def score_rows(i, g):
                    pe.wait_ge(xT_copied, at2(i, g))
                    pe.wait_ge(sc_copied, at2(i, g, back=1))
                    for k in range(G):
                        pe.matmul(score_bank[:, k * H:(k + 1) * H], xsT[g][:, k, :], s.att_s[:], start=True, stop=False)
                        ins = pe.matmul(score_bank[:, k * H:(k + 1) * H], xdT[g][:, k, :], s.att_d[:], start=False, stop=True)
                    ins.then_inc(scores_done, 1)

                def values(i, g):
                    for k in range(G):
                        pe.wait_ge(scaled, at8(i, g * G + k, back=4))
                        pe.matmul(bank[2 + k][:], xsT[g][:, k, :], s.Wz[:], start=True, stop=True).then_inc(values_done, 1)

                if first:
                    start_counts(pe, quarters=[node_transposed, node_product])
                    in_rounds(pe, iters, (node_multiply(0), 0), (node_turn(1), 0), (project, 0), (node_multiply(1), 0), (node_turn(0), 1), (turn, 1), (score_products, 0))
                else:
                    in_rounds(pe, iters, (score_rows, 0), (turn, 1), (values, 0))

            @block.scalar
            def _(act):
                start_counts(act, [xT_copied, qT_copied, root_copied, exp_done], [scaled])
                act.activation(warm[:], s.eps[:], ACT.Ln if first else ACT.Exp)

                def copy_rows(i, g):
                    act.wait_ge(transposed, at2(i, g))
                    if first:
                        act.wait_ge(values_done, at2(i, g, back=2))
                    else:
                        act.wait_ge(values_done, at8(i, g * G + 3, back=8))
                    act.activation(xsT[g][:], rows4(bank[0]), ACT.Copy)
                    act.activation(xdT[g][:], rows4(bank[1]), ACT.Copy).then_inc(xT_copied, 1)

                def queries(i, g):
                    act.wait_ge(qk_done, at2(i, g))
                    act.wait_ge(prod_done, at2(i, g, back=2))
                    act.activation(qT[g][:], rows4(bank[0]), ACT.Identity, bias=s.bq[:]).then_inc(qT_copied, 1)

                def roots(i, g):
                    act.wait_ge(values_done, at2(i, g))
                    act.wait_ge(row_stored[g], landed(i, back=1))
                    act.activation(root[g][:], rows4(root_bank), ACT.Copy).then_inc(root_copied, 1)

                def weights(i, g):
                    act.wait_ge(diff_done, at2(i, g))
                    act.wait_ge(acc_done, at8(i, g * G + 3, back=8))
                    act.activation(wt[g][:].rearrange("p k two (h w) -> p (k two) h w", h=H)[:, :, :, hw - 1],
                                   diff[g][:].rearrange("p k two h -> p (k two) h"), ACT.Exp).then_inc(exp_done, 1)

                def node_copy(half):
                    def work(i, g):
                        act.wait_ge(node_transposed, at4(i, 2 * g + half))
                        act.wait_ge(node_product, at4(i, 2 * g + half, back=2))
                        act.activation(node_xT[half][:], rows4(bank[6]), ACT.Copy).then_inc(node_xT_copied, 1)
                    return work

                def node_scale(i, g):
                    act.wait_ge(aggr_done, at2(i, g))
                    act.wait_ge(rs_done, at2(i, g, back=2))
                    act.activation(log_var[g][:], mv[g][:, :, 1], ACT.Ln, bias=s.eps[:]).then_inc(log_done, 1)
                    act.wait_ge(log_done, at2(i, g))
                    act.wait_ge(x1_done, at2(i, g, back=2))
                    act.activation(rs[g][:], log_var[g][:], ACT.Exp, scale=-0.5).then_inc(rs_done, 1)

                def node_normalise(i, g):
                    act.wait_ge(x1_stored[g], landed(i, back=1))
                    scale_rows(act, Y[g], x1[g], rs[g], nb[g], nb_done, x1_done, i, g, rows=R)

                def weigh(i, g):
                    weights(i, g)
                    act.wait_ge(exp_done, at2(i, g))
                    for k in range(G):
                        act.wait_ge(values_done, at8(i, g * G + k))
                        for h in range(H):
                            ins = act.activation(wt[g][:, k, 1, h * hw:h * hw + D], bank[2 + k][:, h * D:(h + 1) * D], ACT.Copy,
                                                 scale=wt[g][:, k, 1, (h + 1) * hw - 1:(h + 1) * hw])
                        ins.then_inc(scaled, 1)

                if first:
                    start_counts(act, [log_done, rs_done, x1_done], quarters=[node_xT_copied])
                    in_rounds(act, iters, (node_scale, -1), (queries, 0), (weights, -1), (node_copy(1), 0), (roots, 0), (node_normalise, -1), (node_copy(0), 1), (copy_rows, 1))
                else:
                    start_counts(act, dmas=st_stored)
                    in_rounds(act, iters, (copy_rows, 1), (weigh, 0), (lambda i, g: store_state(act, i, g), -1))

            @block.vector
            def _(dve):
                start_counts(dve, [prod_done, mh_done, diff_m, diff_done, weighted, m_stored, sc_copied, leak_done, cut_ready], [max_done, decayed, acc_done])
                dve.memset(st[1][:], 0.0).then_inc(cleared, 1)
                dve.memset(mh[1][:], 0.0).then_inc(cleared, 1)
                dve.wait_ge(cleared, 2)

                def products(i, g):
                    dve.wait_ge(qk_done, at2(i, g))
                    dve.wait_ge(qT_copied, at2(i, g))
                    dve.wait_ge(scores_done, at2(i, g, back=2))
                    dve.scalar_tensor_tensor(prod[g][:], rows4(bank[1]), s.bk[:], qT[g][:], ALU.add, ALU.mult).then_inc(prod_done, 1)

                def maxima(i, g):
                    dve.wait_ge(diff_done, at2(i, g, back=2))
                    dve.tensor_copy(cut4[g][:], s.cut[:, bass.ds(i * (2 * G) + g * G, G)]).then_inc(cut_ready, 1)
                    if first:
                        dve.wait_ge(scores_done, at2(i, g))
                    else:
                        dve.wait_ge(scores_done, at2(i, g))
                        dve.tensor_copy(leak[g][:], score_bank[:, 0:G * H].rearrange("p (k h) -> p k h", k=G)).then_inc(sc_copied, 1)
                        dve.wait_ge(sc_copied, at2(i, g))
                        dve.wait_ge(diff_m, at2(i, g, back=2))
                        dve.scalar_tensor_tensor(sc[g][:], leak[g][:], 0.2, leak[g][:], ALU.mult, ALU.max).then_inc(leak_done, 1)
                        dve.wait_ge(leak_done, at2(i, g))
                    dve.wait_ge(max_done, at8(i, g * G, back=1))
                    dve.wait_ge(m_stored, at2(i, g, back=2))
                    dve.tensor_copy(mh[g][:, 0, :], mh[1 - g][:, G, :]).then_inc(mh_done, 1)
                    dve.wait_ge(mh_done, at2(i, g))
                    dve.wait_ge(cut_ready, at2(i, g))
                    for k in range(G):
                        dve.scalar_tensor_tensor(mh[g][:, k + 1, :], mh[g][:, k, :], cut4[g][:, k:k + 1], score[g][:, k, :], ALU.add, ALU.max).then_inc(max_done, 1)
                        dve.wait_ge(max_done, at8(i, g * G + k))
                    dve.wait_ge(exp_done, at2(i, g, back=2))
                    dve.tensor_tensor(diff[g][:, :, 0, :], mh[g][:, 0:G, :], mh[g][:, 1:G + 1, :], ALU.subtract)
                    dve.tensor_tensor(diff[g][:, :, 1, :], score[g], mh[g][:, 1:G + 1, :], ALU.subtract).then_inc(diff_m, 1)
                    dve.wait_ge(diff_m, at2(i, g))
                    cuts = cut4[g][:].rearrange("p (k a) -> p k a", a=1).to_broadcast([P, G, H])
                    dve.tensor_tensor(diff[g][:, :, 0, :], diff[g][:, :, 0, :], cuts, ALU.add).then_inc(diff_done, 1)

                def sums(i, g):
                    dve.wait_ge(st_stored[g], landed(i, back=1))
                    dve.tensor_copy(st[g][:, :, A:A + H], mh[g][:, 1:G + 1, :]).then_inc(m_stored, 1)
                    dve.wait_ge(exp_done, at2(i, g))
                    if first:
                        dve.wait_ge(values_done, at2(i, g))
                        w4 = wt[g][:, :, 1, :].rearrange("p k (h w) -> p k h w", h=H)
                        dve.tensor_tensor(w4[:, :, :, 0:C], value_bank[g][:].rearrange("p (k h c) -> p k h c", k=G, h=H),
                                          w4[:, :, :, C:C + 1].to_broadcast([P, G, H, C]), ALU.mult).then_inc(weighted, 1)
                        dve.wait_ge(weighted, at2(i, g))
                    for k in range(G):
                        kk = g * G + k
                        prev = st[g][:, k - 1, 0:A] if k else st[1 - g][:, G - 1, 0:A]
                        dve.wait_ge(acc_done, at8(i, kk, back=1))
                        if not first:
                            dve.wait_ge(scaled, at8(i, kk))
                            for h in range(H):
                                ins = dve.scalar_tensor_tensor(st[g][:, k, h * hw:(h + 1) * hw], prev[:, h * hw:(h + 1) * hw],
                                                               wt[g][:, k, 0, (h + 1) * hw - 1:(h + 1) * hw], wt[g][:, k, 1, h * hw:(h + 1) * hw],
                                                               ALU.mult, ALU.add)
                            ins.then_inc(acc_done, 1)
                            continue
                        dve.tensor_tensor(dec[k % 2][:].rearrange("p (h w) -> p h w", h=H), prev.rearrange("p (h w) -> p h w", h=H),
                                          wt[g][:, k, 0, :].rearrange("p (h w) -> p h w", h=H)[:, :, hw - 1:hw].to_broadcast([P, H, hw]), ALU.mult).then_inc(decayed, 1)
                        dve.wait_ge(decayed, at8(i, kk))
                        dve.tensor_tensor(st[g][:, k, 0:A], dec[k % 2][:], wt[g][:, k, 1, :], ALU.add).then_inc(acc_done, 1)

                def node_add(half):
                    def work(i, g):
                        dve.wait_ge(node_product, at4(i, 2 * g + half))
                        dve.wait_ge(x1_done, at2(i, g, back=2))
                        dve.tensor_tensor(Y[g][:, half * G:(half + 1) * G, :], rows4(bank[7]), s.br_all[:].rearrange("p (a d) -> p a d", a=1).to_broadcast([P, G, D]), ALU.add).then_inc(node_added, 1)
                        if half:
                            dve.wait_ge(node_added, at4(i, 2 * g + half))
                            dve.wait_ge(nb_done, at2(i, g, back=2))
                            rowstats(dve, Y[g], stats[g], mv[g], stat_done, aggr_done, i, g)
                    return work

                def node_shift(i, g):
                    dve.wait_ge(rs_done, at2(i, g))
                    dve.wait_ge(x1_done, at2(i, g, back=2))
                    dve.scalar_tensor_tensor(nb[g][:], mv[g][:, :, 0], -1.0, rs[g][:], ALU.mult, ALU.mult).then_inc(nb_done, 1)

                if first:
                    start_counts(dve, [stat_done, aggr_done, nb_done], quarters=[node_added])
                    in_rounds(dve, iters, (node_add(0), 0), (node_shift, -1), (products, 0), (sums, -1), (node_add(1), 0), (maxima, 0))
                else:
                    in_rounds(dve, iters, (maxima, 1), (sums, 0))

            @block.sync
            def _(sp):
                start_counts(sp, dmas=row_stored)
                if first:
                    start_counts(sp, dmas=st_stored)

                def store_rows(i, g):
                    t, group = now(sp, i * (2 * G) + g * G), now(sp, at2(i, g))
                    if first:
                        sp.wait_ge(root_copied, group)
                        sp.dma_start(rows_out[:, bass.ds(t, G), :], root[g][:]).then_inc(row_stored[g], 16)
                    else:
                        sp.wait_ge(gathered[g], 16 * 2 * G * i + 16 * 2 * G)
                        sp.dma_start(rows_out[:, bass.ds(t, G), :], xd[g][:]).then_inc(row_stored[g], 16)

                def node_load(i, g):
                    row, freed = now(sp, dense_row(s, i, g)), now(sp, at4(i, 2 * g + 1, back=4))
                    sp.wait_ge(node_transposed, freed)
                    sp.dma_start(x_in[g][:], of_block(a["x"], row, s)).then_inc(x_loaded[g], 16)

                def node_store(i, g):
                    store_block(sp, s, s.x1, x1, [x1_done], x1_stored, i, g)
                    if isinstance(i, int) and (i, g) == (iters - 1, 1):
                        sp.wait_ge(zeroed[0], landed(i))
                    sp.dma_start(of_block(s.agg1, dense_row(s, i, g), s), s.zeros[:].rearrange("p (k d) -> p k d", k=R)).then_inc(zeroed[g], 16)

                if first:
                    start_counts(sp, dmas=x_loaded + x1_stored + zeroed)
                    for j in range(3):
                        sp.dma_start(s.agg1[s.N + j * P:s.N + (j + 1) * P, :], s.zeros[:, 0:D]).then_inc(trash_zeroed, 16)
                    in_rounds(sp, iters, (store_rows, 0), (lambda i, g: store_state(sp, i, g), -1), (node_store, -1), (node_load, 2), apart=1)
                    sp.wait_ge(trash_zeroed, 16 * 3)
                    for g in range(2):
                        sp.wait_ge(x1_stored[g], landed(iters - 1))
                        sp.wait_ge(zeroed[g], landed(iters - 1))
                else:
                    in_rounds(sp, iters, (store_rows, 0))
                for g in range(2):
                    sp.wait_ge(row_stored[g], landed(iters - 1))
                    sp.wait_ge(st_stored[g], landed(iters - 1))


def patch_phase(nc, s, table, W, hw):
    T = s.T
    A = H * hw if hw else W
    flat = table.rearrange("p t w -> (p t) w")
    halves = [(0, A)] if A <= G * D else [(0, A // 2), (A // 2, A)]
    with Phase(nc, f"patch{W}") as ph:
        bank = ph.banks()
        head, tail, head_out, tail_out = (ph.sb(n, [P, W]) for n in ("head", "tail", "head_out", "tail_out"))
        far = ph.sb("far", [P, G, D])
        red, best = ph.sb("red", [P, 4, H]), ph.sb("best", [P, 2, H])
        diff, wts = ph.sb("diff", [P, 2, H]), ph.sb("wts", [P, 2, H])
        head_loaded, loaded, turned, calc, exp_done, joined, stored = (
            ph.sem(n) for n in ("head_loaded", "loaded", "turned", "calc", "exp_done", "joined", "stored"))
        sums = [0]
        with nc.Block() as block:
            @block.gpsimd
            def _(pool):
                pool.indirect_dma_start(head[:], None, flat, bass.IndirectOffsetOnAxis(ap=s.head_row[:], axis=0),
                                        bounds_check=P * T - 1, oob_is_err=False).then_inc(head_loaded, 16)

            @block.sync
            def _(sp):
                sp.dma_start(tail[:], table[:, T - 1, :]).then_inc(loaded, 16)

            @block.vector
            def _(dve):
                n = [0]

                def done(ins):
                    n[0] += 1
                    ins.then_inc(calc, 1)
                    dve.wait_ge(calc, n[0])

                dve.wait_ge(loaded, 16)
                dve.wait_ge(head_loaded, 16)
                if hw:
                    dve.wait_ge(turned, 1)
                    for j, (src, m) in enumerate(((0, s.far_tt), (1, s.far_th), (0, s.far_ht), (1, s.far_hh))):
                        done(dve.tensor_tensor(far[:], rows4(bank[src]), m[:].rearrange("p (a d) -> p a d", a=1).to_broadcast([P, G, P]), ALU.add))
                        done(dve.tensor_reduce(red[:, j, :], far[:], X, ALU.max))
                    for j in range(2):
                        done(dve.tensor_tensor(best[:, j, :], red[:, 2 * j, :], red[:, 2 * j + 1, :], ALU.max))
                    for j, part in enumerate((tail, head)):
                        done(dve.tensor_tensor(diff[:, j, :], part[:, A:A + H], best[:, j, :], ALU.subtract))
                    sums[0] = n[0]
                    dve.wait_ge(exp_done, 1)
                    for j, part in enumerate((tail, head)):
                        v = part[:, 0:A].rearrange("p (h w) -> p h w", h=H)
                        done(dve.tensor_tensor(v, v, wts[:, j, :].rearrange("p (h a) -> p h a", a=1).to_broadcast([P, H, hw]), ALU.mult))
                        done(dve.tensor_copy((tail_out, head_out)[j][:, A:A + H], best[:, j, :]))
                else:
                    done(dve.tensor_copy(best[:, 0, :], s.trash[:].to_broadcast([P, H])))
                sums.append(n[0])
                dve.wait_ge(joined, 1)
                for j, out in enumerate((tail_out, head_out)):
                    for b, (lo, hi) in enumerate(halves):
                        done(dve.tensor_copy(out[:, lo:hi], bank[2 + 2 * j + b][:, 0:hi - lo]))
                sums.append(n[0])

            @block.scalar
            def _(act):
                if hw:
                    act.wait_ge(calc, sums[0])
                    act.activation(wts[:], diff[:], ACT.Exp).then_inc(exp_done, 1)

            @block.tensor
            def _(pe):
                if hw:
                    pe.wait_ge(loaded, 16)
                    pe.wait_ge(head_loaded, 16)
                    for j, part in enumerate((tail, head)):
                        for h in range(H):
                            ins = pe.transpose(bank[j][:, h * P:(h + 1) * P], part[:, A + h:A + h + 1].to_broadcast([P, P]), s.ident[:])
                    ins.then_inc(turned, 1)
                pe.wait_ge(loaded, 16)
                pe.wait_ge(head_loaded, 16)
                pe.wait_ge(calc, sums[1])
                for j, (from_tail, from_head) in enumerate(((s.tail_tail, s.head_tail), (s.tail_head, s.head_head))):
                    for b, (lo, hi) in enumerate(halves):
                        pe.matmul(bank[2 + 2 * j + b][:, 0:hi - lo], from_tail[:], tail[:, lo:hi], start=True, stop=False)
                        ins = pe.matmul(bank[2 + 2 * j + b][:, 0:hi - lo], from_head[:], head[:, lo:hi], start=False, stop=True)
                ins.then_inc(joined, 1)

        with nc.Block() as block:
            @block.gpsimd
            def _(pool):
                pool.indirect_dma_start(flat, bass.IndirectOffsetOnAxis(ap=s.head_row[:], axis=0), head_out[:], None,
                                        bounds_check=P * T - 1, oob_is_err=False).then_inc(stored, 16)
                pool.wait_ge(stored, 16)
                pool.dma_start(table[:, T - 1, :], tail_out[:]).then_inc(stored, 16)
                pool.wait_ge(stored, 32)


def backward0_phase(nc, s, a):
    T, iters, hw = s.T, s.T // (2 * G), C + 1
    with Phase(nc, "bwd0") as ph:
        bank = ph.banks()
        st, root, src_rows = ph.two("st", [P, G, W0]), ph.two("root", [P, G, D]), ph.two("src_rows", [P, G, P], I32)
        edgeT, hid, filt = ph.two("edgeT", [RBF, G, P]), ph.two("hid", [P, G, P]), ph.two("filt", [P, G, D])
        inv, Y, x1, x1T, msg, merged, equal, cross = ph.two("inv", [P, G, H]), *(
            ph.two(n, [P, G, D]) for n in ("Y", "x1", "x1T", "msg", "merged", "equal", "cross"))
        stats, mv, sd, rs = ph.two("stats", [P, G, 6]), ph.two("mv", [P, G, 2]), ph.two("sd", [P, G]), ph.two("rs", [P, G])
        earlier, dup, add_f, add_idx = ph.two("earlier", [P, G, D]), ph.two("dup", [P, G]), ph.two("add_f", [P, G]), ph.two("add_idx", [P, G], I32)
        dup_pair, warm = ph.two("dup_pair", [P, G // 2]), ph.sb("warm", [P, 1])
        end_idx, inner, srcs, to_trash = ph.two("end_idx", [P, G], I32), ph.two("inner", [P, G], U32), ph.two("srcs", [P, G]), ph.two("to_trash", [P, G])
        loaded, edge_loaded, src_loaded, x1_stored = (ph.sem2(n) for n in ("loaded", "edge_loaded", "src_loaded", "x1_stored"))
        added, group_before_added = ph.sem("added"), ph.sem("group_before_added")
        names = ("hid_done", "hid_copied", "filt_done", "filt_copied", "x1T_done", "x1T_copied", "h_done",
                 "merge_done", "merge_copied", "inv_done", "Y_scaled", "Y_done", "stat_done", "aggr_done", "sd_done", "rs_done",
                 "rows_done", "msg_done", "equal_done", "dup_done", "dup_summed", "idx_sum", "add_ready", "meta_ready", "srcs_ready", "end_ready")
        (hid_done, hid_copied, filt_done, filt_copied, x1T_done, x1T_copied, h_done,
         merge_done, merge_copied, inv_done, Y_scaled, Y_done, stat_done, aggr_done, sd_done, rs_done,
         rows_done, msg_done, equal_done, dup_done, dup_summed, idx_sum, add_ready, meta_ready, srcs_ready, end_ready) = (ph.sem(n) for n in names)
        spread, cleared = ph.sem("spread"), ph.sem("cleared")

        def first_step(i, g):
            return (T - G - g * G) - (2 * G) * i

        with nc.Block() as block:
            @block.sync
            def _(sp):
                start_counts(sp, dmas=edge_loaded + src_loaded)
                start_counts(sp, dmas=loaded, n=2)

                def load(i, g):
                    t, freed = now(sp, first_step(i, g)), now(sp, at2(i, g, back=2))
                    sp.wait_ge(Y_done, freed)
                    sp.dma_start(st[g][:], s.state0[:, bass.ds(t, G), :]).then_inc(loaded[g], 16)
                    sp.dma_start(root[g][:], s.root0[:, bass.ds(t, G), :]).then_inc(loaded[g], 16)
                    sp.wait_ge(equal_done, freed)
                    src_of_steps = a["src_steps"][bass.ds(t, G), :].rearrange("k p -> (k p)").rearrange("(a n) -> a n", a=1)
                    sp.dma_start(src_rows[g][:].rearrange("q k p -> q (k p)"), src_of_steps.to_broadcast([P, G * P])).then_inc(src_loaded[g], 16)
                    sp.wait_ge(hid_done, freed)
                    sp.dma_start(edgeT[g][:], a["edge_steps"][:, bass.ds(t, G), :]).then_inc(edge_loaded[g], 16)

                in_rounds(sp, iters, (load, 0))

            @block.gpsimd
            def _(pool):
                limit, trash_limit = pool.to_reg(s.N - 1), pool.to_reg(s.agg_rows - 1)
                start_counts(pool, [end_ready, group_before_added])
                first_dma(pool, s, ph, [*x1_stored, added])

                def scatter_late(i, g):
                    t, freed, group, spread_late = (now(pool, v) for v in (first_step(i, g), scattered_at(i, G, back=1), at2(i, g), at8(i, g * G + 1)))
                    pool.wait_ge(x1_stored[g], freed)
                    pool.tensor_copy(end_idx[g][:], s.end_idx[:, bass.ds(t, G)]).then_inc(end_ready, 1)
                    pool.wait_ge(end_ready, 3)
                    pool.wait_ge(end_ready, group)
                    pool.wait_ge(spread, spread_late)
                    scatter(g, (3, 2))

                def scatter_early(i, g):
                    spread_all = now(pool, at8(i, g * G + G - 1))
                    pool.wait_ge(end_ready, 3)
                    pool.wait_ge(spread, spread_all)
                    scatter(g, (1, 0))

                def scatter(g, pair):
                    for k in pair:
                        pool.indirect_dma_start(s.x1, bass.IndirectOffsetOnAxis(ap=end_idx[g][:, k:k + 1], axis=0), x1[g][:, k, :], None,
                                                bounds_check=limit, oob_is_err=False).then_inc(x1_stored[g], 16)

                def add_late(i, g):
                    before, group = now(pool, 16 * 2 * G * i + 16 * (g * G + 1)), now(pool, at2(i, g))
                    pool.wait_ge(end_ready, 3)
                    pool.wait_ge(added, before)
                    pool.sem_inc(group_before_added, 1)
                    pool.wait_ge(end_ready, 3)
                    pool.wait_ge(merge_copied, group)
                    pool.wait_ge(add_ready, group)
                    add(g, (3, 2))

                def add_early(i, g):
                    before = now(pool, 16 * 2 * G * i + 16 * (g * G + 3))
                    pool.wait_ge(end_ready, 3)
                    pool.wait_ge(added, before)
                    add(g, (1, 0))

                def add(g, pair):
                    for k in pair:
                        pool.indirect_dma_start(s.agg1, bass.IndirectOffsetOnAxis(ap=add_idx[g][:, k:k + 1], axis=0), merged[g][:, k, :], None,
                                                bounds_check=trash_limit, oob_is_err=True, compute_op=ALU.add).then_inc(added, 16)

                in_rounds(pool, iters, (scatter_late, 1), (add_late, 0), (scatter_early, 1), (add_early, 0))
                pool.wait_ge(added, 16 * T + 16)
                for g in range(2):
                    pool.wait_ge(x1_stored[g], scattered_at(iters - 1, G))

            @block.tensor
            def _(pe):
                start_counts(pe, [hid_done, filt_done, x1T_done, h_done, merge_done])

                def hidden(i, g):
                    pe.wait_ge(edge_loaded[g], landed(i))
                    pe.wait_ge(hid_copied, at2(i, g, back=1))
                    pe.matmul(bank[2][:], s.W1[:], edgeT[g][:], start=True, stop=True).then_inc(hid_done, 1)

                def filters(i, g):
                    pe.wait_ge(hid_copied, at2(i, g))
                    pe.wait_ge(filt_copied, at2(i, g, back=1))
                    for k in range(G):
                        pe.matmul(bank[3][:, k * D:(k + 1) * D], hid[g][:, k, :], s.W2[:], start=True, stop=False)
                        ins = pe.matmul(bank[3][:, k * D:(k + 1) * D], s.ones3[:], s.b2_parts[:], start=False, stop=True)
                    ins.then_inc(filt_done, 1)

                def turn(i, g):
                    pe.wait_ge(spread, at8(i, g * G + G - 1))
                    pe.wait_ge(x1T_copied, at2(i, g, back=1))
                    for k in range(G):
                        ins = pe.transpose(bank[4][:, k * D:(k + 1) * D], x1[g][:, k, :], s.ident[:])
                    ins.then_inc(x1T_done, 1)

                def project(i, g):
                    pe.wait_ge(x1T_copied, at2(i, g))
                    pe.wait_ge(msg_done, at2(i, g, back=1))
                    for k in range(G):
                        pe.matmul(bank[5][:, k * D:(k + 1) * D], x1T[g][:, k, :], s.Wl[:], start=True, stop=False)
                        ins = pe.matmul(bank[5][:, k * D:(k + 1) * D], s.ones3[:], s.bl_parts[:], start=False, stop=True)
                    ins.then_inc(h_done, 1)

                def merge(i, g):
                    pe.wait_ge(msg_done, at2(i, g))
                    pe.wait_ge(equal_done, at2(i, g))
                    pe.wait_ge(merge_copied, at2(i, g, back=1))
                    for k in range(G):
                        other = k ^ 1
                        pe.matmul(bank[6][:, k * D:(k + 1) * D], equal[g][:, k, :], msg[g][:, k, :], start=True, stop=False)
                        ins = pe.matmul(bank[6][:, k * D:(k + 1) * D], cross[g][:, other, :], msg[g][:, other, :], start=False, stop=True)
                    ins.then_inc(merge_done, 1)

                in_rounds(pe, iters, (merge, -1), (turn, 0), (hidden, 1), (project, 0), (filters, 1))

            @block.scalar
            def _(act):
                start_counts(act, [hid_copied, filt_copied, x1T_copied, merge_copied, sd_done, srcs_ready])
                act.activation(warm[:], s.eps[:], ACT.Sqrt)

                def columns(i, g):
                    t, read = now(act, first_step(i, g)), now(act, at2(i, g, back=2))
                    act.wait_ge(add_ready, read)
                    act.activation(srcs[g][:], s.src_f[:, bass.ds(t, G)], ACT.Copy)
                    act.activation(to_trash[g][:], s.to_trash[:, bass.ds(t, G)], ACT.Copy).then_inc(srcs_ready, 1)

                def copy_hidden(i, g):
                    act.wait_ge(hid_done, at2(i, g))
                    act.wait_ge(filt_done, at2(i, g, back=2))
                    act.activation(hid[g][:], rows4(bank[2]), ACT.Relu, bias=s.b1[:]).then_inc(hid_copied, 1)

                def root_of_variance(i, g):
                    act.wait_ge(aggr_done, at2(i, g))
                    act.wait_ge(rs_done, at2(i, g, back=2))
                    act.activation(sd[g][:], mv[g][:, :, 1], ACT.Sqrt, bias=s.eps[:]).then_inc(sd_done, 1)

                def copy_filters(i, g):
                    act.wait_ge(filt_done, at2(i, g))
                    act.wait_ge(msg_done, at2(i, g, back=2))
                    act.activation(filt[g][:], rows4(bank[3]), ACT.Copy).then_inc(filt_copied, 1)

                def copy_turned(i, g):
                    act.wait_ge(x1T_done, at2(i, g))
                    act.wait_ge(h_done, at2(i, g, back=2))
                    act.activation(x1T[g][:], rows4(bank[4]), ACT.Copy).then_inc(x1T_copied, 1)

                def copy_merged(i, g):
                    act.wait_ge(merge_done, at2(i, g))
                    act.wait_ge(group_before_added, at2(i, g, back=1))
                    act.activation(merged[g][:], rows4(bank[6]), ACT.Copy).then_inc(merge_copied, 1)

                in_rounds(act, iters, (copy_merged, -1), (columns, 1), (copy_turned, 0), (copy_hidden, 1), (root_of_variance, 1), (copy_filters, 1))

            @block.vector
            def _(dve):
                start_counts(dve, [meta_ready, inv_done, Y_scaled, Y_done, stat_done, aggr_done, rs_done, rows_done,
                                   msg_done, equal_done, dup_done, dup_summed, idx_sum, add_ready], [spread])
                dve.memset(x1[1][:], 0.0).then_inc(cleared, 1)
                dve.wait_ge(cleared, 1)

                def rows(i, g):
                    t, spread_read = now(dve, first_step(i, g)), now(dve, at8(i, g * G + G - 1, back=2 * G))
                    dve.wait_ge(spread, spread_read)
                    dve.tensor_copy(inner[g][:], s.inner[:, bass.ds(t, G)]).then_inc(meta_ready, 1)
                    dve.wait_ge(loaded[g], landed(i, 2))
                    sums = st[g][:, :, 0:H * hw].rearrange("p k (h w) -> p k h w", h=H)
                    dve.reciprocal(inv[g][:], sums[:, :, :, C]).then_inc(inv_done, 1)
                    dve.wait_ge(inv_done, at2(i, g))
                    y4 = Y[g][:].rearrange("p k (h c) -> p k h c", h=H)
                    dve.tensor_tensor(y4, sums[:, :, :, 0:C], inv[g][:].rearrange("p k (h a) -> p k h a", a=1).to_broadcast([P, G, H, C]), ALU.mult).then_inc(Y_scaled, 1)
                    dve.wait_ge(Y_scaled, at2(i, g))
                    dve.tensor_tensor(Y[g][:], Y[g][:], root[g][:], ALU.add).then_inc(Y_done, 1)
                    dve.wait_ge(Y_done, at2(i, g))
                    dve.wait_ge(sd_done, at2(i, g, back=2))
                    rowstats(dve, Y[g], stats[g], mv[g], stat_done, aggr_done, i, g)

                def targets(i, g):
                    dve.wait_ge(srcs_ready, at2(i, g))
                    dve.wait_ge(src_loaded[g], landed(i))
                    dve.wait_ge(merge_done, at2(i, g, back=2))
                    own = srcs[g][:].rearrange("p (k a) -> p k a", a=1).to_broadcast([P, G, P])
                    dve.tensor_tensor(equal[g][:], src_rows[g][:], own, ALU.is_equal)
                    dve.tensor_tensor(cross[g][:, 0::2, :], src_rows[g][:, 1::2, :], own[:, 0::2, :], ALU.is_equal)
                    dve.tensor_tensor(cross[g][:, 1::2, :], src_rows[g][:, 0::2, :], own[:, 1::2, :], ALU.is_equal).then_inc(equal_done, 1)
                    dve.wait_ge(equal_done, at2(i, g))
                    for k in range(G):
                        dve.tensor_tensor_reduce(out=earlier[g][:, k, :], in0=equal[g][:, k, :], in1=s.lower[:], scale=1.0, scalar=0.0,
                                                 op0=ALU.mult, op1=ALU.add, accum_out=dup[g][:, k:k + 1])
                    dve.tensor_reduce(dup_pair[g][:], cross[g][:, 0::2, :], X, ALU.add).then_inc(dup_done, 1)
                    dve.wait_ge(dup_done, at2(i, g))
                    dve.tensor_tensor(dup[g][:, 0::2], dup[g][:, 0::2], dup_pair[g][:], ALU.add).then_inc(dup_summed, 1)
                    dve.wait_ge(dup_summed, at2(i, g))
                    dve.scalar_tensor_tensor(add_f[g][:], dup[g][:], 1.0, to_trash[g][:], ALU.min, ALU.mult).then_inc(idx_sum, 1)

                def indices(i, g):
                    dve.wait_ge(idx_sum, at2(i, g))
                    dve.wait_ge(group_before_added, at2(i, g, back=1))
                    dve.tensor_tensor(add_idx[g][:], add_f[g][:], srcs[g][:], ALU.add).then_inc(add_ready, 1)

                def normalise(i, g):
                    dve.wait_ge(x1_stored[g], scattered_at(i, G, back=1))
                    dve.wait_ge(x1T_done, at2(i, g, back=2))
                    norm_rows(dve, sd_done, Y[g], x1[g], mv[g], sd[g], rs[g], rs_done, rows_done, i, g)
                    spread_rows(dve, x1, inner, spread, cleared, rows_done, meta_ready, i, g)

                def messages(i, g):
                    dve.wait_ge(h_done, at2(i, g))
                    dve.wait_ge(filt_copied, at2(i, g))
                    dve.wait_ge(merge_done, at2(i, g, back=2))
                    dve.tensor_tensor(msg[g][:], rows4(bank[5]), filt[g][:], ALU.mult).then_inc(msg_done, 1)

                in_rounds(dve, iters, (messages, -1), (normalise, 0), (indices, 0), (rows, 1), (targets, 1))


def spread_rows(dve, x, inner, spread, cleared, rows_done, meta_ready, i, g):
    group, before = now(dve, at2(i, g)), [now(dve, at8(i, g * G + k, back=1)) for k in range(G)]
    for k in reversed(range(G)):
        later = x[g][:, k + 1, :] if k < G - 1 else x[1 - g][:, 0, :]
        dve.wait_ge(cleared, 1)
        if k == G - 1:
            dve.wait_ge(rows_done, group)
            dve.wait_ge(meta_ready, group)
        dve.wait_ge(spread, before[G - 1 - k])
        dve.copy_predicated(x[g][:, k, :], inner[g][:, k:k + 1].to_broadcast([P, D]), later).then_inc(spread, 1)


def norm_rows(dve, act_sd, Y, out, mv, sd, rs, rs_done, out_done, i, g):
    dve.wait_ge(act_sd, at2(i, g))
    dve.reciprocal(rs[:], sd[:]).then_inc(rs_done, 1)
    dve.wait_ge(rs_done, at2(i, g))
    for k in range(G):
        ins = dve.tensor_scalar(out[:, k, :], Y[:, k, :], mv[:, k, 0:1], rs[:, k:k + 1], ALU.subtract, ALU.mult)
    ins.then_inc(out_done, 1)


def dense1_phase(nc, s, a):
    iters = s.blocks // 2
    with Phase(nc, "dense1") as ph:
        xin, agg = ph.two("xin", [P, R, D]), ph.two("agg", [P, R, D])
        Y = [ph.two(f"Y{j}", [P, R, D]) for j in range(3)]
        out = [ph.two(f"out{j}", [P, R, D]) for j in range(3)]
        stats, mv, sd, rs, nb = ([ph.two(f"{n}{j}", [P, R] + w) for j in range(3)] for n, w in (("stats", [6]), ("mv", [2]), ("sd", []), ("rs", []), ("nb", [])))
        loaded, stored = ph.sem2("loaded"), [ph.sem2(f"stored{j}") for j in range(3)]
        Y_done, stat_done, aggr_done, sd_done, rs_done, nb_done, out_done, last_done = ([ph.sem(f"{n}{j}") for j in range(3)] for n in (
            "Y_done", "stat_done", "aggr_done", "sd_done", "rs_done", "nb_done", "out_done", "last_done"))
        tables = (s.x2, s.x3, s.out)

        with nc.Block() as block:
            @block.sync
            def _(sp):
                start_counts(sp, dmas=loaded, n=2)
                start_counts(sp, dmas=stored[0] + stored[1] + stored[2])

                def load(i, g):
                    row, freed = now(sp, dense_row(s, i, g)), now(sp, at2(i, g, back=2))
                    sp.wait_ge(Y_done[0], freed)
                    sp.dma_start(xin[g][:], of_block(s.x1, row, s)).then_inc(loaded[g], 16)
                    sp.dma_start(agg[g][:], of_block(s.agg1, row, s)).then_inc(loaded[g], 16)

                def store(j):
                    return lambda i, g: store_block(sp, s, tables[j], out[j], [out_done[j], last_done[j]], stored[j], i, g)

                in_rounds(sp, iters, (store(0), -2), (store(1), -4), (store(2), -6), (load, 2), apart=1)
                for j in range(3):
                    for g in range(2):
                        sp.wait_ge(stored[j][g], landed(iters - 1))

            @block.gpsimd
            def _(pool):
                start_counts(pool, Y_done)
                biases = [None, s.bt_all, s.rbn_all]

                def add(j):
                    def work(i, g):
                        if j == 0:
                            pool.wait_ge(loaded[g], landed(i, 2))
                            one, two = xin[g][:], agg[g][:]
                        else:
                            pool.wait_ge(out_done[j - 1], at2(i, g))
                            pool.wait_ge(last_done[j - 1], at2(i, g))
                            one, two = out[j - 1][g][:], biases[j][:].rearrange("p (a d) -> p a d", a=1).to_broadcast([P, R, D])
                        pool.wait_ge(out_done[j], at2(i, g, back=2))
                        pool.wait_ge(last_done[j], at2(i, g, back=2))
                        pool.tensor_tensor(Y[j][g][:], one, two, ALU.add).then_inc(Y_done[j], 1)
                    return work

                in_rounds(pool, iters, (add(0), 0), (add(1), -2), (add(2), -4))

            @block.vector
            def _(dve):
                start_counts(dve, [*stat_done, *aggr_done, *rs_done, *nb_done, *last_done])

                def statistics(j):
                    def work(i, g):
                        dve.wait_ge(Y_done[j], at2(i, g))
                        dve.wait_ge(last_done[j], at2(i, g, back=2))
                        rowstats(dve, Y[j][g], stats[j][g], mv[j][g], stat_done[j], aggr_done[j], i, g)
                    return work

                def scale(j):
                    def work(i, g):
                        dve.wait_ge(out_done[j], at2(i, g, back=2))
                        scales(dve, mv[j][g], sd[j][g], rs[j][g], nb[j][g], sd_done[j], rs_done[j], nb_done[j], i, g)
                        dve.wait_ge(stored[j][g], landed(i, back=1))
                        if j < 2:
                            dve.wait_ge(Y_done[j + 1], at2(i, g, back=2))
                        for k in range(R - VR, R):
                            ins = dve.tensor_scalar(out[j][g][:, k, :], Y[j][g][:, k, :], mv[j][g][:, k, 0:1], rs[j][g][:, k:k + 1], ALU.subtract, ALU.mult)
                        ins.then_inc(last_done[j], 1)
                    return work

                in_rounds(dve, iters, (scale(0), -1), (statistics(0), 0), (scale(1), -3), (statistics(1), -2), (scale(2), -5), (statistics(2), -4))

            @block.scalar
            def _(act):
                start_counts(act, [*sd_done, *out_done])

                def root_of_variance(j):
                    def work(i, g):
                        act.wait_ge(aggr_done[j], at2(i, g))
                        act.wait_ge(rs_done[j], at2(i, g, back=2))
                        act.activation(sd[j][g][:], mv[j][g][:, :, 1], ACT.Sqrt, bias=s.eps[:]).then_inc(sd_done[j], 1)
                    return work

                def normalise(j):
                    def work(i, g):
                        act.wait_ge(stored[j][g], landed(i, back=1))
                        if j < 2:
                            act.wait_ge(Y_done[j + 1], at2(i, g, back=2))
                        scale_rows(act, Y[j][g], out[j][g], rs[j][g], nb[j][g], nb_done[j], out_done[j], i, g, rows=R - VR)
                    return work

                act.activation(ph.sb("warm", [P, 1])[:], s.eps[:], ACT.Sqrt)
                in_rounds(act, iters, (normalise(0), -1), (root_of_variance(0), 0), (normalise(1), -3),
                          (root_of_variance(1), -2), (normalise(2), -5), (root_of_variance(2), -4))


def backward2_phase(nc, s, a):
    T, iters, hw = s.T, s.T // (2 * G), D + 1
    with Phase(nc, "bwd2") as ph:
        bank = ph.banks()
        st, own, inv = ph.two("st", [P, G, W2]), ph.two("own", [P, G, D]), ph.two("inv", [P, G, H])
        base = ph.two("base", [P, G, D])
        part, x3, warm = ph.two("part", [P, G, H, D]), ph.two("x3", [P, G, D]), ph.sb("warm", [P, 1])
        stats, mv, sd, rs, nb = ph.two("stats", [P, G, 6]), ph.two("mv", [P, G, 2]), ph.two("sd", [P, G]), ph.two("rs", [P, G]), ph.two("nb", [P, G])
        end_idx, inner = ph.two("end_idx", [P, G], I32), ph.two("inner", [P, G], U32)
        loaded, scattered, x3_stored = ph.sem2("loaded"), ph.sem2("scattered"), ph.sem2("x3_stored")
        inv_done, base_done, part_done, sum_done, stat_done, aggr_done, sd_done, rs_done, nb_done, rows_done, end_ready, meta_ready, spread, cleared = (ph.sem(n) for n in (
            "inv_done", "base_done", "part_done", "sum_done", "stat_done", "aggr_done", "sd_done", "rs_done", "nb_done", "rows_done", "end_ready", "meta_ready", "spread", "cleared"))

        def first_step(i, g):
            return (T - G - g * G) - (2 * G) * i

        with nc.Block() as block:
            @block.sync
            def _(sp):
                start_counts(sp, dmas=loaded, n=2)

                def load(i, g):
                    t, freed = now(sp, first_step(i, g)), now(sp, at2(i, g, back=2))
                    sp.wait_ge(part_done, freed)
                    sp.dma_start(st[g][:], s.state2[:, bass.ds(t, G), :]).then_inc(loaded[g], 16)
                    sp.wait_ge(base_done, freed)
                    sp.dma_start(own[g][:], s.own2[:, bass.ds(t, G), :]).then_inc(loaded[g], 16)

                in_rounds(sp, iters, (load, 0))

            @block.gpsimd
            def _(pool):
                limit = pool.to_reg(s.N - 1)
                start_counts(pool, [end_ready, base_done])
                first_dma(pool, s, ph, scattered)

                def add_bias(i, g):
                    pool.wait_ge(loaded[g], landed(i, 2))
                    pool.wait_ge(sum_done, at2(i, g, back=2))
                    pool.tensor_tensor(base[g][:], own[g][:], s.bt_all[:].rearrange("p (a d) -> p a d", a=1).to_broadcast([P, G, D]), ALU.add).then_inc(base_done, 1)

                def scatter(i, g):
                    t, freed, group, ready = (now(pool, v) for v in (first_step(i, g), scattered_at(i, G, back=1), at2(i, g), at8(i, g * G + G - 1)))
                    pool.wait_ge(scattered[g], freed)
                    pool.tensor_copy(end_idx[g][:], s.end_idx[:, bass.ds(t, G)]).then_inc(end_ready, 1)
                    pool.wait_ge(end_ready, 3)
                    pool.wait_ge(end_ready, group)
                    pool.wait_ge(spread, ready)
                    for k in reversed(range(G)):
                        pool.indirect_dma_start(s.x3, bass.IndirectOffsetOnAxis(ap=end_idx[g][:, k:k + 1], axis=0), x3[g][:, k, :], None,
                                                bounds_check=limit, oob_is_err=False).then_inc(scattered[g], 16)

                in_rounds(pool, iters, (add_bias, 1), (scatter, -1))
                for g in range(2):
                    pool.wait_ge(scattered[g], scattered_at(iters - 1, G))

            @block.tensor
            def _(pe):
                start_counts(pe, [sum_done])

                def total(i, g):
                    pe.wait_ge(base_done, at2(i, g))
                    pe.wait_ge(part_done, at2(i, g))
                    pe.wait_ge(rows_done, at2(i, g, back=2))
                    pe.matmul(bank[g][:], s.ident[:], base[g][:], start=True, stop=False)
                    for h in range(H):
                        ins = pe.matmul(bank[g][:], s.ident[:], part[g][:, :, h, :], start=False, stop=(h == H - 1))
                    ins.then_inc(sum_done, 1)

                in_rounds(pe, iters, (total, 0))

            @block.scalar
            def _(act):
                start_counts(act, [sd_done, rows_done])
                start_counts(act, dmas=x3_stored)
                act.activation(warm[:], s.eps[:], ACT.Sqrt)

                def root_of_variance(i, g):
                    act.wait_ge(aggr_done, at2(i, g))
                    act.wait_ge(rs_done, at2(i, g, back=2))
                    act.activation(sd[g][:], mv[g][:, :, 1], ACT.Sqrt, bias=s.eps[:]).then_inc(sd_done, 1)

                def normalise(i, g):
                    act.wait_ge(scattered[g], scattered_at(i, G, back=1))
                    act.wait_ge(x3_stored[g], landed(i, back=1))
                    scale_rows(act, rows4(bank[g]), x3[g], rs[g], nb[g], nb_done, rows_done, i, g, rows=G)

                def store(i, g):
                    t, ready = now(act, first_step(i, g)), now(act, at8(i, g * G + G - 1))
                    act.wait_ge(spread, ready)
                    act.dma_start(s.dst3[:, bass.ds(t, G), :], x3[g][:]).then_inc(x3_stored[g], 16)

                in_rounds(act, iters, (normalise, -1), (root_of_variance, 0), (store, -1))
                for g in range(2):
                    act.wait_ge(x3_stored[g], landed(iters - 1))

            @block.vector
            def _(dve):
                start_counts(dve, [meta_ready, inv_done, part_done, stat_done, aggr_done, rs_done, nb_done], [spread])
                dve.memset(x3[1][:], 0.0).then_inc(cleared, 1)
                dve.wait_ge(cleared, 1)

                def parts(i, g):
                    dve.wait_ge(loaded[g], landed(i, 2))
                    sums = st[g][:, :, 0:H * hw].rearrange("p k (h w) -> p k h w", h=H)
                    dve.reciprocal(inv[g][:], sums[:, :, :, D]).then_inc(inv_done, 1)
                    dve.wait_ge(inv_done, at2(i, g))
                    dve.wait_ge(sum_done, at2(i, g, back=2))
                    for k in range(G):
                        ins = dve.tensor_tensor(part[g][:, k], sums[:, k, :, 0:D], inv[g][:, k, :].rearrange("p (h a) -> p h a", a=1).to_broadcast([P, H, D]), ALU.mult)
                    ins.then_inc(part_done, 1)

                def statistics(i, g):
                    t, spread_read = now(dve, first_step(i, g)), now(dve, at8(i, g * G + G - 1, back=2 * G))
                    dve.wait_ge(spread, spread_read)
                    dve.tensor_copy(inner[g][:], s.inner[:, bass.ds(t, G)]).then_inc(meta_ready, 1)
                    dve.wait_ge(sum_done, at2(i, g))
                    dve.wait_ge(nb_done, at2(i, g, back=2))
                    rowstats(dve, rows4(bank[g]), stats[g], mv[g], stat_done, aggr_done, i, g)

                def scale(i, g):
                    dve.wait_ge(rows_done, at2(i, g, back=2))
                    scales(dve, mv[g], sd[g], rs[g], nb[g], sd_done, rs_done, nb_done, i, g)

                def spread_x3(i, g):
                    spread_rows(dve, x3, inner, spread, cleared, rows_done, meta_ready, i, g)

                in_rounds(dve, iters, (scale, -1), (parts, 1), (spread_x3, -1), (statistics, 0))


def forward3_phase(nc, s, a):
    T, iters = s.T, s.T // (2 * G)
    with Phase(nc, "fwd3") as ph:
        bank = ph.banks()
        xs, xd, xsT, xdT, old = (ph.two(n, [P, G, D]) for n in ("xs", "xd", "xsT", "xdT", "old"))
        idx, same4, st = ph.two("idx", [P, 2 * G], I32), ph.two("same4", [P, G]), ph.two("st", [P, G, W3])
        idx_ready, gathered, own_loaded, st_stored = ph.sem("idx_ready"), ph.sem2("gathered"), ph.sem2("own_loaded"), ph.sem2("st_stored")
        transposed, xT_copied, rows_done, same_ready, decayed, acc_done, cnt_done, cleared = (
            ph.sem(n) for n in ("transposed", "xT_copied", "rows_done", "same_ready", "decayed", "acc_done", "cnt_done", "cleared"))
        with nc.Block() as block:
            @block.gpsimd
            def _(pool):
                limit = pool.to_reg(s.N - 1)

                def gather(i, g):
                    column, freed, ready = (now(pool, v) for v in (i * (4 * G) + g * 2 * G, at2(i, g, back=2), 2 * i + (g + 1)))
                    pool.wait_ge(transposed, freed)
                    pool.tensor_copy(idx[g][:], s.gather_idx[:, bass.ds(column, 2 * G)]).then_inc(idx_ready, 1)
                    pool.wait_ge(idx_ready, 1)
                    pool.wait_ge(idx_ready, ready)
                    for k in range(G):
                        pool.indirect_dma_start(xs[g][:, k, :], None, s.x3, bass.IndirectOffsetOnAxis(ap=idx[g][:, k:k + 1], axis=0),
                                                bounds_check=limit, oob_is_err=False).then_inc(gathered[g], 16)

                in_rounds(pool, iters, (gather, 0))

            @block.sync
            def _(sp):
                start_counts(sp, dmas=own_loaded)

                def load(i, g):
                    t, freed = now(sp, i * (2 * G) + g * G), now(sp, at2(i, g, back=2))
                    sp.wait_ge(transposed, freed)
                    sp.dma_start(xd[g][:], s.dst3[:, bass.ds(t, G), :]).then_inc(own_loaded[g], 16)

                in_rounds(sp, iters, (load, 0))

            @block.tensor
            def _(pe):
                start_counts(pe, [transposed, rows_done])

                def turn(i, g):
                    pe.wait_ge(gathered[g], 16 * G * i + 16 * G)
                    pe.wait_ge(own_loaded[g], landed(i))
                    pe.wait_ge(xT_copied, at2(i, g, back=2))
                    for k in range(G):
                        pe.transpose(bank[g][:, k * D:(k + 1) * D], xs[g][:, k, :], s.ident[:])
                    for k in range(G):
                        ins = pe.transpose(bank[2 + g][:, k * D:(k + 1) * D], xd[g][:, k, :], s.ident[:])
                    ins.then_inc(transposed, 1)

                def edge_rows(i, g):
                    pe.wait_ge(xT_copied, at2(i, g))
                    pe.wait_ge(acc_done, at8(i, g * G + 3, back=8))
                    for k in range(G):
                        pe.matmul(bank[4 + g][:, k * D:(k + 1) * D], xsT[g][:, k, :], s.WeT[:, 0, :], start=True, stop=False)
                        ins = pe.matmul(bank[4 + g][:, k * D:(k + 1) * D], xdT[g][:, k, :], s.WeT[:, 1, :], start=False, stop=True)
                    ins.then_inc(rows_done, 1)

                in_rounds(pe, iters, (turn, 1), (edge_rows, 0))

            @block.scalar
            def _(act):
                start_counts(act, [xT_copied])
                start_counts(act, dmas=st_stored)

                def copy_rows(i, g):
                    act.wait_ge(transposed, at2(i, g))
                    act.wait_ge(rows_done, at2(i, g, back=2))
                    act.activation(xsT[g][:], rows4(bank[g]), ACT.Copy)
                    act.activation(xdT[g][:], rows4(bank[2 + g]), ACT.Copy).then_inc(xT_copied, 1)

                def store(i, g):
                    t, step = now(act, i * (2 * G) + g * G), now(act, at8(i, g * G + 3))
                    act.wait_ge(acc_done, step)
                    act.wait_ge(cnt_done, step)
                    act.dma_start(s.state3[:, bass.ds(t, G), :], st[g][:]).then_inc(st_stored[g], 16)

                in_rounds(act, iters, (copy_rows, 0), (store, -1))
                for g in range(2):
                    act.wait_ge(st_stored[g], landed(iters - 1))

            @block.vector
            def _(dve):
                start_counts(dve, [same_ready], [decayed, acc_done, cnt_done])
                dve.memset(st[1][:], 0.0).then_inc(cleared, 1)
                dve.wait_ge(cleared, 1)

                def sums(i, g):
                    t, read = now(dve, i * (2 * G) + g * G), now(dve, at8(i, g * G + 3, back=8))
                    dve.wait_ge(acc_done, read)
                    dve.wait_ge(cnt_done, read)
                    dve.tensor_copy(same4[g][:], s.same[:, bass.ds(t, G)]).then_inc(same_ready, 1)
                    dve.wait_ge(same_ready, at2(i, g))
                    dve.wait_ge(rows_done, at2(i, g))
                    dve.wait_ge(st_stored[g], landed(i, back=1))
                    for k in range(G):
                        kk = g * G + k
                        prev = st[g][:, k - 1, :] if k else st[1 - g][:, G - 1, :]
                        dve.wait_ge(acc_done, at8(i, kk, back=1))
                        dve.wait_ge(cnt_done, at8(i, kk, back=1))
                        dve.tensor_scalar(old[g][:, k, :], prev[:, 0:D], same4[g][:, k:k + 1], None, ALU.mult).then_inc(decayed, 1)
                        dve.tensor_scalar(st[g][:, k, D:W3], prev[:, D:W3], same4[g][:, k:k + 1], 1.0, ALU.mult, ALU.add).then_inc(cnt_done, 1)
                        dve.wait_ge(decayed, at8(i, kk))
                        dve.scalar_tensor_tensor(st[g][:, k, 0:D], bank[4 + g][:, k * D:(k + 1) * D], 0.0, old[g][:, k, :], ALU.max, ALU.add).then_inc(acc_done, 1)

                in_rounds(dve, iters, (sums, 0))


def backward3_phase(nc, s, a):
    T, iters = s.T, s.T // (2 * G)
    with Phase(nc, "bwd3") as ph:
        bank = ph.banks()
        st, own, inv = ph.two("st", [P, G, W3]), ph.two("own", [P, G, D]), ph.two("inv", [P, G])
        mean, meanT, Y, out = (ph.two(n, [P, G, D]) for n in ("mean", "meanT", "Y", "out"))
        stats, mv, sd, rs = ph.two("stats", [P, G, 6]), ph.two("mv", [P, G, 2]), ph.two("sd", [P, G]), ph.two("rs", [P, G])
        end_idx, warm = ph.two("end_idx", [P, G], I32), ph.sb("warm", [P, 1])
        loaded, own_loaded, scattered = ph.sem2("loaded"), ph.sem2("own_loaded"), ph.sem2("scattered")
        inv_done, mean_done, meanT_done, meanT_copied, node_done, Y_done, stat_done, aggr_done, sd_done, rs_done, out_done, end_ready = (ph.sem(n) for n in (
            "inv_done", "mean_done", "meanT_done", "meanT_copied", "node_done", "Y_done", "stat_done", "aggr_done", "sd_done", "rs_done", "out_done", "end_ready"))
        with nc.Block() as block:
            @block.sync
            def _(sp):
                start_counts(sp, dmas=loaded + own_loaded)

                def load_state(i, g):
                    t, freed = now(sp, i * (2 * G) + g * G), now(sp, at2(i, g, back=2))
                    sp.wait_ge(mean_done, freed)
                    sp.dma_start(st[g][:], s.state3[:, bass.ds(t, G), :]).then_inc(loaded[g], 16)

                def load_own(i, g):
                    t, freed = now(sp, i * (2 * G) + g * G), now(sp, at2(i, g, back=2))
                    sp.wait_ge(Y_done, freed)
                    sp.dma_start(own[g][:], s.dst3[:, bass.ds(t, G), :]).then_inc(own_loaded[g], 16)

                in_rounds(sp, iters, (load_state, 1), (load_own, 0))

            @block.gpsimd
            def _(pool):
                limit = pool.to_reg(s.N - 1)
                start_counts(pool, [end_ready])
                first_dma(pool, s, ph, scattered)

                def scatter(i, g):
                    t, freed, group = (now(pool, v) for v in (i * (2 * G) + g * G, scattered_at(i, G, back=1), at2(i, g)))
                    pool.wait_ge(scattered[g], freed)
                    pool.tensor_copy(end_idx[g][:], s.end_idx[:, bass.ds(t, G)]).then_inc(end_ready, 1)
                    pool.wait_ge(end_ready, 3)
                    pool.wait_ge(end_ready, group)
                    pool.wait_ge(out_done, group)
                    for k in range(G):
                        pool.indirect_dma_start(s.out, bass.IndirectOffsetOnAxis(ap=end_idx[g][:, k:k + 1], axis=0), out[g][:, k, :], None,
                                                bounds_check=limit, oob_is_err=False).then_inc(scattered[g], 16)

                in_rounds(pool, iters, (scatter, 0))
                for g in range(2):
                    pool.wait_ge(scattered[g], scattered_at(iters - 1, G))

            @block.tensor
            def _(pe):
                start_counts(pe, [meanT_done, node_done])

                def turn(i, g):
                    pe.wait_ge(mean_done, at2(i, g))
                    pe.wait_ge(meanT_copied, at2(i, g, back=2))
                    for k in range(G):
                        ins = pe.transpose(bank[g][:, k * D:(k + 1) * D], mean[g][:, k, :], s.ident[:])
                    ins.then_inc(meanT_done, 1)

                def node_rows(i, g):
                    pe.wait_ge(meanT_copied, at2(i, g))
                    pe.wait_ge(Y_done, at2(i, g, back=2))
                    for k in range(G):
                        pe.matmul(bank[2 + g][:, k * D:(k + 1) * D], meanT[g][:, k, :], s.WnT[:], start=True, stop=False)
                        ins = pe.matmul(bank[2 + g][:, k * D:(k + 1) * D], s.ones3[:], s.bn_parts[:], start=False, stop=True)
                    ins.then_inc(node_done, 1)

                in_rounds(pe, iters, (node_rows, 0), (turn, 1))

            @block.scalar
            def _(act):
                start_counts(act, [mean_done, meanT_copied, sd_done])
                act.activation(warm[:], s.eps[:], ACT.Sqrt)

                def means(i, g):
                    act.wait_ge(inv_done, at2(i, g))
                    act.wait_ge(meanT_done, at2(i, g, back=2))
                    for k in range(G):
                        ins = act.activation(mean[g][:, k, :], st[g][:, k, 0:D], ACT.Copy, scale=inv[g][:, k:k + 1])
                    ins.then_inc(mean_done, 1)

                def copy_turned(i, g):
                    act.wait_ge(meanT_done, at2(i, g))
                    act.wait_ge(node_done, at2(i, g, back=2))
                    act.activation(meanT[g][:], rows4(bank[g]), ACT.Copy).then_inc(meanT_copied, 1)

                def root_of_variance(i, g):
                    act.wait_ge(aggr_done, at2(i, g))
                    act.wait_ge(rs_done, at2(i, g, back=2))
                    act.activation(sd[g][:], mv[g][:, :, 1], ACT.Sqrt, bias=s.eps[:]).then_inc(sd_done, 1)

                in_rounds(act, iters, (means, 1), (copy_turned, 1), (root_of_variance, 0))

            @block.vector
            def _(dve):
                start_counts(dve, [inv_done, Y_done, stat_done, aggr_done, rs_done, out_done])

                def inverses(i, g):
                    dve.wait_ge(loaded[g], landed(i))
                    dve.wait_ge(mean_done, at2(i, g, back=2))
                    dve.reciprocal(inv[g][:], st[g][:, :, D]).then_inc(inv_done, 1)

                def rows(i, g):
                    dve.wait_ge(node_done, at2(i, g))
                    dve.wait_ge(own_loaded[g], landed(i))
                    dve.scalar_tensor_tensor(Y[g][:], rows4(bank[2 + g]), 0.0, own[g][:], ALU.max, ALU.add).then_inc(Y_done, 1)
                    dve.wait_ge(Y_done, at2(i, g))
                    dve.wait_ge(sd_done, at2(i, g, back=2))
                    rowstats(dve, Y[g], stats[g], mv[g], stat_done, aggr_done, i, g)

                def normalise(i, g):
                    dve.wait_ge(scattered[g], scattered_at(i, G, back=1))
                    norm_rows(dve, sd_done, Y[g], out[g], mv[g], sd[g], rs[g], rs_done, out_done, i, g)

                in_rounds(dve, iters, (inverses, 1), (normalise, -1), (rows, 0))


def build(nc, a, out):
    N, T = a["x"].shape[0], a["src2"].shape[1]
    s = Kept()
    s.N, s.T, s.block = N, T, P * R
    s.blocks = -(-N // (2 * s.block)) * 2
    assert T % (2 * G) == 0 and N > (s.blocks - 1) * s.block
    s.agg_rows = N + 3 * P
    assert s.blocks == T // G

    def table(name, shape):
        return nc.dram_tensor(name, shape, F32, kind="Internal").ap()

    s.x1, s.x2, s.x3 = (table(f"x{j}", (N, D)) for j in (1, 2, 3))
    s.agg1 = table("agg1", (s.agg_rows, D))
    s.state0, s.state2, s.state3 = table("state0", (P, T, W0)), table("state2", (P, T, W2)), table("state3", (P, T, W3))
    s.root0, s.own2, s.dst3 = table("root0", (P, T, D)), table("own2", (P, T, D)), table("dst3", (P, T, D))
    s.out = out
    with ExitStack() as c:
        def sb(names, shape, dt=F32):
            return [c.enter_context(nc.sbuf_tensor(n, shape, dt)) for n in names.split()]

        s.ident, s.lower, s.Wq, s.Wk, s.Wv, s.WrI, s.W2, s.Wl, s.WnT = sb("ident lower Wq Wk Wv WrI W2 Wl WnT", [P, D])
        s.br_all, s.bt_all, s.bn_all, s.rbn_all = sb("br_all bt_all bn_all rbn_all", [P, D])
        s.tail_tail, s.tail_head, s.head_tail, s.head_head = sb("tail_tail tail_head head_tail head_head", [P, P])
        s.far_tt, s.far_th, s.far_ht, s.far_hh = sb("far_tt far_th far_ht far_hh", [P, P])
        s.brv_parts, s.b2_parts, s.bl_parts, s.bn_parts, s.ones3 = sb("brv_parts b2_parts bl_parts bn_parts ones3", [3, D], BF16)
        s.bq, s.bk, s.b1, s.eps, s.trash = sb("bq bk b1 eps trash", [P, 1])
        [s.W1], [s.WeT], [s.Wz] = sb("W1", [RBF, D]), sb("WeT", [P, 2, D]), sb("Wz", [P, H, D])
        s.headsel, s.att_s, s.att_d = sb("headsel att_s att_d", [P, H])
        s.src_f, s.dst_f, s.same, s.cut, s.to_trash = sb("src_f dst_f same cut to_trash", [P, T])
        [s.inner], [s.end_idx], [s.gather_idx] = sb("inner", [P, T], U32), sb("end_idx", [P, T], I32), sb("gather_idx", [P, 2 * T], I32)
        [s.head_row], [s.zeros] = sb("head_row", [P, 1], I32), sb("zeros", [P, R * D])
        setup_phase(nc, s, a)
        forward_attention_phase(nc, s, a, 0)
        patch_phase(nc, s, s.state0, W0, C + 1)
        backward0_phase(nc, s, a)
        dense1_phase(nc, s, a)
        forward_attention_phase(nc, s, a, 2)
        patch_phase(nc, s, s.state2, W2, D + 1)
        backward2_phase(nc, s, a)
        forward3_phase(nc, s, a)
        patch_phase(nc, s, s.state3, W3, 0)
        backward3_phase(nc, s, a)


def laid_out(inputs):
    g = {k: np.asarray(v) for k, v in inputs.items()}
    N, E = g["x"].shape[0], g["src"].shape[0]
    T = steps_of(E)
    pad = P * T - E

    def per_partition(v, fill):
        return np.concatenate([v, np.full(P * T - v.shape[0], fill, v.dtype)]).reshape(P, T)

    flip = np.ascontiguousarray
    src2 = per_partition(g["src"], N + 2 * P)
    out = {
        "x": g["x"],
        "src2": src2, "dst2": per_partition(g["dst"], N), "next_dst2": per_partition(g["dst"][1:], N + 1),
        "src_steps": flip(src2.T),
        "edge_steps": flip(np.concatenate([g["edge_attr_64"], np.zeros((pad, RBF), g["edge_attr_64"].dtype)]).reshape(P, T, RBF).transpose(2, 1, 0)),
        "Wq": g["L0_gnn_Wq"], "Wk": g["L0_gnn_Wk"], "Wv": g["L0_gnn_Wv"], "Wr": g["L0_gnn_Wr"],
        "bq": g["L0_gnn_bq"], "bk": g["L0_gnn_bk"], "bv": g["L0_gnn_bv"], "br": g["L0_gnn_br"],
        "W1": g["L1_gnn_W1"], "b1": g["L1_gnn_b1"], "W2": g["L1_gnn_W2"], "b2": g["L1_gnn_b2"], "Wl": g["L1_gnn_Wl"], "bl": g["L1_gnn_bl"],
        "WfcT": flip(g["L2_gnn_W_fc"].T), "Wtr": g["L2_gnn_W_trans"], "bt": g["L2_gnn_b_trans"],
        "att2": flip(np.stack([g["L2_gnn_att_ns"][0].T, g["L2_gnn_att_nd"][0].T], axis=2)),
        "WeT": flip(g["L3_gnn_W_edge"].T), "WnT": flip(g["L3_gnn_W_node"].T), "bn": g["L3_gnn_b_node"],
        "c_ident": np.eye(P, dtype=np.float32), "c_lower": np.tri(P, k=-1, dtype=np.float32),
        "c_headsel": flip(np.repeat(np.eye(H, dtype=np.float32), C, axis=0) / np.float32(np.sqrt(C))),
        "c_trash": np.arange(N, N + P, dtype=np.float32).reshape(P, 1),
    }
    return out


def kernel(**inputs):
    import concourse.bacc as bacc
    from concourse.bass_utils import run_bass_kernel_spmd

    arrays = laid_out(inputs)
    nc = bacc.Bacc("TRN2", target_bir_lowering=False, num_devices=1)
    a = {name: nc.dram_tensor(f"in_{name}", v.shape, mybir.dt.from_np(v.dtype), kind="ExternalInput").ap() for name, v in arrays.items()}
    out = nc.dram_tensor("out", inputs["x"].shape, F32, kind="ExternalOutput").ap()
    build(nc, a, out)
    r = run_bass_kernel_spmd(nc, [{f"in_{name}": v for name, v in arrays.items()}], core_ids=[0])
    return r.results[0]["out"]
```
